# Optimizing a Trainium2 kernel written in Bass

```python
import numpy as np
import jax
import jax.numpy as jnp

def _softmax(x, axis=-1):
    return jax.nn.softmax(x, axis=axis)

def _gelu(x):
    return jax.nn.gelu(x, approximate=True)

def _silu(x):
    return jax.nn.silu(x)

def _sigmoid(x):
    return jax.nn.sigmoid(x)

def _layernorm(x, axis=-1, eps=1e-05):
    m = jnp.mean(x, axis=axis, keepdims=True)
    v = jnp.var(x, axis=axis, keepdims=True)
    return (x - m) / jnp.sqrt(v + eps)

def _scatter_add(tgt, idx, src, axis=0):
    return tgt.at[idx].add(src)

def _segment_sum(src, seg, n):
    return jax.ops.segment_sum(src, seg, n)
kernel_name = 'mk_gps_d1_gnn_r32_9efdfa'

def setup_inputs(seed: int=0):
    np.random.seed(seed)
    _w = jnp.asarray

    def _rec_inputs():
        import jax
        import jax.numpy as jnp
        _gk = jax.random.key(seed)
        x = -0.0003713 + 1 * jax.random.normal(jax.random.fold_in(_gk, 1), (3125, 256), jnp.float32)
        src = jax.random.randint(jax.random.fold_in(_gk, 2), (50000,), 0, 3125, jnp.int32)
        dst = jax.random.randint(jax.random.fold_in(_gk, 3), (50000,), 0, 3125, jnp.int32)
        _o = jnp.argsort(dst, stable=True)
        src = src[_o]
        dst = dst[_o]
        edge_type_4 = jax.random.randint(jax.random.fold_in(_gk, 12), (50000,), 0, 4, jnp.int32)
        return (x, src, dst, edge_type_4)
    x, src, dst, edge_type_4 = _rec_inputs()

    def _L0_gnn_setup():
        import jax, jax.numpy as jnp
        import numpy as np
        N_NODES = 50000
        N_EDGES = 25000
        C = 256
        R = 4

        def _rgcn(node_features, edge_index, edge_type, rel_weight, root_weight, rgcn_bias):
            N = node_features.shape[0]
            src, dst = (edge_index[0], edge_index[1])
            out = node_features @ root_weight + rgcn_bias
            num_rel = rel_weight.shape[0]
            for r in range(num_rel):
                trans = node_features @ rel_weight[r]
                mask = edge_type == r
                msg = jnp.where(mask[:, None], trans[src], 0.0)
                ssum = jax.ops.segment_sum(msg, dst, num_segments=N)
                cnt = jax.ops.segment_sum(mask.astype(node_features.dtype), dst, num_segments=N)
                out = out + ssum / jnp.maximum(cnt, 1.0)[:, None]
            return out
        key = jax.random.key(seed)
        ks = jax.random.split(key, 8)
        node_features = jax.random.normal(ks[0], (N_NODES, C), dtype=jnp.float32)
        edge_index = jax.random.randint(ks[1], (2, N_EDGES), 0, N_NODES, dtype=jnp.int64)
        edge_type = jax.random.randint(ks[2], (N_EDGES,), 0, R, dtype=jnp.int64)
        s = 1.0 / np.sqrt(C)
        rel_weight = jax.random.normal(ks[3], (R, C, C), dtype=jnp.float32) * s
        root_weight = jax.random.normal(ks[4], (C, C), dtype=jnp.float32) * s
        rgcn_bias = jax.random.normal(ks[5], (C,), dtype=jnp.float32) * 0.01
        att_weight = jax.random.normal(ks[6], (1, 2 * C), dtype=jnp.float32) * (1.0 / np.sqrt(2 * C))
        att_bias = jax.random.normal(ks[7], (1,), dtype=jnp.float32) * 0.01
        return {'node_features': node_features, 'edge_index': edge_index, 'edge_type': edge_type, 'rel_weight': rel_weight, 'root_weight': root_weight, 'rgcn_bias': rgcn_bias, 'att_weight': att_weight, 'att_bias': att_bias}
    _L0_gnn_all = _L0_gnn_setup()
    _L0_gnn_in = {k: v for k, v in _L0_gnn_all.items() if k in ('rel_weight', 'root_weight', 'rgcn_bias', 'att_weight', 'att_bias')}
    del _L0_gnn_all

    def _L0_mix_setup():
        import jax, jax.numpy as jnp
        import numpy as np
        MIDC = 256
        HEADS = 8
        HEADC = MIDC // HEADS
        EPS = 1e-05

        def _ln(x, gamma, beta):
            mu = jnp.mean(x, axis=-1, keepdims=True)
            var = jnp.var(x, axis=-1, keepdims=True)
            return (x - mu) * jax.lax.rsqrt(var + EPS) * gamma + beta
        key = jax.random.key(seed)
        ks = jax.random.split(key, 8)
        B, HW, C = (8, 128, MIDC)
        s = 1.0 / np.sqrt(C)
        return {'x': jax.random.normal(ks[0], (B, HW, C), jnp.float32), 'w_qkv': jax.random.normal(ks[1], (C, 3 * C), jnp.float32) * s, 'b_qkv': jnp.zeros((3 * C,), jnp.float32), 'kln_g': jnp.ones((HEADC,), jnp.float32), 'kln_b': jnp.zeros((HEADC,), jnp.float32), 'vln_g': jnp.ones((HEADC,), jnp.float32), 'vln_b': jnp.zeros((HEADC,), jnp.float32), 'w1': jax.random.normal(ks[2], (C, C), jnp.float32) * s, 'b1': jnp.zeros((C,), jnp.float32), 'w2': jax.random.normal(ks[3], (C, C), jnp.float32) * s, 'b2': jnp.zeros((C,), jnp.float32)}
    _L0_mix_all = _L0_mix_setup()
    _L0_mix_in = {k: v for k, v in _L0_mix_all.items() if k in ('w_qkv', 'b_qkv', 'kln_g', 'kln_b', 'vln_g', 'vln_b', 'w1', 'b1', 'w2', 'b2')}
    del _L0_mix_all

    def _L0_ffn_setup():
        import jax, jax.numpy as jnp
        import numpy as np
        B, S, D = (8, 128, 256)
        H = 4 * D
        CAPACITY = 0.5
        key = jax.random.key(seed)
        ks = jax.random.split(key, 6)
        x = jax.random.normal(ks[0], (B, S, D), dtype=jnp.float32)
        attention_mask = jnp.zeros((B, 1, 1, S), dtype=jnp.float32)
        wr = jax.random.normal(ks[1], (D, 1), dtype=jnp.float32) * 0.02
        br = jnp.zeros((1,), dtype=jnp.float32)
        w1 = jax.random.normal(ks[2], (D, H), dtype=jnp.float32) * 0.02
        b1 = jnp.zeros((H,), dtype=jnp.float32)
        w2 = jax.random.normal(ks[3], (H, D), dtype=jnp.float32) * 0.02
        b2 = jnp.zeros((D,), dtype=jnp.float32)
        return {'x': x, 'attention_mask': attention_mask, 'wr': wr, 'br': br, 'w1': w1, 'b1': b1, 'w2': w2, 'b2': b2}
    _L0_ffn_all = _L0_ffn_setup()
    _L0_ffn_in = {k: v for k, v in _L0_ffn_all.items() if k in ('attention_mask', 'wr', 'br', 'w1', 'b1', 'w2', 'b2')}
    del _L0_ffn_all
    return {'x': x, 'src': src, 'dst': dst, 'edge_type_4': edge_type_4, 'L0_gnn_rel_weight': _L0_gnn_in['rel_weight'], 'L0_gnn_root_weight': _L0_gnn_in['root_weight'], 'L0_gnn_rgcn_bias': _L0_gnn_in['rgcn_bias'], 'L0_gnn_att_weight': _L0_gnn_in['att_weight'], 'L0_gnn_att_bias': _L0_gnn_in['att_bias'], 'L0_mix_w_qkv': _L0_mix_in['w_qkv'], 'L0_mix_b_qkv': _L0_mix_in['b_qkv'], 'L0_mix_kln_g': _L0_mix_in['kln_g'], 'L0_mix_kln_b': _L0_mix_in['kln_b'], 'L0_mix_vln_g': _L0_mix_in['vln_g'], 'L0_mix_vln_b': _L0_mix_in['vln_b'], 'L0_mix_w1': _L0_mix_in['w1'], 'L0_mix_b1': _L0_mix_in['b1'], 'L0_mix_w2': _L0_mix_in['w2'], 'L0_mix_b2': _L0_mix_in['b2'], 'L0_ffn_attention_mask': _L0_ffn_in['attention_mask'], 'L0_ffn_wr': _L0_ffn_in['wr'], 'L0_ffn_br': _L0_ffn_in['br'], 'L0_ffn_w1': _L0_ffn_in['w1'], 'L0_ffn_b1': _L0_ffn_in['b1'], 'L0_ffn_w2': _L0_ffn_in['w2'], 'L0_ffn_b2': _L0_ffn_in['b2']}

def reference(x, src, dst, edge_type_4, L0_gnn_rel_weight, L0_gnn_root_weight, L0_gnn_rgcn_bias, L0_gnn_att_weight, L0_gnn_att_bias, L0_mix_w_qkv, L0_mix_b_qkv, L0_mix_kln_g, L0_mix_kln_b, L0_mix_vln_g, L0_mix_vln_b, L0_mix_w1, L0_mix_b1, L0_mix_w2, L0_mix_b2, L0_ffn_attention_mask, L0_ffn_wr, L0_ffn_br, L0_ffn_w1, L0_ffn_b1, L0_ffn_w2, L0_ffn_b2):
    import jax
    import jax.numpy as jnp

    def _L0_gnn_ref(node_features, edge_index, edge_type, rel_weight, root_weight, rgcn_bias, att_weight, att_bias):
        import jax, jax.numpy as jnp
        import numpy as np
        N_NODES = 50000
        N_EDGES = 25000
        C = 256
        R = 4

        def _rgcn(node_features, edge_index, edge_type, rel_weight, root_weight, rgcn_bias):
            N = node_features.shape[0]
            src, dst = (edge_index[0], edge_index[1])
            out = node_features @ root_weight + rgcn_bias
            num_rel = rel_weight.shape[0]
            for r in range(num_rel):
                trans = node_features @ rel_weight[r]
                mask = edge_type == r
                msg = jnp.where(mask[:, None], trans[src], 0.0)
                ssum = jax.ops.segment_sum(msg, dst, num_segments=N)
                cnt = jax.ops.segment_sum(mask.astype(node_features.dtype), dst, num_segments=N)
                out = out + ssum / jnp.maximum(cnt, 1.0)[:, None]
            return out
        u0 = _rgcn(node_features, edge_index, edge_type, rel_weight, root_weight, rgcn_bias)
        cat = jnp.concatenate([u0, node_features], axis=1)
        a = jax.nn.sigmoid(cat @ att_weight.T + att_bias)
        h = jnp.tanh(u0) * a + node_features * (1.0 - a)
        return h

    def _L0_mix_ref(x, w_qkv, b_qkv, kln_g, kln_b, vln_g, vln_b, w1, b1, w2, b2):
        import jax, jax.numpy as jnp
        import numpy as np
        MIDC = 256
        HEADS = 8
        HEADC = MIDC // HEADS
        EPS = 1e-05

        def _ln(x, gamma, beta):
            mu = jnp.mean(x, axis=-1, keepdims=True)
            var = jnp.var(x, axis=-1, keepdims=True)
            return (x - mu) * jax.lax.rsqrt(var + EPS) * gamma + beta
        B, HW, C = x.shape
        bias = x
        qkv = (x @ w_qkv + b_qkv).reshape(B, HW, HEADS, 3 * HEADC)
        qkv = qkv.transpose(0, 2, 1, 3)
        q, k, v = jnp.split(qkv, 3, axis=-1)
        k = _ln(k, kln_g, kln_b)
        v = _ln(v, vln_g, vln_b)
        kv = jnp.einsum('bhnd,bhne->bhde', k, v) / HW
        out = jnp.einsum('bhnd,bhde->bhne', q, kv)
        out = out.transpose(0, 2, 1, 3).reshape(B, HW, C)
        ret = out + bias
        h = jax.nn.gelu(ret @ w1 + b1, approximate=False)
        return h @ w2 + b2 + bias

    def _L0_ffn_ref(x, attention_mask, wr, br, w1, b1, w2, b2):
        import jax, jax.numpy as jnp
        import numpy as np
        B, S, D = (8, 128, 256)
        H = 4 * D
        CAPACITY = 0.5
        b, s, d = x.shape
        weights = (jnp.einsum('bsd,do->bso', x, wr) + br)[..., 0]
        k = max(1, int(CAPACITY * s))
        kk = k - 1 if k > 1 else 1
        _, idx = jax.lax.top_k(weights, k)
        sel_idx = idx[:, :kk]
        sel = jnp.take_along_axis(x, sel_idx[:, :, None], axis=1)
        h = jax.nn.gelu(jnp.einsum('bkd,dh->bkh', sel, w1) + b1)
        y = jnp.einsum('bkh,hd->bkd', h, w2) + b2
        w_sel = jnp.take_along_axis(weights, sel_idx, axis=1)
        y = y * w_sel[..., None]
        batch_idx = jnp.arange(b)[:, None]
        processed = jnp.zeros_like(x).at[batch_idx, sel_idx].set(y)
        return processed + x
    edge_index = jnp.stack([src, dst])
    xn = _layernorm(x, axis=-1)
    x = x + _L0_gnn_ref(xn, edge_index, edge_type_4, L0_gnn_rel_weight, L0_gnn_root_weight, L0_gnn_rgcn_bias, L0_gnn_att_weight, L0_gnn_att_bias) + _L0_mix_ref(xn[None], L0_mix_w_qkv, L0_mix_b_qkv, L0_mix_kln_g, L0_mix_kln_b, L0_mix_vln_g, L0_mix_vln_b, L0_mix_w1, L0_mix_b1, L0_mix_w2, L0_mix_b2)[0]
    x = x + _L0_ffn_ref(_layernorm(x, axis=-1)[None], L0_ffn_attention_mask, L0_ffn_wr, L0_ffn_br, L0_ffn_w1, L0_ffn_b1, L0_ffn_w2, L0_ffn_b2)[0]
    return x

_drawn_inputs = setup_inputs


def setup_inputs(seed=0):
    import zlib

    import numpy as np

    out = dict(_drawn_inputs(seed))
    spreads = {'L0_mix_b_qkv': (0.0, 0.323),
     'L0_mix_kln_g': (1.0, 0.6),
     'L0_mix_kln_b': (0.0, 0.551),
     'L0_mix_vln_g': (1.0, 0.6),
     'L0_mix_vln_b': (0.0, 0.489),
     'L0_mix_b1': (0.0, 0.319),
     'L0_mix_b2': (0.0, 0.1),
     'L0_ffn_b1': (0.0, 0.8),
     'L0_ffn_b2': (0.0, 0.8)}
    factors = {'L0_gnn_rgcn_bias': 22.629, 'L0_ffn_wr': 6.49, 'L0_ffn_w1': 7.251, 'L0_ffn_w2': 6.8}
    for name, (base, spread) in spreads.items():
        noise = np.random.default_rng([zlib.crc32(name.encode()), seed]).standard_normal(out[name].shape)
        drawn = base * np.exp(spread * noise) if base else spread * noise
        out[name] = jnp.asarray(drawn.astype(out[name].dtype))
    for name, factor in factors.items():
        out[name] = (out[name] * factor).astype(out[name].dtype)
    return out
```

```python
import concourse.bass as bass
from concourse import mybir
from contextlib import ExitStack

N = 3125
C = 256
EDGES = 50000
RELS = 4
HEADS, HEADC = 8, 32
HIDDEN = 1024
P = 128
TOK = 125
TILES = N // TOK
KEYS = TOK * RELS
WIN = 128
GROUP = 256
GROUPS = -(-EDGES // GROUP)
GATHERS = 2 * GROUPS
SLOTS = 7
NODE_GROUPS = 7
MIX_GROUPS = GROUPS - TILES * NODE_GROUPS
MIX_FIRST = TILES - MIX_GROUPS
ACC = (N - 1) * RELS + WIN
GENERAL_WINDOWS = -(-N * RELS // WIN)
KEPT = 1561
EPS = 1e-5
PAD_NODE = 1000000
HCHUNKS = HIDDEN // P


class Tile:

    def __init__(self, half, offset):
        self.half, self.offset = half, offset
        self.static = half is None
        self.i = offset if self.static else half * 2 + offset
        self.b = offset % 2
        self.u = offset // 2 if self.static else half + offset // 2

    def back(self, n):
        return Tile(self.half, self.offset - n)

    def exists(self):
        return not self.static or 0 <= self.offset < TILES


def steps(eng, step, first, last):
    stop = first + (TILES - first) // 2 * 2
    for i in range(first):
        step(Tile(None, i))
    with eng.Fori(0, (stop - first) // 2) as half:
        for k in range(2):
            step(Tile(half, first + k))
    for i in range(stop, last):
        step(Tile(None, i))


def wait_past(eng, sem, count):
    if not isinstance(count, int) or count > 0:
        eng.wait_ge(sem, count)


class Links:

    def __init__(self, eng, sem):
        self.eng, self.sem, self.start, self.n = eng, sem, 0, 0

    def at(self, start):
        self.start, self.n = start, 0

    def __call__(self, ins):
        self.n += 1
        ins.then_inc(self.sem, 1)
        self.eng.wait_ge(self.sem, self.start + self.n)


def gps_block(nc, x, src, dst, etype, rel_w, root_w, gnn_b, att_w, att_b, w_qkv, b_qkv, kln_g, kln_b,
              vln_g, vln_b, mix_w1, mix_b1, mix_w2, mix_b2, wr, br, ffn_w1, ffn_b1, ffn_w2, ffn_b2, out):
    f32, f16, i32, u16 = mybir.dt.float32, mybir.dt.float16, mybir.dt.int32, mybir.dt.uint16
    ALU, ACT, AX = mybir.AluOpType, mybir.ActivationFunctionType, mybir.AxisListType
    ds = bass.ds

    table = nc.dram_tensor("table", (N, 2 * C), f16).ap()
    xn_d = nc.dram_tensor("xn_d", (N, C), f32).ap()
    base1_d = nc.dram_tensor("base1_d", (N, C), f32).ap()
    base_d = nc.dram_tensor("base_d", (N, C), f32).ap()
    xt_d = nc.dram_tensor("xt_d", (TILES, P, 2 * TOK), f32).ap()

    with ExitStack() as ctx:
        def sb(name, shape, dt):
            return ctx.enter_context(nc.sbuf_tensor(name, shape, dt))

        acc = sb("acc", [P, 2 * ACC], f32)
        acc3 = acc[:, :].rearrange("p (h k) -> p h k", h=2)
        cnt = sb("cnt", [P, ACC], u16)
        relw = sb("relw", [P, 2, RELS, C + 1], f32)
        rootw = sb("rootw", [P, 2, C + 1], f32)
        fw = sb("fw", [P, 4096], f32)
        w1 = fw[:, 0:2048].rearrange("p (a n) -> p a n", a=2)
        w2 = fw[:, 2048:4096].rearrange("p (a n) -> p a n", a=HCHUNKS)
        rows = sb("rows", [P, SLOTS, 2 * C], f16)
        onehot = sb("onehot", [P, SLOTS, WIN], f16)
        key_t = sb("key_t", [P, 2, GROUPS], f32)
        src_t = sb("src_t", [P, GATHERS], i32)
        index = sb("index", [P, 2, SLOTS], i32)
        ident = sb("ident", [P, P], f32)
        onesf = sb("onesf", [P, P], f32)
        onesh = sb("onesh", [P, P], f16)
        keyrow = sb("keyrow", [P, WIN], f16)
        base_row = sb("base_row", [1, 2 * P], i32)
        flag_row = sb("flag_row", [1, 2 * P], i32)
        any_left = sb("any_left", [1, 1], i32)
        biases = sb("biases", [65, C + 1], f32)
        fb1 = sb("fb1", [P, HCHUNKS], f32)
        wr_rep = sb("wr_rep", [P, C], f32)
        br_rep = sb("br_rep", [P, 1], f32)
        w_all = sb("w_all", [P, TILES], f32)
        small = sb("small", [P, 64], f32)
        stats = sb("stats", [P, 2, 64], f32)
        ctmp = sb("ctmp", [P, 2304], f32)
        work = sb("work", [P, 5000], f32)

        tri = sb("tri", [P, P], f32)

        eps_col = small[:, 40:41]
        att2, attb, mb1, bq = small[:, 20:22], small[0:1, 22:23], small[:, 24:26], small[:, 26:28]
        kg, kb, vg, vb = (small[:, 28 + k:29 + k] for k in range(4))

        mw1, wqT, b1w, wq = (ctmp[:, 512 * k:512 * k + 512].rearrange("p (a n) -> p a n", a=2) for k in range(4))
        a_rep = ctmp[:, 2048:2304]

        TEMP = 8500
        used = [2 * ACC - TEMP]

        def temp(n):
            used[0] += n
            assert used[0] <= 2 * ACC
            return acc[:, used[0] - n:used[0]]

        x_in = temp(512).rearrange("p (b n) -> p b n", b=2)
        xn = temp(512).rearrange("p (b n) -> p b n", b=2)
        tab = temp(512).bitcast(f16).rearrange("p (b n) -> p b n", b=2)
        base1 = temp(512).rearrange("p (b n) -> p b n", b=2)
        xt = temp(500).rearrange("p (b h n) -> p b h n", b=2, h=2)
        sq = temp(1024).rearrange("p (b n) -> p b n", b=2)
        kvn = temp(1024).rearrange("p (b n) -> p b n", b=2)
        wkv = temp(1024).rearrange("p (a n) -> p a n", a=2)
        wqkv = temp(1536).rearrange("p (a n) -> p a n", a=2)
        bkv = temp(512)
        bqkv = temp(768)
        means = temp(48)

        ep = [fw[:, 512 * k:512 * k + 512] for k in range(8)]
        src_g, dst_g, typ_g = [e.bitcast(i32).rearrange("p (b n) -> p b n", b=2) for e in ep[0:3]]
        src_f, dst_f, typ_f, key_f, left_f = [e.rearrange("p (b n) -> p b n", b=2) for e in ep[3:8]]
        tmp_g = work[:, 0:512].rearrange("p (b n) -> p b n", b=2)
        thr = work[:, 1024:1048]
        gcol = work[:, 1048:1050]
        thr_i = work[:, 1050:1074].bitcast(i32)
        gcol_i = work[:, 1074:1076].bitcast(i32)
        cmp_g = work[:, 1076:1124].rearrange("p (b n) -> p b n", b=2)
        base_g = work[:, 1124:1126]
        flag_g = work[:, 1126:1128]
        min_g = work[:, 1128:1130]
        done_g = work[:, 1130:1132]
        iota_i = work[:, 1132:1260].bitcast(i32)
        left_t = work[:, 1300:1300 + 2 * GROUPS].rearrange("p (s g) -> p s g", s=2)
        left_rel = work[:, 1960:1962]
        any_f = work[0:1, 1970:1971]
        gate_junk = work[:, 1700:1956]

        m_xt = work[:, 2000:2500].rearrange("p (b h n) -> p b h n", b=2, h=2)
        m_base = work[:, 2500:3012].rearrange("p (b n) -> p b n", b=2)
        m_h = work[:, 3012:3512].rearrange("p (b h n) -> p b h n", b=2, h=2)
        m_out = work[:, 3520:4032].rearrange("p (b n) -> p b n", b=2)
        weff = work[:, 0:512].rearrange("p (a n) -> p a n", a=2)
        mw2 = work[:, 512:1024].rearrange("p (a n) -> p a n", a=2)
        kv_t = work[:, 4032:4288].rearrange("p (a n) -> p a n", a=2)
        vec = work[:, 4288:4296]
        vrow = work[:, 4300:4812]
        beff = work[:, 4850:4852]
        grow = work[:, 4860:4892]

        sn = work[:, 0:1000].rearrange("p (h r n) -> p h r n", h=2, r=RELS)
        spread = work[:TOK, 1000:1500]
        inverse = work[:TOK, 4562:4566]
        hT = work[:, 1500:2500].rearrange("p (c n) -> p c n", c=HCHUNKS)
        n_xt = work[:, 2500:2750].rearrange("p (h n) -> p h n", h=2)
        n_xn = work[:, 2750:3006]
        n_base = work[:, 3006:3262]
        th = work[:, 3262:3518]
        x1 = work[:, 3518:3774]
        xn2 = work[:, 3774:4030]
        xt3 = work[:, 4030:4280].rearrange("p (h n) -> p h n", h=2)
        junk = work[:, 4280:4536]
        ta = work[:, 4540:4541]
        ga = work[:, 4541:4542]
        st2 = work[:, 4544:4550]
        mv2 = work[:, 4550:4552]
        nw = work[:, 4552:4560]
        wcol = work[:, 4560:4561]
        count_rows = sb("count_rows", [32 * (RELS - 1) + 1, TOK], f32)

        bank = [ctx.enter_context(nc.psum_tensor(f"bank{k}", [P, 512], f32)) for k in range(8)]

        def sem(name):
            return ctx.enter_context(nc.semaphore(name))

        def sems(names):
            return [sem(n) for n in names.split()]

        edges_cleared, edges_in, weights_in, small_in, mix_w_in, ffn_w_in = sems(
            "edges_cleared edges_in weights_in small_in mix_w_in ffn_w_in")
        pool_link, dve_link, act_link, pool_consts, keys_ready, acc_cleared, cnt_cleared = sems(
            "pool_link dve_link act_link pool_consts keys_ready acc_cleared cnt_cleared")
        prep_inputs, prep_turned, src_ready, rows_ready, keys_in_place, any_ready, tail_cleared = sems(
            "prep_inputs prep_turned src_ready rows_ready keys_in_place any_ready tail_cleared")
        x_loaded = sems("x_loaded0 x_loaded1")
        stored = sems("stored0 stored1")
        wkv_ready, stats_link, stats_order, stats_done, std_done, rstd_link, rstd_done = sems(
            "wkv_ready stats_link stats_order stats_done std_done rstd_link rstd_done")
        xn_done, hi_done, lo_done, base1_done, turned, xt_done = sems(
            "xn_done hi_done lo_done base1_done turned xt_done")
        kv_done, squared, var_done, kstd_done, kstd_link, kvn_done, kv_summed = sems(
            "kv_done squared var_done kstd_done kstd_link kvn_done kv_summed")
        wq_ready, vec_ready, vec_turned, vrow_ready, outer_done, kvt_ready, wq_turned, wqt_ready = sems(
            "wq_ready vec_ready vec_turned vrow_ready outer_done kvt_ready wq_turned wqt_ready")
        b1w_done, b1w_ready, weff_done, weff_ready, gnn_w_ready = sems(
            "b1w_done b1w_ready weff_done weff_ready gnn_w_ready")
        general_index, general_in, general_link, general_hot, general_sum, general_added = sems(
            "general_index general_in general_link general_hot general_sum general_added")
        pool_at_group, pe_at_group, general_turn = sems("pool_at_group pe_at_group general_turn")
        slot_in = [sem(f"slot_in{k}") for k in range(SLOTS)]
        index_ready, gathered, hot_done, group_summed, acc_added = sems(
            "index_ready gathered hot_done group_summed acc_added")
        mix_loaded, mix_stored = sems("mix_loaded0 mix_loaded1"), sems("mix_stored0 mix_stored1")
        h_done, gelu_done, mix_done, mixed = sems("h_done gelu_done mix_done mixed")
        n_xt_in, n_rows_in, final_stored = sems("n_xt_in n_rows_in final_stored")
        count_ready, count_turned, inverse_ready, spread_ready, inverse_spread = sems(
            "count_ready count_turned inverse_ready spread_ready inverse_spread")
        scaled, u_done, tanh_done, node_link, x1_done, rstd2_done = sems(
            "scaled u_done tanh_done node_link x1_done rstd2_done")
        route_link, xn2_done, base2_done, turned2, xt3_done, hid_done, gelu2_done, y_done, y_kept = sems(
            "route_link xn2_done base2_done turned2 xt3_done hid_done gelu2_done y_done y_kept")
        select_link, counts_ready, counts_summed, chosen = sems("select_link counts_ready counts_summed chosen")

        block = ctx.enter_context(nc.Block())

        def rows_of(t, ap):
            return ap[ds(t.i * TOK, TOK), :] if not t.static else ap[t.i * TOK:(t.i + 1) * TOK, :]

        def span(start, n):
            return slice(start, start + n) if isinstance(start, int) else ds(start, n)

        def slot_of(g, k):
            return (g * 2 + k) % SLOTS

        def tile_of(t, ap):
            return ap[span(t.i, 1), :, :].rearrange("a p n -> p (a n)")

        @block.sync
        def _(sp):
            sp.dma_start(wqkv, w_qkv.rearrange("(a p) n -> p a n", p=P)).then_inc(weights_in, 16)
            sp.dma_start(bqkv[0:1, :], b_qkv.rearrange("(a n) -> a n", a=1)).then_inc(weights_in, 16)

            def norm_step(t):
                if t.exists():
                    wait_past(sp, base1_done, t.i - 1)
                    sp.dma_start(x_in[:TOK, t.b, :], rows_of(t, x)).then_inc(x_loaded[t.b], 16)
                if t.static and t.offset == 0:
                    first_loads()
                s = t.back(1)
                if s.exists():
                    sp.wait_ge(lo_done, s.i + 1)
                    sp.dma_start(rows_of(s, table), tab[:TOK, s.b, :]).then_inc(stored[s.b], 16)
                    sp.dma_start(rows_of(s, xn_d), xn[:TOK, s.b, :]).then_inc(stored[s.b], 16)
                    sp.wait_ge(base1_done, s.i + 1)
                    sp.dma_start(rows_of(s, base1_d), base1[:TOK, s.b, :]).then_inc(stored[s.b], 16)
                    sp.wait_ge(xt_done, s.i + 1)
                    sp.dma_start(tile_of(s, xt_d), xt[:, s.b, :, :].rearrange("p h n -> p (h n)"))\
                      .then_inc(stored[s.b], 16)

            def first_loads():
                sp.wait_ge(edges_cleared, 1)
                tail = EDGES - (GROUPS - 1) * GROUP
                full = GROUPS - 1 - P
                for ap, d in ((src_g, src), (dst_g, dst), (typ_g, etype)):
                    sp.dma_start(ap[:, 0, :], d[0:P * GROUP].rearrange("(p n) -> p n", n=GROUP)).then_inc(edges_in, 16)
                    sp.dma_start(ap[0:full, 1, :], d[P * GROUP:(GROUPS - 1) * GROUP].rearrange("(p n) -> p n", n=GROUP))\
                      .then_inc(edges_in, 16)
                    sp.dma_start(ap[full:full + 1, 1, 0:tail], d[EDGES - tail:EDGES].rearrange("(p n) -> p n", p=1))\
                      .then_inc(edges_in, 16)
                for to, ap in ((mw1, mix_w1.rearrange("(a p) n -> p a n", p=P)),
                               (rootw[:, :, 0:C], root_w.rearrange("(a p) n -> p a n", p=P)),
                               (relw[:, 0, :, 0:C], rel_w[:, 0:P, :].rearrange("r p n -> p r n")),
                               (relw[:, 1, :, 0:C], rel_w[:, P:C, :].rearrange("r p n -> p r n")),
                               (a_rep, att_w[0:1, 0:C].broadcast_to([P, C])),
                               (att2, att_w[0:1, C:2 * C].rearrange("o (a p) -> p (o a)", p=P)),
                               (biases[0:1, 0:C], gnn_b.rearrange("(a n) -> a n", a=1)),
                               (biases[32:33, 0:C], mix_b2.rearrange("(a n) -> a n", a=1)),
                               (biases[64:65, 0:C], ffn_b2.rearrange("(a n) -> a n", a=1)),
                               (attb, att_b.rearrange("(a n) -> a n", a=1)),
                               (wr_rep[:, :], wr.rearrange("c o -> o c").broadcast_to([P, C])),
                               (br_rep[:, :], br.rearrange("(a n) -> a n", a=1).broadcast_to([P, 1])),
                               (fb1[:, :], ffn_b1.rearrange("(c p) -> p c", p=P)),
                               (mb1, mix_b1.rearrange("(c p) -> p c", p=P)),
                               (grow, kln_g.rearrange("(a n) -> a n", a=1).broadcast_to([P, HEADC]))):
                    sp.dma_start(to, ap, allow_slow_non_contiguous=True).then_inc(small_in, 16)
                for to, g in ((kg, kln_g), (kb, kln_b), (vg, vln_g), (vb, vln_b)):
                    for h in range(4):
                        sp.dma_start(to[h * HEADC:(h + 1) * HEADC, :], g.rearrange("(n a) -> n a", a=1))\
                          .then_inc(small_in, 16)
                for h in range(HEADS):
                    sp.dma_start(bq[(h % 4) * HEADC:(h % 4 + 1) * HEADC, h // 4:h // 4 + 1],
                                 b_qkv[h * 3 * HEADC:h * 3 * HEADC + HEADC].rearrange("(n a) -> n a", a=1))\
                      .then_inc(small_in, 16)

            steps(sp, norm_step, 4, TILES + 1)

            sp.wait_ge(stored[0], 64 * 13)
            sp.wait_ge(stored[1], 64 * 12)
            sp.dma_start(mw2, mix_w2.rearrange("(a p) n -> p a n", p=P)).then_inc(mix_w_in, 16)
            sp.wait_ge(prep_turned, 4)
            sp.dma_start(w1, ffn_w1.rearrange("(a p) n -> p a n", p=P)).then_inc(ffn_w_in, 16)
            sp.dma_start(w2, ffn_w2.rearrange("(c p) n -> p c n", p=P)).then_inc(ffn_w_in, 16)

            def mix_step(t):
                if t.exists():
                    wait_past(sp, h_done, t.i - 1)
                    wait_past(sp, mixed, t.i - 1)
                    sp.dma_start(m_xt[:, t.b, :, :].rearrange("p h n -> p (h n)"), tile_of(t, xt_d))\
                      .then_inc(mix_loaded[t.b], 16)
                    sp.dma_start(m_base[:TOK, t.b, :], rows_of(t, base1_d)).then_inc(mix_loaded[t.b], 16)
                s = t.back(2)
                if s.exists():
                    sp.wait_ge(mixed, s.i + 1)
                    sp.dma_start(rows_of(s, base_d), m_out[:TOK, s.b, :]).then_inc(mix_stored[s.b], 16)

            steps(sp, mix_step, MIX_FIRST + 2, TILES + 2)
            sp.wait_ge(mix_stored[0], 16 * 13)
            sp.wait_ge(mix_stored[1], 16 * 12)

            def node_step(t):
                if t.exists():
                    if t.static and t.offset == 0:
                        sp.wait_ge(h_done, TILES)
                        sp.wait_ge(mixed, TILES)
                    wait_past(sp, u_done, t.i)
                    sp.dma_start(n_xt.rearrange("p h n -> p (h n)"), tile_of(t, xt_d)).then_inc(n_xt_in, 16)
                    wait_past(sp, x1_done, t.i)
                    sp.dma_start(n_xn[:TOK, :], rows_of(t, xn_d)).then_inc(n_rows_in, 16)
                    sp.dma_start(n_base[:TOK, :], rows_of(t, base_d)).then_inc(n_rows_in, 16)

            steps(sp, node_step, 4, TILES)

            with sp.Fori(0, 5) as c:
                sp.wait_ge(chosen, c * 5 + 5)
                sp.dma_start(out[ds(c * (5 * TOK), 5 * TOK), :].rearrange("(t p) n -> p t n", p=TOK),
                             acc[:TOK, ds(c * (5 * KEYS), 5 * KEYS)].rearrange("p (t k) -> p t k", k=KEYS)[:, :, 0:C])\
                  .then_inc(final_stored, 16)
            sp.wait_ge(final_stored, 16 * 5)

        @block.gpsimd
        def _(pool):
            link = Links(pool, pool_link)
            pool.memset(src_g, 0)
            pool.memset(typ_g, 0)
            link(pool.memset(dst_g, PAD_NODE))
            pool.sem_inc(edges_cleared, 1)
            link(pool.memset(ident[:, :], 0.0))
            link(pool.affine_select(out=ident[:, :], in_=ident[:, :], compare_op=ALU.not_equal, fill=1.0, base=0,
                                    pattern=[[-1, P]], channel_multiplier=1))
            pool.memset(onesf[:, :], 1.0)
            link(pool.memset(onesh[:, :], 1.0))
            link(pool.affine_select(out=tri[:, :], in_=onesf[:, :], compare_op=ALU.is_gt, fill=0.0, base=0,
                                    pattern=[[1, P]], channel_multiplier=-1))
            link(pool.iota(iota_i, pattern=[[1, WIN]], base=0, channel_multiplier=0))
            link(pool.tensor_copy(keyrow[:, :], iota_i))
            pool.sem_inc(pool_consts, 1)
            pool.iota(thr_i, pattern=[[NODE_GROUPS, TILES - 1]], base=MIX_GROUPS + NODE_GROUPS, channel_multiplier=0)
            link(pool.iota(gcol_i, pattern=[[P, 2]], base=0, channel_multiplier=1))
            pool.tensor_copy(thr, thr_i)
            link(pool.tensor_copy(gcol, gcol_i))
            for blk in range(2):
                last = pool.tensor_scalar(cmp_g[:, blk, :], thr, gcol[:, blk:blk + 1], None, ALU.is_le)
            link(last)
            pool.wait_ge(edges_in, 16 * 9)
            pool.tensor_copy(src_f, src_g)
            pool.tensor_copy(typ_f, typ_g)
            link(pool.tensor_copy(dst_f, dst_g))
            pool.sem_inc(keys_ready, 1)
            pool.memset(cnt[:, :], 0).then_inc(cnt_cleared, 1)
            pool.memset(acc[:, 0:2 * ACC - TEMP], 0.0).then_inc(acc_cleared, 1)

            pool.wait_ge(stored[0], 64 * 13)
            pool.wait_ge(stored[1], 64 * 12)
            pool.wait_ge(src_ready, 1)
            pool.wait_ge(any_ready, 1)

            def gather(into, idx):
                return pool.indirect_dma_start(into, None, table, bass.IndirectOffsetOnAxis(ap=idx, axis=0))

            left = pool.value_load(any_left[0:1, 0:1], min_val=0, max_val=1)
            with pool.If(left > 0):
                with pool.Fori(0, GROUPS) as g:
                    pool.sem_inc(pool_at_group, 1)
                    pool.wait_ge(general_turn, g + 1)
                    pool.tensor_copy(index[:, 0, 0:2], src_t[:, ds(g * 2, 2)]).then_inc(general_index, 1)
                    pool.wait_ge(general_index, g * 2 + 1)
                    pool.sem_inc(general_index, 1)
                    for k in range(2):
                        gather(rows[:, k, :], index[:, 0, k:k + 1]).then_inc(general_in, 16)
                    pool.wait_ge(general_in, g * 32 + 32)
                pool.wait_ge(general_added, GROUPS * GENERAL_WINDOWS + 1)

            def gather_round(a):
                for half in range(2):
                    pool.tensor_copy(index[:, half, :], src_t[:, span(a * (2 * SLOTS) + half * SLOTS, SLOTS)])\
                        .then_inc(index_ready, 1)
                    pool.wait_ge(index_ready, a * 2 + (half + 1))
                    for k in range(SLOTS):
                        pool.wait_ge(group_summed, a * (2 * SLOTS) + (half * SLOTS + k + 1))
                        wait_past(pool, slot_in[(k - 3) % SLOTS], a * 32 + 16 * (half + (k >= 3)))
                        pool.sem_inc(gathered, 1)
                        gather(rows[:, k, :], index[:, half, k:k + 1]).then_inc(slot_in[k], 16)

            gather_round(0)
            with pool.Fori(1, GATHERS // (2 * SLOTS)) as a:
                gather_round(a)
            for k in range(SLOTS - 3, SLOTS):
                pool.wait_ge(slot_in[k], GATHERS // SLOTS * 16)
                pool.sem_inc(gathered, 1)

        @block.scalar
        def _(act):
            link = Links(act, act_link)

            act.wait_ge(weights_in, 32)
            for a in range(2):
                last = act.activation(wq[:, a, :].rearrange("p (h j) -> p h j", h=HEADS),
                                      wqkv[:, a, :].rearrange("p (h t j) -> p h t j", h=HEADS, t=3)[:, :, 0, :], ACT.Copy)
            last.then_inc(wq_ready, 1)

            def norm_step(t):
                s = t.back(1)
                if t.exists():
                    act.wait_ge(stats_done, t.i + 1)
                    wait_past(act, rstd_done, t.i - 1)
                    act.activation(stats[:TOK, t.b, 8:9], stats[:TOK, t.b, 7:8], ACT.Sqrt, bias=eps_col[:TOK, :])\
                       .then_inc(std_done, 1)
                    act.wait_ge(rstd_done, t.i + 1)
                    wait_past(act, stored[t.b], t.u * 64)
                    wait_past(act, turned, t.i - 1)
                    wait_past(act, base1_done, t.i - 1)
                    act.activation(xn[:TOK, t.b, :], x_in[:TOK, t.b, :], ACT.Identity, bias=stats[:TOK, t.b, 10:11],
                                   scale=stats[:TOK, t.b, 9:10]).then_inc(xn_done, 1)
                    act.wait_ge(xn_done, t.i + 1)
                    act.activation(tab[:TOK, t.b, 0:C], xn[:TOK, t.b, :], ACT.Copy).then_inc(hi_done, 1)
                if s.exists():
                    act.wait_ge(kv_done, s.i + 1)
                    wait_past(act, var_done, s.i - 1)
                    act.activation(sq[:TOK, s.b, :], bank[2 + s.b][:TOK, :], ACT.Square).then_inc(squared, 1)
                if t.exists():
                    act.wait_ge(turned, t.i + 1)
                    wait_past(act, kv_done, t.i - 1)
                    act.activation(xt[:, t.b, :, :], bank[t.b][:, 0:2 * TOK].rearrange("p (h n) -> p h n", h=2),
                                   ACT.Copy).then_inc(xt_done, 1)
                if s.exists():
                    act.wait_ge(var_done, s.i + 1)
                    act.activation(stats[:TOK, s.b, 32:48], stats[:TOK, s.b, 16:32], ACT.Sqrt, bias=eps_col[:TOK, :],
                                   scale=1.0 / HEADC).then_inc(kstd_done, 1)

            act.wait_ge(wkv_ready, 1)
            steps(act, norm_step, 4, TILES + 1)

            act.wait_ge(prep_turned, 1)
            act.activation(src_t[:, :].rearrange("p (g s) -> p s g", s=2),
                           bank[5][:, 0:2 * GROUPS].rearrange("p (s g) -> p s g", s=2), ACT.Copy)\
               .then_inc(src_ready, 1)
            act.wait_ge(prep_turned, 3)
            act.activation(base_row[:, :], bank[7][0:1, 0:2 * P], ACT.Copy, scale=float(RELS))
            act.activation(flag_row[:, :], bank[7][0:1, 2 * P:4 * P], ACT.Copy).then_inc(rows_ready, 1)

            act.wait_ge(vec_turned, 1)
            act.activation(vrow[0:2, :], bank[0][0:2, :], ACT.Copy).then_inc(vrow_ready, 1)
            act.wait_ge(wq_turned, 1)
            act.activation(wqT.rearrange("p a n -> p (a n)"), bank[1][:, :], ACT.Copy).then_inc(wqt_ready, 1)
            act.wait_ge(b1w_done, 1)
            act.activation(b1w.rearrange("p a n -> p (a n)"), bank[2][:, :], ACT.Copy, scale=1.0 / N)\
               .then_inc(b1w_ready, 1)

            act.wait_ge(weff_ready, 1)

            def mix_step(t):
                if t.exists():
                    act.wait_ge(h_done, t.i + 1)
                    wait_past(act, mix_done, t.i - 1)
                    for o in range(2):
                        last = act.activation(m_h[:, t.b, o, :], bank[2 + t.b][:, o * TOK:(o + 1) * TOK], ACT.Gelu,
                                              bias=beff[:, o:o + 1])
                    last.then_inc(gelu_done, 1)

            steps(act, mix_step, MIX_FIRST + 2, TILES)

            def node_step(t):
                s, r = t.back(1), t.back(2)
                if r.exists():
                    act.wait_ge(turned2, r.i + 1)
                    wait_past(act, hid_done, r.i * 2)
                    act.activation(xt3, bank[3][:, 0:2 * TOK].rearrange("p (h n) -> p h n", h=2), ACT.Copy)\
                       .then_inc(xt3_done, 1)
                if s.exists():
                    act.wait_ge(inverse_ready, s.i + 1)
                    wait_past(act, inverse_spread, s.i)
                    for k in range(RELS):
                        last = act.activation(spread[:, k * TOK:(k + 1) * TOK], ident[:TOK, 0:TOK], ACT.Copy,
                                              scale=inverse[:, k:k + 1])
                    last.then_inc(spread_ready, 1)
                if r.exists():
                    for half in range(2):
                        act.wait_ge(hid_done, r.i * 2 + half + 1)
                        wait_past(act, y_done, r.i)
                        for c in range(4 * half, 4 * half + 4):
                            k = c - 4 * half
                            last = act.activation(hT[:, c, :], bank[4 + half][:, k * TOK:(k + 1) * TOK],
                                                  ACT.Gelu_apprx_tanh, bias=fb1[:, c:c + 1])
                        last.then_inc(gelu2_done, 1)
                if s.exists():
                    act.wait_ge(u_done, s.i + 1)
                    wait_past(act, x1_done, s.i)
                    act.activation(th[:TOK, :], bank[2][:TOK, 0:C], ACT.Tanh)
                    act.activation(ta[:TOK, :], bank[2][:TOK, C:C + 1], ACT.Tanh, scale=0.5).then_inc(tanh_done, 1)
                if r.exists():
                    act.wait_ge(y_done, r.i + 1)
                    act.activation(acc[:TOK, span(r.i * KEYS, C)], bank[6][:TOK, 0:C], ACT.Copy).then_inc(y_kept, 1)
                if s.exists():
                    act.wait_ge(rstd2_done, s.i + 1)
                    wait_past(act, turned2, s.i)
                    wait_past(act, base2_done, s.i)
                    act.activation(xn2[:TOK, :], x1[:TOK, :], ACT.Identity, bias=nw[:TOK, 7:8], scale=nw[:TOK, 6:7])\
                       .then_inc(xn2_done, 1)

            steps(act, node_step, 4, TILES + 2)

        @block.vector
        def _(dve):
            link = Links(dve, dve_link)
            dve.memset(eps_col, EPS)
            link(dve.memset(vrow[0:1, :], 0.0))
            dve.wait_ge(weights_in, 32)
            kv_view = wqkv.rearrange("p a (h t j) -> p a h t j", h=HEADS, t=3)
            for a in range(2):
                for t in range(2):
                    dve.reduce_sum(means[:, 16 * a + 8 * t:16 * a + 8 * t + 8], kv_view[:, a, :, 1 + t, :], axis=AX.X)
            for t in range(2):
                last = dve.reduce_sum(means[0:1, 32 + 8 * t:40 + 8 * t],
                                      bqkv[0:1, :].rearrange("p (h t j) -> p h t j", h=HEADS, t=3)[:, :, 1 + t, :],
                                      axis=AX.X)
            link(last)
            link(dve.tensor_scalar(means[:, 0:32], means[:, 0:32], 1.0 / HEADC, None, ALU.mult))
            link(dve.tensor_scalar(means[0:1, 32:48], means[0:1, 32:48], 1.0 / HEADC, None, ALU.mult))
            for a in range(2):
                for t in range(2):
                    m = 16 * a + 8 * t
                    dve.tensor_tensor(wkv[:, a, C * t:C * t + C].rearrange("p (h j) -> p h j", h=HEADS),
                                      kv_view[:, a, :, 1 + t, :],
                                      means[:, m:m + 8].rearrange("p (h o) -> p h o", o=1).broadcast_to([P, HEADS, HEADC]),
                                      ALU.subtract)
            for t in range(2):
                m = 32 + 8 * t
                last = dve.tensor_tensor(
                    bkv[0:1, C * t:C * t + C].rearrange("p (h j) -> p h j", h=HEADS),
                    bqkv[0:1, :].rearrange("p (h t j) -> p h t j", h=HEADS, t=3)[:, :, 1 + t, :],
                    means[0:1, m:m + 8].rearrange("p (h o) -> p h o", o=1).broadcast_to([1, HEADS, HEADC]), ALU.subtract)
            last.then_inc(wkv_ready, 1)

            def norm_step(t):
                s = t.back(1)
                if t.exists():
                    if t.static and t.offset == 0:
                        take_stats(t)
                    dve.wait_ge(std_done, t.i + 1)
                    wait_past(dve, xn_done, t.i - 1)
                    dve.reciprocal(stats[:TOK, t.b, 9:10], stats[:TOK, t.b, 8:9]).then_inc(rstd_link, 1)
                    dve.wait_ge(rstd_link, t.i + 1)
                    dve.tensor_scalar(stats[:TOK, t.b, 10:11], stats[:TOK, t.b, 6:7], stats[:TOK, t.b, 9:10], -1.0,
                                      ALU.mult, ALU.mult).then_inc(rstd_done, 1)
                    n = t.back(-1)
                    if not t.static or n.exists():
                        take_stats(n)
                    dve.wait_ge(hi_done, t.i + 1)
                    dve.tensor_tensor(tab[:TOK, t.b, C:2 * C], xn[:TOK, t.b, :], tab[:TOK, t.b, 0:C], ALU.subtract)\
                       .then_inc(lo_done, 1)
                    wait_past(dve, stored[t.b], t.u * 64)
                    dve.scalar_tensor_tensor(base1[:TOK, t.b, :], xn[:TOK, t.b, :], 2.0, x_in[:TOK, t.b, :],
                                             ALU.mult, ALU.add).then_inc(base1_done, 1)
                if s.exists():
                    dve.wait_ge(squared, s.i + 1)
                    dve.reduce_sum(stats[:TOK, s.b, 16:32], sq[:TOK, s.b, :].rearrange("p (g j) -> p g j", j=HEADC),
                                   axis=AX.X).then_inc(var_done, 1)
                    dve.wait_ge(kstd_done, s.i + 1)
                    dve.reciprocal(stats[:TOK, s.b, 48:64], stats[:TOK, s.b, 32:48]).then_inc(kstd_link, 1)
                    dve.wait_ge(kstd_link, s.i + 1)
                    wait_past(dve, kv_summed, s.i - 1)
                    dve.tensor_tensor(kvn[:TOK, s.b, :].rearrange("p (g j) -> p g j", j=HEADC),
                                      bank[2 + s.b][:TOK, :].rearrange("p (g j) -> p g j", j=HEADC),
                                      stats[:TOK, s.b, 48:64].rearrange("p (g o) -> p g o", o=1)
                                      .broadcast_to([TOK, 16, HEADC]), ALU.mult).then_inc(kvn_done, 1)

            def take_stats(t):
                dve.wait_ge(x_loaded[t.b], t.u * 16 + 16)
                wait_past(dve, rstd_done, t.i - 1)
                dve.bn_stats(stats[:TOK, t.b, 0:6], x_in[:TOK, t.b, :]).then_inc(stats_link, 1)
                dve.wait_ge(stats_link, t.i + 1)
                dve.sem_inc(stats_order, 1)
                dve.bn_aggr(stats[:TOK, t.b, 6:8], stats[:TOK, t.b, 0:6]).then_inc(stats_done, 1)

            steps(dve, norm_step, 4, TILES + 1)

            dve.wait_ge(keys_ready, 1)
            dve.tensor_reduce(min_g, dst_f, axis=AX.X, op=ALU.min)
            link(dve.reduce_sum(done_g, cmp_g, axis=AX.X))
            link(dve.tensor_scalar(done_g, done_g, float(TOK), None, ALU.mult))
            link(dve.tensor_tensor(base_g, min_g, done_g, ALU.max))
            wide = [P, 2, GROUP]
            link(dve.tensor_tensor(key_f, dst_f, base_g.rearrange("p (b o) -> p b o", o=1).broadcast_to(wide), ALU.subtract))
            link(dve.scalar_tensor_tensor(key_f, key_f, float(RELS), typ_f, ALU.mult, ALU.add))
            dve.tensor_scalar(tmp_g, key_f, -0.5, None, ALU.is_lt)
            link(dve.scalar_tensor_tensor(left_f, dst_f, float(RELS), typ_f, ALU.mult, ALU.add))
            link(dve.scalar_tensor_tensor(tmp_g, key_f, WIN - 0.5, tmp_g, ALU.is_gt, ALU.add))
            link(dve.scalar_tensor_tensor(left_f, left_f, 1e6, tmp_g, ALU.add, ALU.mult))
            link(dve.tensor_scalar(left_f, left_f, -1e6, None, ALU.add))
            link(dve.tensor_scalar(tmp_g, left_f, -0.5, None, ALU.is_gt))
            link(dve.scalar_tensor_tensor(tmp_g, left_f, N * RELS - 0.5, tmp_g, ALU.is_lt, ALU.mult))
            link(dve.reduce_sum(flag_g, tmp_g, axis=AX.X))
            dve.sem_inc(prep_inputs, 1)

            dve.wait_ge(kv_summed, TILES)
            dve.wait_ge(stored[0], 64 * 13)
            dve.wait_ge(stored[1], 64 * 12)
            dve.wait_ge(wq_ready, 1)
            dve.memset(acc[:, 2 * ACC - TEMP:2 * ACC], 0.0).then_inc(tail_cleared, 1)

            dve.wait_ge(small_in, 16 * 39)
            for a in range(2):
                v = 4 * a
                dve.tensor_copy(vec[:, v:v + 1], vb)
                dve.tensor_tensor(vec[:, v + 1:v + 2], bank[4][:, 258 + a:259 + a], vg, ALU.mult)
                dve.tensor_tensor(small[:, a:a + 1], bank[4][:, 256 + a:257 + a], kg, ALU.mult)
                last = dve.tensor_copy(vec[:, v + 3:v + 4], kb)
            link(last)
            for a in range(2):
                last = dve.scalar_tensor_tensor(vec[:, 4 * a + 2:4 * a + 3], kb, float(N), small[:, a:a + 1],
                                                ALU.mult, ALU.add)
            last.then_inc(vec_ready, 1)
            dve.memset(kv_t, 0.0)
            dve.wait_ge(prep_turned, 2)
            dve.tensor_copy(key_t[:, :, :], bank[6][:, 0:2 * GROUPS].rearrange("p (s g) -> p s g", s=2))\
               .then_inc(keys_in_place, 1)
            dve.wait_ge(rows_ready, 1)
            link(dve.reduce_sum(any_f, flag_row[0:1, 0:GROUPS], axis=AX.X))
            link(dve.tensor_scalar(any_f, any_f, 0.5, None, ALU.is_gt))
            dve.tensor_copy(any_left[:, :], any_f)
            dve.wait_ge(prep_turned, 4)
            link(dve.tensor_copy(left_t, bank[5][:, 0:2 * GROUPS].rearrange("p (s g) -> p s g", s=2)))
            dve.sem_inc(any_ready, 1)

            dve.wait_ge(outer_done, 1)
            for a in range(2):
                for h in range(4):
                    lo, hi = h * HEADC, (h + 1) * HEADC
                    last = dve.scalar_tensor_tensor(kv_t[lo:hi, a, lo:hi], bank[4][lo:hi, a * P + lo:a * P + hi],
                                                    vg[lo:hi, :], grow[lo:hi, :], ALU.mult, ALU.mult)
            link(last)
            for a in range(2):
                for h in range(4):
                    lo, hi = h * HEADC, (h + 1) * HEADC
                    last = dve.tensor_tensor(kv_t[lo:hi, a, lo:hi], bank[3][lo:hi, a * P + lo:a * P + hi],
                                             kv_t[lo:hi, a, lo:hi], ALU.add)
            last.then_inc(kvt_ready, 1)

            link(dve.memset(biases[0:1, C:C + 1], 0.0))
            for h in range(2):
                for r in range(RELS):
                    link(dve.tensor_tensor_reduce(out=gate_junk, in0=relw[:, h, r, 0:C], in1=a_rep, scale=1.0,
                                                  scalar=0.0, op0=ALU.mult, op1=ALU.add,
                                                  accum_out=relw[:, h, r, C:C + 1]))
                link(dve.tensor_tensor_reduce(out=gate_junk, in0=rootw[:, h, 0:C], in1=a_rep, scale=1.0,
                                              scalar=0.0, op0=ALU.mult, op1=ALU.add, accum_out=small[:, 4 + h:5 + h]))
            link(dve.tensor_tensor_reduce(out=gate_junk[0:1, :], in0=biases[0:1, 0:C], in1=a_rep[0:1, :], scale=1.0,
                                          scalar=0.0, op0=ALU.mult, op1=ALU.add, accum_out=small[0:1, 6:7]))
            dve.tensor_tensor(rootw[:, :, C], small[:, 4:6], att2, ALU.add)
            dve.tensor_tensor(biases[0:1, C:C + 1], small[0:1, 6:7], attb, ALU.add).then_inc(gnn_w_ready, 1)

            dve.wait_ge(weff_done, 1)
            for a in range(2):
                dve.tensor_tensor(weff[:, a, :], bank[1][:, a * C:a * C + C], mw1[:, a, :], ALU.add)
            dve.tensor_tensor(beff[:, :], bank[3][:, 400:402], mb1, ALU.add).then_inc(weff_ready, 1)

            dve.wait_ge(acc_cleared, 1)
            dve.wait_ge(cnt_cleared, 1)
            dve.wait_ge(tail_cleared, 1)

            left = dve.value_load(any_left[0:1, 0:1], min_val=0, max_val=1)
            with dve.If(left > 0):
                dve.sem_inc(general_added, 1)
                with dve.Fori(0, GROUPS) as g:
                    dve.wait_ge(pool_at_group, g + 1)
                    dve.wait_ge(pe_at_group, g + 1)
                    dve.sem_inc(general_turn, 1)
                    flagged = dve.value_load(flag_row[0:1, ds(g, 1)], min_val=0, max_val=GROUP)
                    with dve.If(flagged > 0):
                        with dve.Fori(0, GENERAL_WINDOWS) as w:
                            with dve.If(w < 1):
                                dve.tensor_copy(left_rel, left_t[:, :, ds(g, 1)].rearrange("p s o -> p (s o)"))\
                                   .then_inc(general_link, 1)
                            with dve.Else():
                                dve.tensor_scalar(left_rel, left_rel, -float(WIN), None, ALU.add).then_inc(general_link, 1)
                            dve.wait_ge(general_link, g * GENERAL_WINDOWS + w + 1)
                            for k in range(2):
                                last = dve.tensor_scalar(onehot[:, k, :], keyrow[:, :], left_rel[:, k:k + 1], None,
                                                         ALU.is_equal)
                            last.then_inc(general_hot, 1)
                            dve.wait_ge(general_sum, g * GENERAL_WINDOWS + w + 1)
                            dve.wait_ge(general_added, g * GENERAL_WINDOWS + w + 1)
                            dve.tensor_tensor(acc3[:, :, ds(w * WIN, WIN)],
                                              bank[0][:, 0:2 * WIN].rearrange("p (h k) -> p h k", h=2),
                                              acc3[:, :, ds(w * WIN, WIN)], ALU.add)
                            dve.tensor_tensor(cnt[:, ds(w * WIN, WIN)], bank[0][:, 2 * WIN:3 * WIN],
                                              cnt[:, ds(w * WIN, WIN)], ALU.add).then_inc(general_added, 1)
                    with dve.Else():
                        dve.sem_inc(general_link, GENERAL_WINDOWS)
                        dve.sem_inc(general_hot, GENERAL_WINDOWS)
                        dve.sem_inc(general_added, GENERAL_WINDOWS)
                dve.wait_ge(general_added, GROUPS * GENERAL_WINDOWS + 1)

            def hot(g, slots):
                for k in range(2):
                    dve.wait_ge(group_summed, g * 2 + k + 1)
                    dve.tensor_scalar(onehot[:, span(slots[k], 1), :].rearrange("p o n -> p (o n)"), keyrow[:, :],
                                      key_t[:, k, span(g, 1)], None, ALU.is_equal).then_inc(hot_done, 1)

            def first_columns(g, n):
                _, cols = nc.values_load_multi_w_load_instructions(
                    base_row[0:1, span(g, n)], engines=[mybir.EngineType.DVE], min_val=0, max_val=ACC - WIN,
                    skip_runtime_bounds_check_because="a node's number times four")
                return cols

            def add(g, b, col):
                dve.wait_ge(group_summed, g * 2 + 2 + SLOTS)
                wait_past(dve, acc_added, g)
                dve.tensor_tensor(acc3[:, :, ds(col, WIN)], bank[b][:, 0:2 * WIN].rearrange("p (h k) -> p h k", h=2),
                                  acc3[:, :, ds(col, WIN)], ALU.add)
                dve.tensor_tensor(cnt[:, ds(col, WIN)], bank[b][:, 2 * WIN:3 * WIN], cnt[:, ds(col, WIN)], ALU.add)\
                   .then_inc(acc_added, 1)

            def mix_step(t):
                s = t.back(1)
                if s.exists():
                    dve.wait_ge(mix_done, s.i + 1)
                    dve.wait_ge(mix_loaded[s.b], s.u * 32 + 32)
                    wait_past(dve, mix_stored[s.b], s.u * 16)
                    dve.tensor_tensor(m_out[:TOK, s.b, :], bank[6 + s.b][:TOK, 0:C], m_base[:TOK, s.b, :], ALU.add)\
                       .then_inc(mixed, 1)
                g = t.i - MIX_FIRST
                if not t.static or 0 <= g < MIX_GROUPS:
                    hot(g + 2, [slot_of(g + 2, 0), slot_of(g + 2, 1)])
                    add(g, (t.b + MIX_FIRST) % 2, first_columns(g, 1)[0])

            dve.wait_ge(keys_in_place, 1)
            hot(0, [0, 1])
            hot(1, [2, 3])
            steps(dve, mix_step, MIX_FIRST + 2, TILES + 1)

            link(dve.memset(count_rows[:, :], 0.0))
            def take_counts(t):
                dve.wait_ge(acc_added, t.i * NODE_GROUPS + MIX_GROUPS + NODE_GROUPS)
                wait_past(dve, count_turned, t.i)
                for r in range(RELS):
                    k = 32 * r
                    last = dve.tensor_scalar(
                        count_rows[k:k + 1, :],
                        cnt[k:k + 1, span(t.i * KEYS, KEYS)].rearrange("p (n r) -> p n r", r=RELS)[:, :, r],
                        1.0, None, ALU.max)
                last.then_inc(count_ready, 1)

            def invert_counts(t):
                dve.wait_ge(count_turned, t.i + 1)
                if t.static and t.offset == 0:
                    dve.wait_ge(mix_done, TILES)
                dve.reciprocal(inverse, bank[7][:TOK, 0:32 * RELS].rearrange("p (r k) -> p r k", k=32)[:, :, 0]).then_inc(inverse_ready, 1)

            def scale_sums(t):
                dve.wait_ge(inverse_spread, t.i + 1)
                wait_past(dve, u_done, t.i)
                for h in range(2):
                    last = dve.tensor_tensor(sn[:, h, :, :],
                                             acc3[:, h, span(t.i * KEYS, KEYS)].rearrange("p (n r) -> p r n", r=RELS),
                                             bank[7][:, 0:KEYS].rearrange("p (r n) -> p r n", r=RELS), ALU.mult)
                last.then_inc(scaled, 1)

            NODE_LINKS = 14
            v, half, y, e, y_step = (nw[:TOK, k:k + 1] for k in (0, 1, 6, 2, 3))

            def blend(t, node):
                dve.wait_ge(tanh_done, t.i + 1)
                dve.wait_ge(n_rows_in, t.i * 32 + 32)
                wait_past(dve, xn2_done, t.i)
                dve.tensor_tensor(th[:TOK, :], th[:TOK, :], n_xn[:TOK, :], ALU.subtract)
                node(dve.tensor_scalar(ga[:TOK, :], ta[:TOK, :], 0.5, 0.5, ALU.mult, ALU.add))
                node(dve.scalar_tensor_tensor(x1[:TOK, :], th[:TOK, :], ga[:TOK, :], n_base[:TOK, :], ALU.mult, ALU.add))
                node(dve.bn_stats(st2[:TOK, :], x1[:TOK, :]))
                dve.sem_inc(x1_done, 1)
                node(dve.bn_aggr(mv2[:TOK, :], st2[:TOK, :]))

            def estimate(t, node):
                node(dve.tensor_scalar(v, mv2[:TOK, 1:2], EPS, None, ALU.add))
                dve.tensor_scalar(e, v, -0.5, None, ALU.mult)
                node(dve.tensor_scalar(half.bitcast(i32), v.bitcast(i32), 1, None, ALU.logical_shift_right))
                node(dve.tensor_scalar(y.bitcast(i32), half.bitcast(i32), -1.0, float(0x5f3759df), ALU.mult, ALU.add))

            def newton(node):
                node(dve.scalar_tensor_tensor(y_step, y, e, y, ALU.mult, ALU.mult))
                node(dve.scalar_tensor_tensor(y, y_step, 1.5, y, ALU.add, ALU.mult))

            def newton_end(t, node):
                newton(node)
                node(dve.tensor_scalar(nw[:TOK, 7:8], mv2[:TOK, 0:1], y, -1.0, ALU.mult, ALU.mult))
                assert node.n == NODE_LINKS, node.n
                dve.sem_inc(rstd2_done, 1)

            def route(t):
                dve.wait_ge(xn2_done, t.i + 1)
                dve.tensor_tensor_reduce(out=junk[:TOK, :], in0=xn2[:TOK, :], in1=wr_rep[:TOK, :], scale=1.0, scalar=0.0,
                                         op0=ALU.mult, op1=ALU.add, accum_out=wcol[:TOK, :]).then_inc(route_link, 1)
                dve.wait_ge(route_link, t.i + 1)
                dve.tensor_copy(w_all[:TOK, span(t.i, 1)], wcol[:TOK, :])
                dve.tensor_tensor(acc[:TOK, span(t.i * KEYS + ACC, C)], x1[:TOK, :], xn2[:TOK, :], ALU.add)\
                   .then_inc(base2_done, 1)

            def node_step(t):
                s, r = t.back(1), t.back(2)
                node = Links(dve, node_link)
                node.at(s.i * NODE_LINKS)
                if s.exists():
                    invert_counts(s)
                if t.exists():
                    cols = first_columns(t.i * NODE_GROUPS + MIX_GROUPS, NODE_GROUPS)
                for q in range(NODE_GROUPS):
                    if t.exists():
                        g = t.i * NODE_GROUPS + (MIX_GROUPS + q)
                        if not (t.static and g + 2 >= GROUPS):
                            hot(g + 2, [(2 * (MIX_GROUPS + t.b * NODE_GROUPS + q + 2) + k) % SLOTS for k in range(2)])
                        add(g, (MIX_GROUPS + t.b * NODE_GROUPS + q) % 2, cols[q])
                    if q == 1:
                        if r.exists():
                            route(r)
                        if s.exists():
                            scale_sums(s)
                    if q == 4 and s.exists():
                        blend(s, node)
                    if q == 5 and s.exists():
                        estimate(s, node)
                        newton(node)
                        newton(node)
                        newton_end(s, node)
                    if q == 6 and t.exists():
                        take_counts(t)

            steps(dve, node_step, 4, TILES + 2)

            dve.wait_ge(y_kept, TILES)
            dve.wait_ge(base2_done, TILES)
            pick = Links(dve, select_link)
            T, S = TOK, TILES

            def field(at, n):
                return work[:T, at:at + n]

            w, sign, hi_i, lo_i, hi, lo = (field(32 * k, S) for k in range(6))
            dve.wait_ge(turned2, TILES)
            pick(dve.tensor_scalar(w, w_all[:T, :], br_rep[:T, :], None, ALU.add))
            pick(dve.tensor_scalar(sign.bitcast(i32), w.bitcast(i32), 31, 0x7fffffff, ALU.arith_shift_right,
                                   ALU.bitwise_and))
            pick(dve.tensor_tensor(sign.bitcast(i32), sign.bitcast(i32), w.bitcast(i32), ALU.bitwise_xor))
            dve.tensor_scalar(hi_i.bitcast(i32), sign.bitcast(i32), 16, None, ALU.arith_shift_right)
            pick(dve.tensor_scalar(lo_i.bitcast(i32), sign.bitcast(i32), 0xffff, None, ALU.bitwise_and))
            dve.tensor_scalar(hi, hi_i.bitcast(i32), 32768.0, None, ALU.add)
            pick(dve.tensor_copy(lo, lo_i.bitcast(i32)))
            digits = keyrow[:T, 1:16]
            cur, step, thresholds, digit = field(240, 1), field(241, 1), field(248, 15), field(242, 1)
            per_row, hits = field(264, 15), field(280, 15)
            cmp = work[:T, 300:300 + 15 * S].rearrange("p (d s) -> p d s", d=15)
            low = field(700, S)

            def kth_largest(keys, rounds_before):
                dve.memset(step, 4096.0)
                pick(dve.memset(cur, 0.0))
                base_links = pick.start + pick.n
                ROUND_LINKS = 6
                with dve.Fori(0, 4) as r:
                    pick.at(r * ROUND_LINKS + base_links)
                    pick(dve.tensor_scalar(thresholds, digits, step, cur, ALU.mult, ALU.add))
                    pick(dve.tensor_tensor(cmp, keys.rearrange("p (o s) -> p o s", o=1).broadcast_to([T, 15, S]),
                                           thresholds.rearrange("p (d o) -> p d o", o=1).broadcast_to([T, 15, S]),
                                           ALU.is_ge))
                    dve.reduce_sum(per_row, cmp, axis=AX.X).then_inc(counts_ready, 1)
                    dve.wait_ge(counts_summed, r + (rounds_before + 1))
                    pick(dve.tensor_scalar(hits, bank[0][:T, 0:15], KEPT - 0.5, None, ALU.is_gt))
                    pick(dve.reduce_sum(digit, hits, axis=AX.X))
                    pick(dve.scalar_tensor_tensor(cur, digit, step, cur, ALU.mult, ALU.add))
                    pick(dve.tensor_scalar(step, step, 1.0 / 16, None, ALU.mult))
                pick.at(4 * ROUND_LINKS + base_links)

            kth_largest(hi, 0)
            t0, t1 = field(730, S), field(760, S)
            dve.tensor_scalar(t0, hi, cur, 65537.0, ALU.is_gt, ALU.mult)
            pick(dve.tensor_scalar(t1, hi, cur, None, ALU.is_equal))
            pick(dve.scalar_tensor_tensor(low, lo, 1.0, t1, ALU.add, ALU.mult))
            pick(dve.tensor_tensor(low, low, t0, ALU.add))
            pick(dve.tensor_scalar(low, low, -1.0, None, ALU.add))
            kth_largest(low, 4)
            greater, equal = field(790, S), field(820, S + 1)
            dve.tensor_scalar(greater, low, cur, None, ALU.is_gt)
            pick(dve.tensor_scalar(equal[:, 0:S], low, cur, None, ALU.is_equal))
            dve.reduce_sum(equal[:, S:S + 1], greater, axis=AX.X).then_inc(counts_ready, 1)
            dve.wait_ge(counts_summed, 9)
            sums = [work[:T, 860 + 64 * k:860 + 64 * k + 64] for k in range(2)]
            for s_ in sums:
                dve.memset(s_[:, 0:32], 0.0)
            pick(dve.tensor_copy(sums[0][:, 32:32 + S + 1], bank[0][:T, 0:S + 1]))
            a, b = sums
            shift = 1
            while shift < S:
                pick(dve.tensor_tensor(b[:, 32:32 + S], a[:, 32:32 + S], a[:, 32 - shift:32 - shift + S], ALU.add))
                a, b = b, a
                shift *= 2
            before, room = field(1000, S), field(1030, 1)
            pick(dve.tensor_tensor(before, bank[1][:T, 0:S], a[:, 31:31 + S], ALU.add))
            pick(dve.tensor_scalar(room, sums[0][:, 32 + S:33 + S], -1.0, float(KEPT), ALU.mult, ALU.add))
            pick(dve.tensor_scalar(before, before, room, None, ALU.is_lt))
            pick(dve.tensor_tensor(before, before, equal[:, 0:S], ALU.mult))
            pick(dve.tensor_tensor(before, before, greater, ALU.add))
            pick(dve.tensor_tensor(w, w, before, ALU.mult))
            with dve.Fori(0, TILES) as i:
                dve.scalar_tensor_tensor(acc[:T, ds(i * KEYS, C)], acc[:T, ds(i * KEYS, C)], w[:, ds(i, 1)],
                                         acc[:T, ds(i * KEYS + ACC, C)], ALU.mult, ALU.add).then_inc(chosen, 1)

        @block.tensor
        def _(pe):
            pe.sem_inc(group_summed, SLOTS)
            pe.wait_ge(wkv_ready, 1)
            pe.wait_ge(pool_consts, 1)
            pe.matmul(bank[4][:, 0:260], vrow[0:1, 0:P], vrow[0:1, 0:260], start=True, stop=False, skip_group_check=True)

            def turn(to, rows_ap, n_rows, **flags):
                return pe.transpose(to, rows_ap, ident[:n_rows, :n_rows])

            def norm_step(t):
                s, r = t.back(1), t.back(2)
                if s.exists():
                    pe.wait_ge(xt_done, s.i + 1)
                    wait_past(pe, kvn_done, s.i - 1)
                    pe.matmul(bank[2 + s.b][:TOK, :], onesf[0:1, 0:TOK], bkv[0:1, :], start=True, stop=False)
                    for h in range(2):
                        last = pe.matmul(bank[2 + s.b][:TOK, :], xt[:, s.b, h, :], wkv[:, h, :], start=False, stop=h == 1)
                    last.then_inc(kv_done, 1)
                if t.exists():
                    pe.wait_ge(xn_done, t.i + 1)
                    wait_past(pe, xt_done, t.i - 1)
                    for h in range(2):
                        last = turn(bank[t.b][:, h * TOK:(h + 1) * TOK], xn[:TOK, t.b, h * P:(h + 1) * P], TOK)
                    last.then_inc(turned, 1)
                if r.exists():
                    pe.wait_ge(kvn_done, r.i + 1)
                    for a in range(2):
                        k, v = kvn[:TOK, r.b, a * P:(a + 1) * P], kvn[:TOK, r.b, C + a * P:C + (a + 1) * P]
                        pe.matmul(bank[4][:, a * P:(a + 1) * P], v, k, start=False, stop=False, skip_group_check=True)
                        pe.matmul(bank[4][:, 256 + a:257 + a], k, onesf[:TOK, 0:1], start=False, stop=False,
                                  skip_group_check=True)
                        last = pe.matmul(bank[4][:, 258 + a:259 + a], v, onesf[:TOK, 0:1], start=False, stop=True,
                                         skip_group_check=True)
                    last.then_inc(kv_summed, 1)

            steps(pe, norm_step, 4, TILES + 2)

            rest = GROUPS - P

            def turn_edges(b, ap):
                for blk, n in ((0, P), (1, rest)):
                    for k in range(2):
                        last = turn(bank[b][:, k * GROUPS + blk * P:k * GROUPS + blk * P + n],
                                    ap[:n, blk, k * P:(k + 1) * P], n)
                return last

            pe.wait_ge(keys_ready, 1)
            turn_edges(5, src_f).then_inc(prep_turned, 1)
            pe.wait_ge(prep_inputs, 1)
            turn_edges(6, key_f).then_inc(prep_turned, 1)
            for k, ap in enumerate((base_g[:, 0:1], base_g[:, 1:2], flag_g[:, 0:1], flag_g[:, 1:2])):
                last = turn(bank[7][0:1, k * P:(k + 1) * P], ap, P)
            last.then_inc(prep_turned, 1)
            pe.wait_ge(src_ready, 1)
            turn_edges(5, left_f).then_inc(prep_turned, 1)

            pe.wait_ge(vec_ready, 1)
            for k in range(4):
                last = turn(bank[0][0:2, k * P:(k + 1) * P], vec[:, 2 * k:2 * k + 2], P)
            last.then_inc(vec_turned, 1)
            pe.wait_ge(wq_ready, 1)
            for a in range(2):
                for h in range(2):
                    last = turn(bank[1][:, a * C + h * P:a * C + (h + 1) * P], wq[:, h, a * P:(a + 1) * P], P)
            last.then_inc(wq_turned, 1)
            pe.wait_ge(vrow_ready, 1)
            for a in range(2):
                last = pe.matmul(bank[3][:, a * P:(a + 1) * P], vrow[0:2, 2 * a * P:(2 * a + 1) * P],
                                 vrow[0:2, (2 * a + 1) * P:(2 * a + 2) * P], start=True, stop=True)
            last.then_inc(outer_done, 1)
            pe.wait_ge(kvt_ready, 1)
            for a in range(2):
                last = pe.matmul(bank[2][:, a * C:(a + 1) * C], kv_t[:, a, :], mw1[:, a, :], start=True, stop=True)
            last.then_inc(b1w_done, 1)
            pe.wait_ge(b1w_ready, 1)
            pe.wait_ge(wqt_ready, 1)
            for o in range(2):
                for a in range(2):
                    pe.matmul(bank[3][:, 400 + o:401 + o], b1w[:, a, o * P:(o + 1) * P], bq[:, a:a + 1], start=a == 0,
                              stop=a == 1)
            for h in range(2):
                for a in range(2):
                    last = pe.matmul(bank[1][:, h * C:(h + 1) * C], wqT[:, a, h * P:(h + 1) * P], b1w[:, a, :],
                                     start=a == 0, stop=a == 1)
            last.then_inc(weff_done, 1)

            def sum_group(b, slots, last_inc):
                rows_k = [rows[:, span(s_, 1), :].rearrange("p o n -> p (o n)") for s_ in slots]
                hot_k = [onehot[:, span(s_, 1), :].rearrange("p o n -> p (o n)") for s_ in slots]
                for h in range(2):
                    for k in range(2):
                        for part in range(2):
                            pe.matmul(bank[b][:, h * WIN:(h + 1) * WIN],
                                      rows_k[k][:, part * C + h * P:part * C + (h + 1) * P], hot_k[k],
                                      start=k == 0 and part == 0, stop=k == 1 and part == 1)
                for k in range(2):
                    last = pe.matmul(bank[b][:, 2 * WIN:3 * WIN], onesh[:, :], hot_k[k], start=k == 0, stop=k == 1)
                last_inc(last)

            pe.wait_ge(any_ready, 1)
            pe.wait_ge(vrow_ready, 1)
            left = pe.value_load(any_left[0:1, 0:1], min_val=0, max_val=1)
            with pe.If(left > 0):
                with pe.Fori(0, GROUPS) as g:
                    pe.sem_inc(pe_at_group, 1)
                    pe.wait_ge(general_turn, g + 1)
                    flagged = pe.value_load(flag_row[0:1, ds(g, 1)], min_val=0, max_val=GROUP)
                    with pe.If(flagged > 0):
                        with pe.Fori(0, GENERAL_WINDOWS) as w:
                            pe.wait_ge(general_in, g * 32 + 32)
                            pe.wait_ge(general_hot, g * GENERAL_WINDOWS + w + 1)
                            pe.wait_ge(general_added, g * GENERAL_WINDOWS + w + 1)
                            sum_group(0, [0, 1], lambda ins: ins.then_inc(general_sum, 1))
                    with pe.Else():
                        pe.sem_inc(general_sum, GENERAL_WINDOWS)

            def agg(g, b, slots):
                pe.wait_ge(gathered, g * 2 + 5)
                pe.wait_ge(hot_done, g * 2 + 2)
                wait_past(pe, acc_added, g - 1)
                sum_group(b, slots, lambda ins: ins.then_inc(group_summed, 2))

            pe.wait_ge(weff_ready, 1)
            pe.wait_ge(mix_w_in, 16)

            def mix_step(t):
                s = t.back(1)
                if t.exists():
                    pe.wait_ge(mix_loaded[t.b], t.u * 32 + 32)
                    wait_past(pe, gelu_done, t.i - 1)
                    for o in range(2):
                        for h in range(2):
                            last = pe.matmul(bank[2 + t.b][:, o * TOK:(o + 1) * TOK], weff[:, h, o * P:(o + 1) * P],
                                             m_xt[:, t.b, h, :], start=h == 0, stop=h == 1)
                    last.then_inc(h_done, 1)
                g = t.i - MIX_FIRST
                if not t.static or 0 <= g < MIX_GROUPS:
                    agg(g, (t.b + MIX_FIRST) % 2, [slot_of(g, 0), slot_of(g, 1)])
                if s.exists():
                    pe.wait_ge(gelu_done, s.i + 1)
                    wait_past(pe, mixed, s.i - 1)
                    pe.matmul(bank[6 + s.b][:TOK, 0:C], onesf[32:33, 0:TOK], biases[32:33, 0:C], start=True, stop=False)
                    for o in range(2):
                        last = pe.matmul(bank[6 + s.b][:TOK, 0:C], m_h[:, s.b, o, :], mw2[:, o, :], start=False,
                                         stop=o == 1)
                    last.then_inc(mix_done, 1)

            steps(pe, mix_step, MIX_FIRST + 2, TILES + 1)

            pe.wait_ge(gelu_done, TILES)
            pe.wait_ge(mixed, TILES)
            pe.wait_ge(gnn_w_ready, 1)
            pe.wait_ge(ffn_w_in, 32)

            u = bank[2][:TOK, 0:C + 1]

            def own_part(t):
                pe.wait_ge(n_xt_in, t.i * 16 + 16)
                wait_past(pe, tanh_done, t.i)
                pe.matmul(u, onesf[0:1, 0:TOK], biases[0:1, :], start=True, stop=False)
                for h in range(2):
                    pe.matmul(u, n_xt[:, h, :], rootw[:, h, :], start=False, stop=False)

            def relations_part(t):
                pe.wait_ge(scaled, t.i + 1)
                for h in range(2):
                    for r in range(RELS):
                        last = pe.matmul(u, sn[:, h, r, :], relw[:, h, r, :], start=False,
                                         stop=h == 1 and r == RELS - 1)
                last.then_inc(u_done, 1)

            def ffn_up(t, half):
                if half == 0:
                    pe.wait_ge(xt3_done, t.i + 1)
                wait_past(pe, gelu2_done, t.i * 2 + half - 1)
                for k in range(4):
                    c = 4 * half + k
                    for h in range(2):
                        last = pe.matmul(bank[4 + half][:, k * TOK:(k + 1) * TOK], w1[:, h, c * P:(c + 1) * P],
                                         xt3[:, h, :], start=h == 0, stop=h == 1)
                last.then_inc(hid_done, 1)

            def ffn_down(t):
                wait_past(pe, y_kept, t.i)
                y = bank[6][:TOK, 0:C]
                pe.matmul(y, onesf[64:65, 0:TOK], biases[64:65, 0:C], start=True, stop=False)
                for c in range(HCHUNKS):
                    if c % 4 == 0:
                        pe.wait_ge(gelu2_done, t.i * 2 + c // 4 + 1)
                    last = pe.matmul(y, hT[:, c, :], w2[:, c, :], start=False, stop=c == HCHUNKS - 1)
                last.then_inc(y_done, 1)

            def node_step(t):
                s, r = t.back(1), t.back(2)

                def agg_at(q):
                    if t.exists():
                        agg(t.i * NODE_GROUPS + (MIX_GROUPS + q), (MIX_GROUPS + t.b * NODE_GROUPS + q) % 2,
                            [(2 * (MIX_GROUPS + q) + k) % SLOTS for k in range(2)])

                agg_at(0)
                if s.exists():
                    own_part(s)
                if r.exists():
                    pe.wait_ge(xn2_done, r.i + 1)
                    wait_past(pe, xt3_done, r.i)
                    for h in range(2):
                        last = turn(bank[3][:, h * TOK:(h + 1) * TOK], xn2[:TOK, h * P:(h + 1) * P], TOK)
                    last.then_inc(turned2, 1)
                if s.exists():
                    pe.wait_ge(count_ready, s.i + 1)
                    turn(bank[7][:TOK, 0:97], count_rows[:, :], 97).then_inc(count_turned, 1)
                agg_at(1)
                if r.exists():
                    ffn_up(r, 0)
                if s.exists():
                    pe.wait_ge(spread_ready, s.i + 1)
                    pe.matmul(bank[7][:, 0:KEYS], onesf[:TOK, :], spread, start=True, stop=True)\
                      .then_inc(inverse_spread, 1)
                agg_at(2)
                if r.exists():
                    ffn_up(r, 1)
                agg_at(3)
                if s.exists():
                    relations_part(s)
                agg_at(4)
                agg_at(5)
                if r.exists():
                    ffn_down(r)
                agg_at(6)

            steps(pe, node_step, 4, TILES + 2)

            with pe.Fori(0, 8) as r:
                pe.wait_ge(counts_ready, r + 1)
                pe.matmul(bank[0][:TOK, 0:15], onesf[:TOK, 0:TOK], work[:TOK, 264:279], start=True, stop=True)\
                  .then_inc(counts_summed, 1)
            pe.wait_ge(counts_ready, 9)
            equal = work[:TOK, 820:820 + TILES + 1]
            pe.matmul(bank[0][:TOK, 0:TILES + 1], onesf[:TOK, 0:TOK], equal, start=True, stop=True)
            pe.matmul(bank[1][:TOK, 0:TILES], tri[:TOK, 0:TOK], equal[:, 0:TILES], start=True, stop=True)\
              .then_inc(counts_summed, 1)


_INS = ["x", "src", "dst", "edge_type_4", "L0_gnn_rel_weight", "L0_gnn_root_weight", "L0_gnn_rgcn_bias",
        "L0_gnn_att_weight", "L0_gnn_att_bias", "L0_mix_w_qkv", "L0_mix_b_qkv", "L0_mix_kln_g", "L0_mix_kln_b",
        "L0_mix_vln_g", "L0_mix_vln_b", "L0_mix_w1", "L0_mix_b1", "L0_mix_w2", "L0_mix_b2", "L0_ffn_wr", "L0_ffn_br",
        "L0_ffn_w1", "L0_ffn_b1", "L0_ffn_w2", "L0_ffn_b2"]


def kernel(**inputs):
    import numpy as np
    import concourse.bacc as bacc
    from concourse.bass_utils import run_bass_kernel_spmd

    nc = bacc.Bacc("TRN2", target_bir_lowering=False, num_devices=1)
    arrays, args = {}, []
    for name in _INS:
        a = np.ascontiguousarray(inputs[name])
        arrays[f"in_{name}"] = a
        args.append(nc.dram_tensor(f"in_{name}", a.shape, mybir.dt.from_np(a.dtype), kind="ExternalInput").ap())
    args.append(nc.dram_tensor("out", (N, C), mybir.dt.float32, kind="ExternalOutput").ap())
    gps_block(nc, *args)
    result = run_bass_kernel_spmd(nc, [arrays], core_ids=[0])
    return result.results[0]["out"]
```

```python
import concourse.bass as bass
from concourse import mybir
from contextlib import ExitStack

N = 3125
C = 256
EDGES = 50000
RELS = 4
HEADS, HEADC = 8, 32
HIDDEN = 1024
P = 128
TOK = 125
TILES = N // TOK
KEYS = TOK * RELS
WIN = 128
GROUP = 256
GROUPS = -(-EDGES // GROUP)
GATHERS = 2 * GROUPS
SLOTS = 7
NODE_GROUPS = 7
MIX_GROUPS = GROUPS - TILES * NODE_GROUPS
MIX_FIRST = TILES - MIX_GROUPS
ACC = (N - 1) * RELS + WIN
GENERAL_WINDOWS = -(-N * RELS // WIN)
KEPT = 1561
EPS = 1e-5
PAD_NODE = 1000000
HCHUNKS = HIDDEN // P
PARTS = 65
STORED = 3 * 16


class Tile:

    def __init__(self, half, offset):
        self.half, self.offset = half, offset
        self.static = half is None
        self.i = offset if self.static else half * 2 + offset
        self.b = offset % 2
        self.u = offset // 2 if self.static else half + offset // 2

    def back(self, n):
        return Tile(self.half, self.offset - n)

    def exists(self):
        return not self.static or 0 <= self.offset < TILES


def steps(eng, step, first, last, ahead=0):
    stop = first + (TILES - ahead - first) // 2 * 2
    for i in range(first):
        step(Tile(None, i))
    with eng.Fori(0, (stop - first) // 2) as half:
        for k in range(2):
            step(Tile(half, first + k))
    for i in range(stop, last):
        step(Tile(None, i))


def wait_past(eng, sem, count):
    if not isinstance(count, int) or count > 0:
        eng.wait_ge(sem, count)


class Links:

    def __init__(self, eng, sem):
        self.eng, self.sem, self.start, self.n = eng, sem, 0, 0

    def at(self, start):
        self.start, self.n = start, 0

    def __call__(self, ins):
        self.n += 1
        ins.then_inc(self.sem, 1)
        self.eng.wait_ge(self.sem, self.start + self.n)


def gps_block(nc, x, src, dst, etype, rel_w, root_w, gnn_b, att_w, att_b, w_qkv, b_qkv, kln_g, kln_b,
              vln_g, vln_b, mix_w1, mix_b1, mix_w2, mix_b2, wr, br, ffn_w1, ffn_b1, ffn_w2, ffn_b2, out):
    f32, f16, bf16, i32, u16 = (mybir.dt.float32, mybir.dt.float16, mybir.dt.bfloat16, mybir.dt.int32,
                                mybir.dt.uint16)
    ALU, ACT, AX = mybir.AluOpType, mybir.ActivationFunctionType, mybir.AxisListType
    ds = bass.ds

    table = nc.dram_tensor("table", (N, 2 * C), f16).ap()
    xn_d = nc.dram_tensor("xn_d", (N, C), f32).ap()
    base_d = nc.dram_tensor("base_d", (N, C), f32).ap()
    xt_d = nc.dram_tensor("xt_d", (TILES, P, 2 * TOK), f32).ap()

    with ExitStack() as ctx:
        def sb(name, shape, dt):
            return ctx.enter_context(nc.sbuf_tensor(name, shape, dt))

        acc = sb("acc", [P, 2 * ACC], f32)
        acc3 = acc[:, :].rearrange("p (h k) -> p h k", h=2)
        cnt = sb("cnt", [P, ACC], u16)
        relw = sb("relw", [P, 2, RELS, C + 1], f32)
        rootw = sb("rootw", [P, 2, C + 1], f32)
        fw = sb("fw", [P, 4096], f32)
        w1 = fw[:, 0:2048].rearrange("p (a n) -> p a n", a=2)
        w2 = fw[:, 2048:4096].rearrange("p (a n) -> p a n", a=HCHUNKS)
        rows = sb("rows", [P, SLOTS, 2 * C], f16)
        onehot = sb("onehot", [P, SLOTS, WIN], f16)
        key_t = sb("key_t", [P, 2, GROUPS], f32)
        src_t = sb("src_t", [P, GATHERS], i32)
        index = sb("index", [P, 2, SLOTS], i32)
        ident = sb("ident", [P, P], f32)
        onesf = sb("onesf", [P, P], f32)
        onesh = sb("onesh", [P, P], f16)
        keyrow = sb("keyrow", [P, WIN], f16)
        base_row = sb("base_row", [1, 2 * P], i32)
        flag_row = sb("flag_row", [1, 2 * P], i32)
        any_left = sb("any_left", [1, 1], i32)
        biases = sb("biases", [PARTS, 3, C + 1], f32)
        bias_parts = sb("bias_parts", [PARTS, 3, C + 1], bf16)
        kv_parts = sb("kv_parts", [PARTS, 2 * C], bf16)
        onesb = sb("onesb", [PARTS, P], bf16)
        fb1 = sb("fb1", [P, HCHUNKS], f32)
        wr_rep = sb("wr_rep", [P, C], f32)
        br_rep = sb("br_rep", [P, 1], f32)
        w_all = sb("w_all", [P, TILES], f32)
        small = sb("small", [P, 64], f32)
        stats = sb("stats", [P, 2, 64], f32)
        ctmp = sb("ctmp", [P, 2304], f32)
        work = sb("work", [P, 5000], f32)

        tri = sb("tri", [P, P], f32)

        eps_col, zero_col = small[:, 40:41], small[:, 41:42]
        att2, attb, mb1, bq = small[:, 20:22], small[0:PARTS, 22:23], small[:, 24:26], small[:, 26:28]
        kg, kb, vg, vb = (small[:, 28 + k:29 + k] for k in range(4))

        mw1, wqT, b1w, wq = (ctmp[:, 512 * k:512 * k + 512].rearrange("p (a n) -> p a n", a=2) for k in range(4))
        a_rep = ctmp[:, 2048:2304]

        TEMP = 8500
        used = [2 * ACC - TEMP]

        def temp(n):
            used[0] += n
            assert used[0] <= 2 * ACC
            return acc[:, used[0] - n:used[0]]

        x_in = temp(512).rearrange("p (b n) -> p b n", b=2)
        xn = temp(512).rearrange("p (b n) -> p b n", b=2)
        tab = temp(512).bitcast(f16).rearrange("p (b n) -> p b n", b=2)
        kv_total = temp(512)
        xt = temp(500).rearrange("p (b h n) -> p b h n", b=2, h=2)
        sq = temp(1024).rearrange("p (b n) -> p b n", b=2)
        kvn = temp(1024).rearrange("p (b n) -> p b n", b=2)
        wkv = temp(1024).rearrange("p (a n) -> p a n", a=2)
        wqkv = temp(1536).rearrange("p (a n) -> p a n", a=2)
        bkv = temp(512)
        bqkv = temp(768)
        means = temp(48)

        ep = [fw[:, 512 * k:512 * k + 512] for k in range(8)]
        src_g, dst_g, typ_g = [e.bitcast(i32).rearrange("p (b n) -> p b n", b=2) for e in ep[0:3]]
        src_f, dst_f, typ_f, key_f, left_f = [e.rearrange("p (b n) -> p b n", b=2) for e in ep[3:8]]
        tmp_g = work[:, 0:512].rearrange("p (b n) -> p b n", b=2)
        out_g = work[:, 512:1024].rearrange("p (b n) -> p b n", b=2)
        thr = work[:, 1024:1048]
        gcol = work[:, 1048:1050]
        thr_i = work[:, 1050:1074].bitcast(i32)
        gcol_i = work[:, 1074:1076].bitcast(i32)
        cmp_g = work[:, 1076:1124].rearrange("p (b n) -> p b n", b=2)
        base_g = work[:, 1124:1126]
        flag_g = work[:, 1126:1128]
        min_g = work[:, 1128:1130]
        done_g = work[:, 1130:1132]
        iota_i = work[:, 1132:1260].bitcast(i32)
        left_t = work[:, 1300:1300 + 2 * GROUPS].rearrange("p (s g) -> p s g", s=2)
        left_rel = work[:, 1960:1962]
        any_f = work[0:1, 1970:1971]
        gate_junk = work[:, 1700:1956]

        part_hi = work[0:PARTS, 2500:2886].bitcast(bf16)
        part_lo = work[0:PARTS, 2886:3272].bitcast(bf16)
        part_rest = work[0:PARTS, 3272:4044]

        m_xt = work[:, 2000:2500].rearrange("p (b h n) -> p b h n", b=2, h=2)
        m_x = work[:, 2500:3012].rearrange("p (b n) -> p b n", b=2)
        m_xn = sb("m_xn", [P, 2, C], f32)
        m_h = work[:, 3012:3512].rearrange("p (b h n) -> p b h n", b=2, h=2)
        m_out = work[:, 3520:4032].rearrange("p (b n) -> p b n", b=2)
        weff = work[:, 0:512].rearrange("p (a n) -> p a n", a=2)
        mw2 = work[:, 512:1024].rearrange("p (a n) -> p a n", a=2)
        kv_t = work[:, 4032:4288].rearrange("p (a n) -> p a n", a=2)
        vec = work[:, 4288:4296]
        vrow = work[:, 4300:4812]
        beff = work[:, 4850:4852]
        grow = work[:, 4860:4892]

        sn = work[:, 0:1000].rearrange("p (h r n) -> p h r n", h=2, r=RELS)
        spread = work[:TOK, 1000:1500]
        inverse = work[:TOK, 4562:4566]
        hT = work[:, 1500:2500].rearrange("p (c n) -> p c n", c=HCHUNKS)
        n_xt = work[:, 2500:2750].rearrange("p (h n) -> p h n", h=2)
        n_xn = work[:, 2750:3006]
        n_base = work[:, 3006:3262]
        th = work[:, 3262:3518]
        x1 = work[:, 3518:3774]
        xn2 = work[:, 3774:4030]
        xt3 = work[:, 4030:4280].rearrange("p (h n) -> p h n", h=2)
        junk = work[:, 4280:4536]
        ta = work[:, 4540:4541]
        ga = work[:, 4541:4542]
        st2 = work[:, 4544:4550]
        mv2 = work[:, 4550:4552]
        nw = work[:, 4552:4560]
        wcol = work[:, 4560:4561]
        count_rows = sb("count_rows", [32 * (RELS - 1) + 1, TOK], f32)

        bank = [ctx.enter_context(nc.psum_tensor(f"bank{k}", [P, 512], f32)) for k in range(8)]

        def sem(name):
            return ctx.enter_context(nc.semaphore(name))

        def sems(names):
            return [sem(n) for n in names.split()]

        edges_cleared, edges_in, weights_in, small_in, mix_w_in, ffn_w_in = sems(
            "edges_cleared edges_in weights_in small_in mix_w_in ffn_w_in")
        pool_link, dve_link, act_link, pool_consts, keys_ready, acc_cleared, cnt_cleared = sems(
            "pool_link dve_link act_link pool_consts keys_ready acc_cleared cnt_cleared")
        bases_ready, flags_ready = sems("bases_ready flags_ready")
        prep_inputs, prep_turned, src_ready, rows_ready, keys_in_place, any_ready, tail_cleared = sems(
            "prep_inputs prep_turned src_ready rows_ready keys_in_place any_ready tail_cleared")
        x_loaded = sems("x_loaded0 x_loaded1")
        stored = sems("stored0 stored1")
        eps_ready = sem("eps_ready")
        wkv_ready, stats_link, stats_order, stats_done, std_done, rstd_link, rstd_done = sems(
            "wkv_ready stats_link stats_order stats_done std_done rstd_link rstd_done")
        xn_done, hi_done, lo_done, turned, xt_done = sems(
            "xn_done hi_done lo_done turned xt_done")
        kv_done, squared, var_done, kstd_done, kstd_link, kvn_done, kv_added, kv_summed = sems(
            "kv_done squared var_done kstd_done kstd_link kvn_done kv_added kv_summed")
        wq_ready, vec_ready, vec_turned, vrow_ready, outer_done, kvt_ready, wq_turned, wqt_ready = sems(
            "wq_ready vec_ready vec_turned vrow_ready outer_done kvt_ready wq_turned wqt_ready")
        b1w_done, b1w_ready, weff_done, weff_ready, gnn_w_ready = sems(
            "b1w_done b1w_ready weff_done weff_ready gnn_w_ready")
        general_index, general_in, general_link, general_hot, general_sum, general_added = sems(
            "general_index general_in general_link general_hot general_sum general_added")
        pool_at_group, pe_at_group, general_turn = sems("pool_at_group pe_at_group general_turn")
        slot_in = [sem(f"slot_in{k}") for k in range(SLOTS)]
        index_ready, gathered, hot_done, group_summed, acc_added = sems(
            "index_ready gathered hot_done group_summed acc_added")
        mix_xt_in, mix_rows_in = sems("mix_xt_in0 mix_xt_in1"), sems("mix_rows_in0 mix_rows_in1")
        mix_stored = sems("mix_stored0 mix_stored1")
        h_done, gelu_done, base_done, mix_done, mixed = sems("h_done gelu_done base_done mix_done mixed")
        n_xt_in, n_rows_in, final_stored = sems("n_xt_in n_rows_in final_stored")
        count_ready, count_turned, inverse_ready, spread_ready, inverse_spread = sems(
            "count_ready count_turned inverse_ready spread_ready inverse_spread")
        scaled, u_done, tanh_done, node_link, x1_done, rstd2_done = sems(
            "scaled u_done tanh_done node_link x1_done rstd2_done")
        route_link, xn2_done, base2_done, turned2, xt3_done, hid_done, gelu2_done, y_done, y_kept = sems(
            "route_link xn2_done base2_done turned2 xt3_done hid_done gelu2_done y_done y_kept")
        select_link, counts_ready, counts_summed, chosen = sems("select_link counts_ready counts_summed chosen")

        block = ctx.enter_context(nc.Block())

        def rows_of(t, ap):
            return ap[ds(t.i * TOK, TOK), :] if not t.static else ap[t.i * TOK:(t.i + 1) * TOK, :]

        def span(start, n):
            return slice(start, start + n) if isinstance(start, int) else ds(start, n)

        def slot_of(g, k):
            return (g * 2 + k) % SLOTS

        def tile_of(t, ap):
            return ap[span(t.i, 1), :, :].rearrange("a p n -> p (a n)")

        @block.sync
        def _(sp):
            def norm_step(t):
                if t.static and t.offset < 1:
                    sp.dma_start(x_in[:TOK, t.b, :], rows_of(t, x)).then_inc(x_loaded[t.b], 16)
                if t.static and t.offset == 0:
                    first_loads()
                s = t.back(1)
                if s.exists():
                    sp.wait_ge(lo_done, s.i + 1)
                    sp.dma_start(rows_of(s, table), tab[:TOK, s.b, :]).then_inc(stored[s.b], 16)
                    sp.dma_start(rows_of(s, xn_d), xn[:TOK, s.b, :]).then_inc(stored[s.b], 16)
                    sp.wait_ge(xt_done, s.i + 1)
                    sp.dma_start(tile_of(s, xt_d), xt[:, s.b, :, :].rearrange("p h n -> p (h n)"))\
                      .then_inc(stored[s.b], 16)

            def first_loads():
                second = Tile(None, 1)
                sp.dma_start(x_in[:TOK, 1, :], rows_of(second, x)).then_inc(x_loaded[1], 16)
                sp.dma_start(wqkv, w_qkv.rearrange("(a p) n -> p a n", p=P)).then_inc(weights_in, 16)
                sp.dma_start(bqkv[0:PARTS, :], b_qkv.rearrange("(a n) -> a n", a=1).broadcast_to([PARTS, 3 * C]))\
                  .then_inc(weights_in, 16)
                sp.wait_ge(edges_cleared, 1)
                tail = EDGES - (GROUPS - 1) * GROUP
                full = GROUPS - 1 - P
                for ap, d in ((src_g, src), (dst_g, dst), (typ_g, etype)):
                    sp.dma_start(ap[:, 0, :], d[0:P * GROUP].rearrange("(p n) -> p n", n=GROUP)).then_inc(edges_in, 16)
                    sp.dma_start(ap[0:full, 1, :], d[P * GROUP:(GROUPS - 1) * GROUP].rearrange("(p n) -> p n", n=GROUP))\
                      .then_inc(edges_in, 16)
                    sp.dma_start(ap[full:full + 1, 1, 0:tail], d[EDGES - tail:EDGES].rearrange("(p n) -> p n", p=1))\
                      .then_inc(edges_in, 16)

            steps(sp, norm_step, 4, TILES + 1)

            sp.wait_ge(stored[0], STORED * 13)
            sp.wait_ge(stored[1], STORED * 12)
            sp.dma_start(mw2, mix_w2.rearrange("(a p) n -> p a n", p=P)).then_inc(mix_w_in, 16)
            sp.wait_ge(prep_turned, 4)
            sp.dma_start(w1, ffn_w1.rearrange("(a p) n -> p a n", p=P)).then_inc(ffn_w_in, 16)
            sp.dma_start(w2, ffn_w2.rearrange("(c p) n -> p c n", p=P)).then_inc(ffn_w_in, 16)

            def mix_step(t):
                if t.exists():
                    wait_past(sp, h_done, t.i - 1)
                    sp.dma_start(m_xt[:, t.b, :, :].rearrange("p h n -> p (h n)"), tile_of(t, xt_d))\
                      .then_inc(mix_xt_in[t.b], 16)
                r, s = t.back(1), t.back(2)
                if r.exists():
                    wait_past(sp, mixed, r.i - 1)
                    sp.dma_start(m_x[:TOK, r.b, :], rows_of(r, x)).then_inc(mix_rows_in[r.b], 16)
                    sp.dma_start(m_xn[:TOK, r.b, :], rows_of(r, xn_d)).then_inc(mix_rows_in[r.b], 16)
                if s.exists():
                    sp.wait_ge(mixed, s.i + 1)
                    sp.dma_start(rows_of(s, base_d), m_out[:TOK, s.b, :]).then_inc(mix_stored[s.b], 16)

            steps(sp, mix_step, MIX_FIRST + 2, TILES + 2)
            sp.wait_ge(mix_stored[0], 16 * 13)
            sp.wait_ge(mix_stored[1], 16 * 12)

            def node_step(t):
                if t.exists():
                    if t.static and t.offset == 0:
                        sp.wait_ge(h_done, TILES)
                        sp.wait_ge(mixed, TILES)
                    wait_past(sp, u_done, t.i)
                    sp.dma_start(n_xt.rearrange("p h n -> p (h n)"), tile_of(t, xt_d)).then_inc(n_xt_in, 16)
                    wait_past(sp, x1_done, t.i)
                    sp.dma_start(n_xn[:TOK, :], rows_of(t, xn_d)).then_inc(n_rows_in, 16)
                    sp.dma_start(n_base[:TOK, :], rows_of(t, base_d)).then_inc(n_rows_in, 16)

            steps(sp, node_step, 4, TILES)

            with sp.Fori(0, 5) as c:
                sp.wait_ge(chosen, c * 5 + 5)
                sp.dma_start(out[ds(c * (5 * TOK), 5 * TOK), :].rearrange("(t p) n -> p t n", p=TOK),
                             acc[:TOK, ds(c * (5 * KEYS), 5 * KEYS)].rearrange("p (t k) -> p t k", k=KEYS)[:, :, 0:C])\
                  .then_inc(final_stored, 16)
            sp.wait_ge(final_stored, 16 * 5)

        @block.gpsimd
        def _(pool):
            link = Links(pool, pool_link)
            pool.memset(src_g, 0)
            pool.memset(typ_g, 0)
            link(pool.memset(dst_g, PAD_NODE))
            pool.sem_inc(edges_cleared, 1)
            link(pool.memset(ident[:, :], 0.0))
            link(pool.affine_select(out=ident[:, :], in_=ident[:, :], compare_op=ALU.not_equal, fill=1.0, base=0,
                                    pattern=[[-1, P]], channel_multiplier=1))
            pool.memset(onesf[:, :], 1.0)
            pool.memset(onesb[:, :], 1.0)
            link(pool.memset(onesh[:, :], 1.0))
            link(pool.affine_select(out=tri[:, :], in_=onesf[:, :], compare_op=ALU.is_gt, fill=0.0, base=0,
                                    pattern=[[1, P]], channel_multiplier=-1))
            link(pool.iota(iota_i, pattern=[[1, WIN]], base=0, channel_multiplier=0))
            link(pool.tensor_copy(keyrow[:, :], iota_i))
            pool.sem_inc(pool_consts, 1)
            pool.iota(thr_i, pattern=[[NODE_GROUPS, TILES - 1]], base=MIX_GROUPS + NODE_GROUPS, channel_multiplier=0)
            link(pool.iota(gcol_i, pattern=[[P, 2]], base=0, channel_multiplier=1))
            pool.tensor_copy(thr, thr_i)
            link(pool.tensor_copy(gcol, gcol_i))
            for blk in range(2):
                last = pool.tensor_scalar(cmp_g[:, blk, :], thr, gcol[:, blk:blk + 1], None, ALU.is_le)
            link(last)
            pool.wait_ge(edges_in, 16 * 9)
            pool.tensor_copy(src_f, src_g)
            pool.tensor_copy(typ_f, typ_g)
            link(pool.tensor_copy(dst_f, dst_g))
            pool.sem_inc(keys_ready, 1)
            wide = [P, 2, GROUP]
            pool.wait_ge(bases_ready, 1)
            bases = base_g.rearrange("p (b o) -> p b o", o=1).broadcast_to(wide)
            link(pool.tensor_tensor(key_f, dst_f, bases, ALU.subtract))
            link(pool.tensor_scalar(key_f, key_f, float(RELS), None, ALU.mult))
            link(pool.tensor_tensor(key_f, key_f, typ_f, ALU.add))
            pool.tensor_scalar(tmp_g, key_f, -0.5, None, ALU.is_lt)
            pool.tensor_scalar(out_g, key_f, WIN - 0.5, None, ALU.is_gt)
            link(pool.tensor_scalar(left_f, dst_f, float(RELS), None, ALU.mult))
            link(pool.tensor_tensor(tmp_g, tmp_g, out_g, ALU.add))
            link(pool.tensor_tensor(left_f, left_f, typ_f, ALU.add))
            link(pool.tensor_scalar(left_f, left_f, 1e6, None, ALU.add))
            link(pool.tensor_tensor(left_f, left_f, tmp_g, ALU.mult))
            link(pool.tensor_scalar(left_f, left_f, -1e6, None, ALU.add))
            pool.tensor_scalar(tmp_g, left_f, -0.5, None, ALU.is_gt)
            link(pool.tensor_scalar(out_g, left_f, N * RELS - 0.5, None, ALU.is_lt))
            link(pool.tensor_tensor(tmp_g, tmp_g, out_g, ALU.mult))
            pool.sem_inc(prep_inputs, 1)
            for to, ap in ((mw1, mix_w1.rearrange("(a p) n -> p a n", p=P)),
                           (rootw[:, :, 0:C], root_w.rearrange("(a p) n -> p a n", p=P)),
                           (relw[:, 0, :, 0:C], rel_w[:, 0:P, :].rearrange("r p n -> p r n")),
                           (relw[:, 1, :, 0:C], rel_w[:, P:C, :].rearrange("r p n -> p r n")),
                           (a_rep, att_w[0:1, 0:C].broadcast_to([P, C])),
                           (att2, att_w[0:1, C:2 * C].rearrange("o (a p) -> p (o a)", p=P)),
                           (biases[:, 0, 0:C], gnn_b.rearrange("(a n) -> a n", a=1).broadcast_to([PARTS, C])),
                           (biases[:, 1, 0:C], mix_b2.rearrange("(a n) -> a n", a=1).broadcast_to([PARTS, C])),
                           (biases[:, 2, 0:C], ffn_b2.rearrange("(a n) -> a n", a=1).broadcast_to([PARTS, C])),
                           (attb, att_b.rearrange("(a n) -> a n", a=1).broadcast_to([PARTS, 1])),
                           (wr_rep[:, :], wr.rearrange("c o -> o c").broadcast_to([P, C])),
                           (br_rep[:, :], br.rearrange("(a n) -> a n", a=1).broadcast_to([P, 1])),
                           (fb1[:, :], ffn_b1.rearrange("(c p) -> p c", p=P)),
                           (mb1, mix_b1.rearrange("(c p) -> p c", p=P)),
                           (grow, kln_g.rearrange("(a n) -> a n", a=1).broadcast_to([P, HEADC]))):
                pool.dma_start(to, ap, allow_slow_non_contiguous=True).then_inc(small_in, 16)
            for to, g in ((kg, kln_g), (kb, kln_b), (vg, vln_g), (vb, vln_b)):
                for h in range(4):
                    pool.dma_start(to[h * HEADC:(h + 1) * HEADC, :], g.rearrange("(n a) -> n a", a=1))\
                      .then_inc(small_in, 16)
            for h in range(HEADS):
                pool.dma_start(bq[(h % 4) * HEADC:(h % 4 + 1) * HEADC, h // 4:h // 4 + 1],
                             b_qkv[h * 3 * HEADC:h * 3 * HEADC + HEADC].rearrange("(n a) -> n a", a=1))\
                  .then_inc(small_in, 16)

            pool.memset(cnt[:, :], 0).then_inc(cnt_cleared, 1)
            pool.memset(acc[:, 0:2 * ACC - TEMP], 0.0).then_inc(acc_cleared, 1)

            pool.wait_ge(stored[0], STORED * 13)
            pool.wait_ge(stored[1], STORED * 12)
            pool.wait_ge(src_ready, 1)
            pool.wait_ge(any_ready, 1)

            def gather(into, idx):
                return pool.indirect_dma_start(into, None, table, bass.IndirectOffsetOnAxis(ap=idx, axis=0))

            left = pool.value_load(any_left[0:1, 0:1], min_val=0, max_val=1)
            with pool.If(left > 0):
                with pool.Fori(0, GROUPS) as g:
                    pool.sem_inc(pool_at_group, 1)
                    pool.wait_ge(general_turn, g + 1)
                    pool.tensor_copy(index[:, 0, 0:2], src_t[:, ds(g * 2, 2)]).then_inc(general_index, 1)
                    pool.wait_ge(general_index, g * 2 + 1)
                    pool.sem_inc(general_index, 1)
                    for k in range(2):
                        gather(rows[:, k, :], index[:, 0, k:k + 1]).then_inc(general_in, 16)
                    pool.wait_ge(general_in, g * 32 + 32)
                pool.wait_ge(general_added, GROUPS * GENERAL_WINDOWS + 1)

            def gather_round(a):
                for half in range(2):
                    pool.tensor_copy(index[:, half, :], src_t[:, span(a * (2 * SLOTS) + half * SLOTS, SLOTS)])\
                        .then_inc(index_ready, 1)
                    pool.wait_ge(index_ready, a * 2 + (half + 1))
                    for k in range(SLOTS):
                        pool.wait_ge(group_summed, a * (2 * SLOTS) + (half * SLOTS + k + 1))
                        wait_past(pool, slot_in[(k - 3) % SLOTS], a * 32 + 16 * (half + (k >= 3)))
                        pool.sem_inc(gathered, 1)
                        gather(rows[:, k, :], index[:, half, k:k + 1]).then_inc(slot_in[k], 16)

            gather_round(0)
            with pool.Fori(1, GATHERS // (2 * SLOTS)) as a:
                gather_round(a)
            for k in range(SLOTS - 3, SLOTS):
                pool.wait_ge(slot_in[k], GATHERS // SLOTS * 16)
                pool.sem_inc(gathered, 1)

        @block.scalar
        def _(act):
            link = Links(act, act_link)

            act.wait_ge(weights_in, 32)
            for a in range(2):
                last = act.activation(wq[:, a, :].rearrange("p (h j) -> p h j", h=HEADS),
                                      wqkv[:, a, :].rearrange("p (h t j) -> p h t j", h=HEADS, t=3)[:, :, 0, :], ACT.Copy)
            last.then_inc(wq_ready, 1)

            def norm_step(t):
                s = t.back(1)
                if t.exists():
                    act.wait_ge(rstd_done, t.i + 1)
                    wait_past(act, stored[t.b], t.u * STORED)
                    wait_past(act, turned, t.i - 1)
                    act.activation(xn[:TOK, t.b, :], x_in[:TOK, t.b, :], ACT.Identity, bias=stats[:TOK, t.b, 10:11],
                                   scale=stats[:TOK, t.b, 9:10]).then_inc(xn_done, 1)
                    act.wait_ge(xn_done, t.i + 1)
                    act.activation(tab[:TOK, t.b, 0:C], xn[:TOK, t.b, :], ACT.Copy).then_inc(hi_done, 1)
                    after_next = t.back(-2)
                    if not t.static or after_next.exists():
                        act.dma_start(x_in[:TOK, t.b, :], rows_of(after_next, x)).then_inc(x_loaded[t.b], 16)
                if s.exists():
                    act.wait_ge(kv_done, s.i + 1)
                    wait_past(act, var_done, s.i - 1)
                    act.activation(sq[:TOK, s.b, :], bank[2 + s.b][:TOK, :], ACT.Square).then_inc(squared, 1)
                if t.exists():
                    act.wait_ge(turned, t.i + 1)
                    wait_past(act, kv_done, t.i - 1)
                    act.activation(xt[:, t.b, :, :], bank[t.b][:, 0:2 * TOK].rearrange("p (h n) -> p h n", h=2),
                                   ACT.Copy).then_inc(xt_done, 1)
                    n = t.back(-1)
                    if not t.static or n.exists():
                        deviation(n)
                if s.exists():
                    act.wait_ge(var_done, s.i + 1)
                    act.activation(stats[:TOK, s.b, 32:48], stats[:TOK, s.b, 16:32], ACT.Sqrt, bias=eps_col[:TOK, :],
                                   scale=1.0 / HEADC).then_inc(kstd_done, 1)

            def deviation(t):
                act.wait_ge(stats_done, t.i + 1)
                wait_past(act, rstd_done, t.i - 1)
                act.activation(stats[:TOK, t.b, 8:9], stats[:TOK, t.b, 7:8], ACT.Sqrt, bias=eps_col[:TOK, :])\
                   .then_inc(std_done, 1)

            act.wait_ge(eps_ready, 1)
            deviation(Tile(None, 0))
            steps(act, norm_step, 4, TILES + 1, ahead=2)

            act.wait_ge(prep_turned, 1)
            act.activation(src_t[:, :].rearrange("p (g s) -> p s g", s=2),
                           bank[5][:, 0:2 * GROUPS].rearrange("p (s g) -> p s g", s=2), ACT.Copy)\
               .then_inc(src_ready, 1)
            act.wait_ge(prep_turned, 3)
            act.activation(base_row[:, :], bank[7][0:1, 0:2 * P], ACT.Copy, scale=float(RELS))
            act.activation(flag_row[:, :], bank[7][0:1, 2 * P:4 * P], ACT.Copy).then_inc(rows_ready, 1)

            act.wait_ge(vec_turned, 1)
            act.activation(vrow[0:2, :], bank[0][0:2, :], ACT.Copy).then_inc(vrow_ready, 1)
            act.wait_ge(wq_turned, 1)
            act.activation(wqT.rearrange("p a n -> p (a n)"), bank[1][:, :], ACT.Copy).then_inc(wqt_ready, 1)
            act.wait_ge(b1w_done, 1)
            act.activation(b1w.rearrange("p a n -> p (a n)"), bank[2][:, :], ACT.Copy, scale=1.0 / N)\
               .then_inc(b1w_ready, 1)

            act.wait_ge(kv_summed, TILES + 1)
            act.wait_ge(stored[0], STORED * 13)
            act.wait_ge(stored[1], STORED * 12)
            act.wait_ge(prep_turned, 1)
            act.activation(acc[:, 2 * ACC - TEMP:2 * ACC], zero_col.broadcast_to([P, TEMP]), ACT.Copy)\
               .then_inc(tail_cleared, 1)

            act.wait_ge(weff_ready, 1)

            def mix_step(t):
                if t.exists():
                    act.wait_ge(h_done, t.i + 1)
                    wait_past(act, mix_done, t.i - 1)
                    for o in range(2):
                        last = act.activation(m_h[:, t.b, o, :], bank[2 + t.b][:, o * TOK:(o + 1) * TOK], ACT.Gelu,
                                              bias=beff[:, o:o + 1])
                    last.then_inc(gelu_done, 1)

            steps(act, mix_step, MIX_FIRST + 2, TILES)

            def node_step(t):
                s, r = t.back(1), t.back(2)
                if r.exists():
                    act.wait_ge(turned2, r.i + 1)
                    wait_past(act, hid_done, r.i * 2)
                    act.activation(xt3, bank[3][:, 0:2 * TOK].rearrange("p (h n) -> p h n", h=2), ACT.Copy)\
                       .then_inc(xt3_done, 1)
                if r.exists():
                    for half in range(2):
                        act.wait_ge(hid_done, r.i * 2 + half + 1)
                        wait_past(act, y_done, r.i)
                        for c in range(4 * half, 4 * half + 4):
                            k = c - 4 * half
                            last = act.activation(hT[:, c, :], bank[4 + half][:, k * TOK:(k + 1) * TOK],
                                                  ACT.Gelu_apprx_tanh, bias=fb1[:, c:c + 1])
                        last.then_inc(gelu2_done, 1)
                if s.exists():
                    act.wait_ge(u_done, s.i + 1)
                    wait_past(act, x1_done, s.i)
                    act.activation(th[:TOK, :], bank[2][:TOK, 0:C], ACT.Tanh)
                    act.activation(ta[:TOK, :], bank[2][:TOK, C:C + 1], ACT.Tanh, scale=0.5).then_inc(tanh_done, 1)
                if r.exists():
                    act.wait_ge(y_done, r.i + 1)
                    act.activation(acc[:TOK, span(r.i * KEYS, C)], bank[6][:TOK, 0:C], ACT.Copy).then_inc(y_kept, 1)
                if t.exists():
                    act.wait_ge(inverse_ready, t.i + 1)
                    wait_past(act, inverse_spread, t.i)
                    for k in range(RELS):
                        last = act.activation(spread[:, k * TOK:(k + 1) * TOK], ident[:TOK, 0:TOK], ACT.Copy,
                                              scale=inverse[:, k:k + 1])
                    last.then_inc(spread_ready, 1)
                if s.exists():
                    act.wait_ge(rstd2_done, s.i + 1)
                    wait_past(act, turned2, s.i)
                    wait_past(act, base2_done, s.i)
                    act.activation(xn2[:TOK, :], x1[:TOK, :], ACT.Identity, bias=nw[:TOK, 7:8], scale=nw[:TOK, 6:7])\
                       .then_inc(xn2_done, 1)

            steps(act, node_step, 4, TILES + 2)

        @block.vector
        def _(dve):
            link = Links(dve, dve_link)
            dve.memset(eps_col, EPS).then_inc(eps_ready, 1)
            dve.memset(zero_col, 0.0)
            dve.memset(kv_total[:TOK, :], 0.0).then_inc(kv_added, 1)
            link(dve.memset(vrow[0:1, :], 0.0))
            dve.wait_ge(weights_in, 32)
            kv_view = wqkv.rearrange("p a (h t j) -> p a h t j", h=HEADS, t=3)
            for a in range(2):
                for t in range(2):
                    dve.reduce_sum(means[:, 16 * a + 8 * t:16 * a + 8 * t + 8], kv_view[:, a, :, 1 + t, :], axis=AX.X)
            for t in range(2):
                last = dve.reduce_sum(means[0:PARTS, 32 + 8 * t:40 + 8 * t],
                                      bqkv[0:PARTS, :].rearrange("p (h t j) -> p h t j", h=HEADS, t=3)[:, :, 1 + t, :],
                                      axis=AX.X)
            link(last)
            link(dve.tensor_scalar(means[:, 0:32], means[:, 0:32], 1.0 / HEADC, None, ALU.mult))
            link(dve.tensor_scalar(means[0:PARTS, 32:48], means[0:PARTS, 32:48], 1.0 / HEADC, None, ALU.mult))
            for a in range(2):
                for t in range(2):
                    m = 16 * a + 8 * t
                    dve.tensor_tensor(wkv[:, a, C * t:C * t + C].rearrange("p (h j) -> p h j", h=HEADS),
                                      kv_view[:, a, :, 1 + t, :],
                                      means[:, m:m + 8].rearrange("p (h o) -> p h o", o=1).broadcast_to([P, HEADS, HEADC]),
                                      ALU.subtract)
            for t in range(2):
                m = 32 + 8 * t
                last = dve.tensor_tensor(
                    bkv[0:PARTS, C * t:C * t + C].rearrange("p (h j) -> p h j", h=HEADS),
                    bqkv[0:PARTS, :].rearrange("p (h t j) -> p h t j", h=HEADS, t=3)[:, :, 1 + t, :],
                    means[0:PARTS, m:m + 8].rearrange("p (h o) -> p h o", o=1).broadcast_to([PARTS, HEADS, HEADC]),
                    ALU.subtract)
            link(last)

            def split(parts, values, n):
                hi, lo, rest = part_hi[:, 0:n], part_lo[:, 0:n], part_rest[:, 0:n]
                dve.memset(parts, 0.0)
                link(dve.tensor_copy(hi, values))
                dve.tensor_copy(parts[0:1, :], hi[0:1, :])
                link(dve.tensor_tensor(rest, values, hi, ALU.subtract))
                link(dve.tensor_copy(lo, rest))
                dve.tensor_copy(parts[32:33, :], lo[32:33, :])
                link(dve.tensor_tensor(rest, rest, lo, ALU.subtract))
                return dve.tensor_copy(parts[64:65, :], rest[64:65, :])

            split(kv_parts[:, :], bkv[0:PARTS, :], 2 * C).then_inc(wkv_ready, 1)

            def norm_step(t):
                s = t.back(1)
                if t.exists():
                    n = t.back(-1)
                    if not t.static or n.exists():
                        take_stats(n)
                    if t.static and t.offset == 3:
                        group_bases()
                    if t.static and t.offset == TILES - 1:
                        dve.wait_ge(prep_inputs, 1)
                        dve.reduce_sum(flag_g, tmp_g, axis=AX.X).then_inc(flags_ready, 1)
                        gate_columns()
                    dve.wait_ge(hi_done, t.i + 1)
                    dve.tensor_tensor(tab[:TOK, t.b, C:2 * C], xn[:TOK, t.b, :], tab[:TOK, t.b, 0:C], ALU.subtract)\
                       .then_inc(lo_done, 1)
                if s.exists():
                    dve.wait_ge(squared, s.i + 1)
                    dve.reduce_sum(stats[:TOK, s.b, 16:32], sq[:TOK, s.b, :].rearrange("p (g j) -> p g j", j=HEADC),
                                   axis=AX.X).then_inc(var_done, 1)
                n = t.back(-1)
                if t.exists() and (not t.static or n.exists()):
                    invert_deviation(n)
                r = t.back(2)
                if r.exists():
                    dve.wait_ge(kvn_done, r.i + 1)
                    dve.wait_ge(kv_added, r.i + 1)
                    dve.tensor_tensor(kv_total[:TOK, :], kv_total[:TOK, :], kvn[:TOK, r.b, :], ALU.add).then_inc(kv_added, 1)
                if s.exists():
                    dve.wait_ge(kstd_done, s.i + 1)
                    dve.reciprocal(stats[:TOK, s.b, 48:64], stats[:TOK, s.b, 32:48]).then_inc(kstd_link, 1)
                    dve.wait_ge(kstd_link, s.i + 1)
                    wait_past(dve, kv_summed, s.i - 1)
                    wait_past(dve, kv_added, s.i)
                    dve.tensor_tensor(kvn[:TOK, s.b, :].rearrange("p (g j) -> p g j", j=HEADC),
                                      bank[2 + s.b][:TOK, :].rearrange("p (g j) -> p g j", j=HEADC),
                                      stats[:TOK, s.b, 48:64].rearrange("p (g o) -> p g o", o=1)
                                      .broadcast_to([TOK, 16, HEADC]), ALU.mult).then_inc(kvn_done, 1)

            def invert_deviation(t):
                dve.wait_ge(std_done, t.i + 1)
                wait_past(dve, xn_done, t.i - 1)
                dve.reciprocal(stats[:TOK, t.b, 9:10], stats[:TOK, t.b, 8:9]).then_inc(rstd_link, 1)
                dve.wait_ge(rstd_link, t.i + 1)
                dve.tensor_scalar(stats[:TOK, t.b, 10:11], stats[:TOK, t.b, 6:7], stats[:TOK, t.b, 9:10], -1.0,
                                  ALU.mult, ALU.mult).then_inc(rstd_done, 1)

            def take_stats(t):
                dve.wait_ge(x_loaded[t.b], t.u * 16 + 16)
                wait_past(dve, rstd_done, t.i - 1)
                dve.bn_stats(stats[:TOK, t.b, 0:6], x_in[:TOK, t.b, :]).then_inc(stats_link, 1)
                dve.wait_ge(stats_link, t.i + 1)
                dve.sem_inc(stats_order, 1)
                dve.bn_aggr(stats[:TOK, t.b, 6:8], stats[:TOK, t.b, 0:6]).then_inc(stats_done, 1)

            def group_bases():
                dve.wait_ge(keys_ready, 1)
                dve.tensor_reduce(min_g, dst_f, axis=AX.X, op=ALU.min)
                link(dve.reduce_sum(done_g, cmp_g, axis=AX.X))
                link(dve.tensor_scalar(done_g, done_g, float(TOK), None, ALU.mult))
                dve.tensor_tensor(base_g, min_g, done_g, ALU.max).then_inc(bases_ready, 1)

            def gate_columns():
                dve.wait_ge(small_in, 16 * 39)
                link(dve.memset(biases[:, :, C:C + 1], 0.0))
                for h in range(2):
                    for r in range(RELS):
                        link(dve.tensor_tensor_reduce(out=gate_junk, in0=relw[:, h, r, 0:C], in1=a_rep, scale=1.0,
                                                      scalar=0.0, op0=ALU.mult, op1=ALU.add,
                                                      accum_out=relw[:, h, r, C:C + 1]))
                    link(dve.tensor_tensor_reduce(out=gate_junk, in0=rootw[:, h, 0:C], in1=a_rep, scale=1.0,
                                                  scalar=0.0, op0=ALU.mult, op1=ALU.add, accum_out=small[:, 4 + h:5 + h]))
                link(dve.tensor_tensor_reduce(out=gate_junk[0:PARTS, :], in0=biases[:, 0, 0:C], in1=a_rep[0:PARTS, :],
                                              scale=1.0, scalar=0.0, op0=ALU.mult, op1=ALU.add,
                                              accum_out=small[0:PARTS, 6:7]))
                dve.tensor_tensor(rootw[:, :, C], small[:, 4:6], att2, ALU.add)
                link(dve.tensor_tensor(biases[:, 0, C:C + 1], small[0:PARTS, 6:7], attb, ALU.add))
                split(bias_parts[:, :, :].rearrange("p a n -> p (a n)"), biases[:, :, :].rearrange("p a n -> p (a n)"),
                      3 * (C + 1)).then_inc(gnn_w_ready, 1)

            take_stats(Tile(None, 0))
            invert_deviation(Tile(None, 0))
            steps(dve, norm_step, 4, TILES + 2, ahead=1)


            dve.wait_ge(kv_summed, TILES + 1)
            for a in range(2):
                v = 4 * a
                dve.tensor_copy(vec[:, v:v + 1], vb)
                dve.tensor_tensor(vec[:, v + 1:v + 2], bank[4][:, 258 + a:259 + a], vg, ALU.mult)
                dve.tensor_tensor(small[:, a:a + 1], bank[4][:, 256 + a:257 + a], kg, ALU.mult)
                last = dve.tensor_copy(vec[:, v + 3:v + 4], kb)
            link(last)
            for a in range(2):
                last = dve.scalar_tensor_tensor(vec[:, 4 * a + 2:4 * a + 3], kb, float(N), small[:, a:a + 1],
                                                ALU.mult, ALU.add)
            last.then_inc(vec_ready, 1)
            dve.memset(kv_t, 0.0)
            dve.wait_ge(prep_turned, 2)
            dve.tensor_copy(key_t[:, :, :], bank[6][:, 0:2 * GROUPS].rearrange("p (s g) -> p s g", s=2))\
               .then_inc(keys_in_place, 1)
            dve.wait_ge(rows_ready, 1)
            link(dve.reduce_sum(any_f, flag_row[0:1, 0:GROUPS], axis=AX.X))
            link(dve.tensor_scalar(any_f, any_f, 0.5, None, ALU.is_gt))
            dve.tensor_copy(any_left[:, :], any_f)
            dve.wait_ge(prep_turned, 4)
            link(dve.tensor_copy(left_t, bank[5][:, 0:2 * GROUPS].rearrange("p (s g) -> p s g", s=2)))
            dve.sem_inc(any_ready, 1)

            dve.wait_ge(outer_done, 1)
            for a in range(2):
                for h in range(4):
                    lo, hi = h * HEADC, (h + 1) * HEADC
                    last = dve.scalar_tensor_tensor(kv_t[lo:hi, a, lo:hi], bank[4][lo:hi, a * P + lo:a * P + hi],
                                                    vg[lo:hi, :], grow[lo:hi, :], ALU.mult, ALU.mult)
            link(last)
            for a in range(2):
                for h in range(4):
                    lo, hi = h * HEADC, (h + 1) * HEADC
                    last = dve.tensor_tensor(kv_t[lo:hi, a, lo:hi], bank[3][lo:hi, a * P + lo:a * P + hi],
                                             kv_t[lo:hi, a, lo:hi], ALU.add)
            last.then_inc(kvt_ready, 1)

            dve.wait_ge(weff_done, 1)
            for a in range(2):
                dve.tensor_tensor(weff[:, a, :], bank[1][:, a * C:a * C + C], mw1[:, a, :], ALU.add)
            dve.tensor_tensor(beff[:, :], bank[3][:, 400:402], mb1, ALU.add).then_inc(weff_ready, 1)

            dve.wait_ge(acc_cleared, 1)
            dve.wait_ge(cnt_cleared, 1)
            dve.wait_ge(tail_cleared, 1)

            left = dve.value_load(any_left[0:1, 0:1], min_val=0, max_val=1)
            with dve.If(left > 0):
                dve.sem_inc(general_added, 1)
                with dve.Fori(0, GROUPS) as g:
                    dve.wait_ge(pool_at_group, g + 1)
                    dve.wait_ge(pe_at_group, g + 1)
                    dve.sem_inc(general_turn, 1)
                    flagged = dve.value_load(flag_row[0:1, ds(g, 1)], min_val=0, max_val=GROUP)
                    with dve.If(flagged > 0):
                        with dve.Fori(0, GENERAL_WINDOWS) as w:
                            with dve.If(w < 1):
                                dve.tensor_copy(left_rel, left_t[:, :, ds(g, 1)].rearrange("p s o -> p (s o)"))\
                                   .then_inc(general_link, 1)
                            with dve.Else():
                                dve.tensor_scalar(left_rel, left_rel, -float(WIN), None, ALU.add).then_inc(general_link, 1)
                            dve.wait_ge(general_link, g * GENERAL_WINDOWS + w + 1)
                            for k in range(2):
                                last = dve.tensor_scalar(onehot[:, k, :], keyrow[:, :], left_rel[:, k:k + 1], None,
                                                         ALU.is_equal)
                            last.then_inc(general_hot, 1)
                            dve.wait_ge(general_sum, g * GENERAL_WINDOWS + w + 1)
                            dve.wait_ge(general_added, g * GENERAL_WINDOWS + w + 1)
                            dve.tensor_tensor(acc3[:, :, ds(w * WIN, WIN)],
                                              bank[0][:, 0:2 * WIN].rearrange("p (h k) -> p h k", h=2),
                                              acc3[:, :, ds(w * WIN, WIN)], ALU.add)
                            dve.tensor_tensor(cnt[:, ds(w * WIN, WIN)], bank[0][:, 2 * WIN:3 * WIN],
                                              cnt[:, ds(w * WIN, WIN)], ALU.add).then_inc(general_added, 1)
                    with dve.Else():
                        dve.sem_inc(general_link, GENERAL_WINDOWS)
                        dve.sem_inc(general_hot, GENERAL_WINDOWS)
                        dve.sem_inc(general_added, GENERAL_WINDOWS)
                dve.wait_ge(general_added, GROUPS * GENERAL_WINDOWS + 1)

            def hot(g, slots):
                for k in range(2):
                    dve.wait_ge(group_summed, g * 2 + k + 1)
                    dve.tensor_scalar(onehot[:, span(slots[k], 1), :].rearrange("p o n -> p (o n)"), keyrow[:, :],
                                      key_t[:, k, span(g, 1)], None, ALU.is_equal).then_inc(hot_done, 1)

            def first_columns(g, n):
                _, cols = nc.values_load_multi_w_load_instructions(
                    base_row[0:1, span(g, n)], engines=[mybir.EngineType.DVE], min_val=0, max_val=ACC - WIN,
                    skip_runtime_bounds_check_because="a node's number times four")
                return cols

            def add(g, b, col):
                dve.wait_ge(group_summed, g * 2 + 2 + SLOTS)
                wait_past(dve, acc_added, g)
                dve.tensor_tensor(acc3[:, :, ds(col, WIN)], bank[b][:, 0:2 * WIN].rearrange("p (h k) -> p h k", h=2),
                                  acc3[:, :, ds(col, WIN)], ALU.add)
                dve.tensor_tensor(cnt[:, ds(col, WIN)], bank[b][:, 2 * WIN:3 * WIN], cnt[:, ds(col, WIN)], ALU.add)\
                   .then_inc(acc_added, 1)

            def mix_step(t):
                s = t.back(1)
                if s.exists():
                    dve.wait_ge(mix_rows_in[s.b], s.u * 32 + 32)
                    wait_past(dve, mix_stored[s.b], s.u * 16)
                    dve.scalar_tensor_tensor(m_out[:TOK, s.b, :], m_xn[:TOK, s.b, :], 2.0, m_x[:TOK, s.b, :],
                                             ALU.mult, ALU.add).then_inc(base_done, 1)
                    dve.wait_ge(base_done, s.i + 1)
                    dve.wait_ge(mix_done, s.i + 1)
                    dve.tensor_tensor(m_out[:TOK, s.b, :], bank[6 + s.b][:TOK, 0:C], m_out[:TOK, s.b, :], ALU.add)\
                       .then_inc(mixed, 1)
                g = t.i - MIX_FIRST
                if not t.static or 0 <= g < MIX_GROUPS:
                    hot(g + 2, [slot_of(g + 2, 0), slot_of(g + 2, 1)])
                    add(g, (t.b + MIX_FIRST) % 2, first_columns(g, 1)[0])

            dve.wait_ge(keys_in_place, 1)
            hot(0, [0, 1])
            hot(1, [2, 3])
            steps(dve, mix_step, MIX_FIRST + 2, TILES + 1)

            link(dve.memset(count_rows[:, :], 0.0))
            def take_counts(t):
                dve.wait_ge(acc_added, t.i * NODE_GROUPS + MIX_GROUPS + NODE_GROUPS)
                wait_past(dve, count_turned, t.i)
                for r in range(RELS):
                    k = 32 * r
                    last = dve.tensor_scalar(
                        count_rows[k:k + 1, :],
                        cnt[k:k + 1, span(t.i * KEYS, KEYS)].rearrange("p (n r) -> p n r", r=RELS)[:, :, r],
                        1.0, None, ALU.max)
                last.then_inc(count_ready, 1)

            def invert_counts(t):
                dve.wait_ge(count_turned, t.i + 1)
                if t.static and t.offset == 0:
                    dve.wait_ge(mix_done, TILES)
                dve.reciprocal(inverse, bank[7][:TOK, 0:32 * RELS].rearrange("p (r k) -> p r k", k=32)[:, :, 0]).then_inc(inverse_ready, 1)

            def scale_sums(t):
                dve.wait_ge(inverse_spread, t.i + 1)
                wait_past(dve, u_done, t.i)
                for h in range(2):
                    last = dve.tensor_tensor(sn[:, h, :, :],
                                             acc3[:, h, span(t.i * KEYS, KEYS)].rearrange("p (n r) -> p r n", r=RELS),
                                             bank[7][:, 0:KEYS].rearrange("p (r n) -> p r n", r=RELS), ALU.mult)
                last.then_inc(scaled, 1)

            NODE_LINKS = 14
            v, half, y, e, y_step = (nw[:TOK, k:k + 1] for k in (0, 1, 6, 2, 3))

            def blend(t, node):
                dve.wait_ge(tanh_done, t.i + 1)
                dve.wait_ge(n_rows_in, t.i * 32 + 32)
                wait_past(dve, xn2_done, t.i)
                dve.tensor_tensor(th[:TOK, :], th[:TOK, :], n_xn[:TOK, :], ALU.subtract)
                node(dve.tensor_scalar(ga[:TOK, :], ta[:TOK, :], 0.5, 0.5, ALU.mult, ALU.add))
                node(dve.scalar_tensor_tensor(x1[:TOK, :], th[:TOK, :], ga[:TOK, :], n_base[:TOK, :], ALU.mult, ALU.add))
                node(dve.bn_stats(st2[:TOK, :], x1[:TOK, :]))
                dve.sem_inc(x1_done, 1)
                node(dve.bn_aggr(mv2[:TOK, :], st2[:TOK, :]))

            def estimate(t, node):
                node(dve.tensor_scalar(v, mv2[:TOK, 1:2], EPS, None, ALU.add))
                dve.tensor_scalar(e, v, -0.5, None, ALU.mult)
                node(dve.tensor_scalar(half.bitcast(i32), v.bitcast(i32), 1, None, ALU.logical_shift_right))
                node(dve.tensor_scalar(y.bitcast(i32), half.bitcast(i32), -1.0, float(0x5f3759df), ALU.mult, ALU.add))

            def newton(node):
                node(dve.scalar_tensor_tensor(y_step, y, e, y, ALU.mult, ALU.mult))
                node(dve.scalar_tensor_tensor(y, y_step, 1.5, y, ALU.add, ALU.mult))

            def newton_end(t, node):
                newton(node)
                node(dve.tensor_scalar(nw[:TOK, 7:8], mv2[:TOK, 0:1], y, -1.0, ALU.mult, ALU.mult))
                assert node.n == NODE_LINKS, node.n
                dve.sem_inc(rstd2_done, 1)

            def route(t):
                dve.wait_ge(xn2_done, t.i + 1)
                dve.tensor_tensor_reduce(out=junk[:TOK, :], in0=xn2[:TOK, :], in1=wr_rep[:TOK, :], scale=1.0, scalar=0.0,
                                         op0=ALU.mult, op1=ALU.add, accum_out=wcol[:TOK, :]).then_inc(route_link, 1)
                dve.wait_ge(route_link, t.i + 1)
                dve.tensor_copy(w_all[:TOK, span(t.i, 1)], wcol[:TOK, :])
                dve.tensor_tensor(acc[:TOK, span(t.i * KEYS + ACC, C)], x1[:TOK, :], xn2[:TOK, :], ALU.add)\
                   .then_inc(base2_done, 1)

            def node_step(t):
                s, r = t.back(1), t.back(2)
                node = Links(dve, node_link)
                node.at(s.i * NODE_LINKS)
                if t.exists():
                    cols = first_columns(t.i * NODE_GROUPS + MIX_GROUPS, NODE_GROUPS)
                for q in range(NODE_GROUPS):
                    if t.exists():
                        g = t.i * NODE_GROUPS + (MIX_GROUPS + q)
                        if not (t.static and g + 2 >= GROUPS):
                            hot(g + 2, [(2 * (MIX_GROUPS + t.b * NODE_GROUPS + q + 2) + k) % SLOTS for k in range(2)])
                        add(g, (MIX_GROUPS + t.b * NODE_GROUPS + q) % 2, cols[q])
                    if q == 1 and s.exists():
                        scale_sums(s)
                    if q == 2 and r.exists():
                        route(r)
                    if q == 5 and s.exists():
                        blend(s, node)
                if t.exists():
                    take_counts(t)
                if s.exists():
                    estimate(s, node)
                    newton(node)
                if t.exists():
                    invert_counts(t)
                if s.exists():
                    newton(node)
                    newton_end(s, node)

            steps(dve, node_step, 4, TILES + 2)

            dve.wait_ge(y_kept, TILES)
            dve.wait_ge(base2_done, TILES)
            pick = Links(dve, select_link)
            T, S = TOK, TILES

            def field(at, n):
                return work[:T, at:at + n]

            w, sign, hi_i, lo_i, hi, lo = (field(32 * k, S) for k in range(6))
            dve.wait_ge(turned2, TILES)
            pick(dve.tensor_scalar(w, w_all[:T, :], br_rep[:T, :], None, ALU.add))
            pick(dve.tensor_scalar(sign.bitcast(i32), w.bitcast(i32), 31, 0x7fffffff, ALU.arith_shift_right,
                                   ALU.bitwise_and))
            pick(dve.tensor_tensor(sign.bitcast(i32), sign.bitcast(i32), w.bitcast(i32), ALU.bitwise_xor))
            dve.tensor_scalar(hi_i.bitcast(i32), sign.bitcast(i32), 16, None, ALU.arith_shift_right)
            pick(dve.tensor_scalar(lo_i.bitcast(i32), sign.bitcast(i32), 0xffff, None, ALU.bitwise_and))
            dve.tensor_scalar(hi, hi_i.bitcast(i32), 32768.0, None, ALU.add)
            pick(dve.tensor_copy(lo, lo_i.bitcast(i32)))
            digits = keyrow[:T, 1:16]
            cur, step, thresholds, digit = field(240, 1), field(241, 1), field(248, 15), field(242, 1)
            per_row, hits = field(264, 15), field(280, 15)
            cmp = work[:T, 300:300 + 15 * S].rearrange("p (d s) -> p d s", d=15)
            low = field(700, S)

            def kth_largest(keys, rounds_before):
                dve.memset(step, 4096.0)
                pick(dve.memset(cur, 0.0))
                base_links = pick.start + pick.n
                ROUND_LINKS = 6
                with dve.Fori(0, 4) as r:
                    pick.at(r * ROUND_LINKS + base_links)
                    pick(dve.tensor_scalar(thresholds, digits, step, cur, ALU.mult, ALU.add))
                    pick(dve.tensor_tensor(cmp, keys.rearrange("p (o s) -> p o s", o=1).broadcast_to([T, 15, S]),
                                           thresholds.rearrange("p (d o) -> p d o", o=1).broadcast_to([T, 15, S]),
                                           ALU.is_ge))
                    dve.reduce_sum(per_row, cmp, axis=AX.X).then_inc(counts_ready, 1)
                    dve.wait_ge(counts_summed, r + (rounds_before + 1))
                    pick(dve.tensor_scalar(hits, bank[0][:T, 0:15], KEPT - 0.5, None, ALU.is_gt))
                    pick(dve.reduce_sum(digit, hits, axis=AX.X))
                    pick(dve.scalar_tensor_tensor(cur, digit, step, cur, ALU.mult, ALU.add))
                    pick(dve.tensor_scalar(step, step, 1.0 / 16, None, ALU.mult))
                pick.at(4 * ROUND_LINKS + base_links)

            kth_largest(hi, 0)
            t0, t1 = field(730, S), field(760, S)
            dve.tensor_scalar(t0, hi, cur, 65537.0, ALU.is_gt, ALU.mult)
            pick(dve.tensor_scalar(t1, hi, cur, None, ALU.is_equal))
            pick(dve.scalar_tensor_tensor(low, lo, 1.0, t1, ALU.add, ALU.mult))
            pick(dve.tensor_tensor(low, low, t0, ALU.add))
            pick(dve.tensor_scalar(low, low, -1.0, None, ALU.add))
            kth_largest(low, 4)
            greater, equal = field(790, S), field(820, S + 1)
            dve.tensor_scalar(greater, low, cur, None, ALU.is_gt)
            pick(dve.tensor_scalar(equal[:, 0:S], low, cur, None, ALU.is_equal))
            dve.reduce_sum(equal[:, S:S + 1], greater, axis=AX.X).then_inc(counts_ready, 1)
            dve.wait_ge(counts_summed, 9)
            sums = [work[:T, 860 + 64 * k:860 + 64 * k + 64] for k in range(2)]
            for s_ in sums:
                dve.memset(s_[:, 0:32], 0.0)
            pick(dve.tensor_copy(sums[0][:, 32:32 + S + 1], bank[0][:T, 0:S + 1]))
            a, b = sums
            shift = 1
            while shift < S:
                pick(dve.tensor_tensor(b[:, 32:32 + S], a[:, 32:32 + S], a[:, 32 - shift:32 - shift + S], ALU.add))
                a, b = b, a
                shift *= 2
            before, room = field(1000, S), field(1030, 1)
            pick(dve.tensor_tensor(before, bank[1][:T, 0:S], a[:, 31:31 + S], ALU.add))
            pick(dve.tensor_scalar(room, sums[0][:, 32 + S:33 + S], -1.0, float(KEPT), ALU.mult, ALU.add))
            pick(dve.tensor_scalar(before, before, room, None, ALU.is_lt))
            pick(dve.tensor_tensor(before, before, equal[:, 0:S], ALU.mult))
            pick(dve.tensor_tensor(before, before, greater, ALU.add))
            pick(dve.tensor_tensor(w, w, before, ALU.mult))
            with dve.Fori(0, TILES) as i:
                dve.scalar_tensor_tensor(acc[:T, ds(i * KEYS, C)], acc[:T, ds(i * KEYS, C)], w[:, ds(i, 1)],
                                         acc[:T, ds(i * KEYS + ACC, C)], ALU.mult, ALU.add).then_inc(chosen, 1)

        @block.tensor
        def _(pe):
            pe.sem_inc(group_summed, SLOTS)
            pe.wait_ge(wkv_ready, 1)
            pe.wait_ge(pool_consts, 1)
            pe.matmul(bank[4][:, 0:260], vrow[0:1, 0:P], vrow[0:1, 0:260], start=True, stop=False, skip_group_check=True)

            def turn(to, rows_ap, n_rows, **flags):
                return pe.transpose(to, rows_ap, ident[:n_rows, :n_rows])

            def norm_step(t):
                s, r = t.back(1), t.back(2)
                if s.exists():
                    pe.wait_ge(xt_done, s.i + 1)
                    wait_past(pe, kvn_done, s.i - 1)
                    pe.matmul(bank[2 + s.b][:TOK, :], onesb[:, 0:TOK], kv_parts[:, :], start=True, stop=False)
                    for h in range(2):
                        last = pe.matmul(bank[2 + s.b][:TOK, :], xt[:, s.b, h, :], wkv[:, h, :], start=False, stop=h == 1)
                    last.then_inc(kv_done, 1)
                if t.exists():
                    pe.wait_ge(xn_done, t.i + 1)
                    wait_past(pe, xt_done, t.i - 1)
                    for h in range(2):
                        last = turn(bank[t.b][:, h * TOK:(h + 1) * TOK], xn[:TOK, t.b, h * P:(h + 1) * P], TOK)
                    last.then_inc(turned, 1)
                if r.exists():
                    pe.wait_ge(kvn_done, r.i + 1)
                    for a in range(2):
                        k, v = kvn[:TOK, r.b, a * P:(a + 1) * P], kvn[:TOK, r.b, C + a * P:C + (a + 1) * P]
                        last = pe.matmul(bank[4][:, a * P:(a + 1) * P], v, k, start=False, stop=False,
                                         skip_group_check=True)
                    last.then_inc(kv_summed, 1)

            steps(pe, norm_step, 4, TILES + 2)
            pe.wait_ge(kv_added, TILES + 1)
            for k in range(4):
                last = pe.matmul(bank[4][:, 256 + k:257 + k], kv_total[:TOK, k * P:(k + 1) * P], onesf[:TOK, 0:1],
                                 start=False, stop=True, skip_group_check=True)
            last.then_inc(kv_summed, 1)

            rest = GROUPS - P

            def turn_edges(b, ap):
                for blk, n in ((0, P), (1, rest)):
                    for k in range(2):
                        last = turn(bank[b][:, k * GROUPS + blk * P:k * GROUPS + blk * P + n],
                                    ap[:n, blk, k * P:(k + 1) * P], n)
                return last

            pe.wait_ge(keys_ready, 1)
            turn_edges(5, src_f).then_inc(prep_turned, 1)
            pe.wait_ge(prep_inputs, 1)
            turn_edges(6, key_f).then_inc(prep_turned, 1)
            pe.wait_ge(flags_ready, 1)
            for k, ap in enumerate((base_g[:, 0:1], base_g[:, 1:2], flag_g[:, 0:1], flag_g[:, 1:2])):
                last = turn(bank[7][0:1, k * P:(k + 1) * P], ap, P)
            last.then_inc(prep_turned, 1)
            pe.wait_ge(src_ready, 1)
            turn_edges(5, left_f).then_inc(prep_turned, 1)

            pe.wait_ge(vec_ready, 1)
            for k in range(4):
                last = turn(bank[0][0:2, k * P:(k + 1) * P], vec[:, 2 * k:2 * k + 2], P)
            last.then_inc(vec_turned, 1)
            pe.wait_ge(wq_ready, 1)
            for a in range(2):
                for h in range(2):
                    last = turn(bank[1][:, a * C + h * P:a * C + (h + 1) * P], wq[:, h, a * P:(a + 1) * P], P)
            last.then_inc(wq_turned, 1)
            pe.wait_ge(vrow_ready, 1)
            for a in range(2):
                last = pe.matmul(bank[3][:, a * P:(a + 1) * P], vrow[0:2, 2 * a * P:(2 * a + 1) * P],
                                 vrow[0:2, (2 * a + 1) * P:(2 * a + 2) * P], start=True, stop=True)
            last.then_inc(outer_done, 1)
            pe.wait_ge(kvt_ready, 1)
            for a in range(2):
                last = pe.matmul(bank[2][:, a * C:(a + 1) * C], kv_t[:, a, :], mw1[:, a, :], start=True, stop=True)
            last.then_inc(b1w_done, 1)
            pe.wait_ge(b1w_ready, 1)
            pe.wait_ge(wqt_ready, 1)
            for o in range(2):
                for a in range(2):
                    pe.matmul(bank[3][:, 400 + o:401 + o], b1w[:, a, o * P:(o + 1) * P], bq[:, a:a + 1], start=a == 0,
                              stop=a == 1)
            for h in range(2):
                for a in range(2):
                    last = pe.matmul(bank[1][:, h * C:(h + 1) * C], wqT[:, a, h * P:(h + 1) * P], b1w[:, a, :],
                                     start=a == 0, stop=a == 1)
            last.then_inc(weff_done, 1)

            def sum_group(b, slots, last_inc):
                rows_k = [rows[:, span(s_, 1), :].rearrange("p o n -> p (o n)") for s_ in slots]
                hot_k = [onehot[:, span(s_, 1), :].rearrange("p o n -> p (o n)") for s_ in slots]
                for h in range(2):
                    for k in range(2):
                        for part in range(2):
                            pe.matmul(bank[b][:, h * WIN:(h + 1) * WIN],
                                      rows_k[k][:, part * C + h * P:part * C + (h + 1) * P], hot_k[k],
                                      start=k == 0 and part == 0, stop=k == 1 and part == 1)
                for k in range(2):
                    last = pe.matmul(bank[b][:, 2 * WIN:3 * WIN], onesh[:, :], hot_k[k], start=k == 0, stop=k == 1)
                last_inc(last)

            pe.wait_ge(any_ready, 1)
            pe.wait_ge(vrow_ready, 1)
            left = pe.value_load(any_left[0:1, 0:1], min_val=0, max_val=1)
            with pe.If(left > 0):
                with pe.Fori(0, GROUPS) as g:
                    pe.sem_inc(pe_at_group, 1)
                    pe.wait_ge(general_turn, g + 1)
                    flagged = pe.value_load(flag_row[0:1, ds(g, 1)], min_val=0, max_val=GROUP)
                    with pe.If(flagged > 0):
                        with pe.Fori(0, GENERAL_WINDOWS) as w:
                            pe.wait_ge(general_in, g * 32 + 32)
                            pe.wait_ge(general_hot, g * GENERAL_WINDOWS + w + 1)
                            pe.wait_ge(general_added, g * GENERAL_WINDOWS + w + 1)
                            sum_group(0, [0, 1], lambda ins: ins.then_inc(general_sum, 1))
                    with pe.Else():
                        pe.sem_inc(general_sum, GENERAL_WINDOWS)

            def agg(g, b, slots):
                pe.wait_ge(gathered, g * 2 + 5)
                pe.wait_ge(hot_done, g * 2 + 2)
                wait_past(pe, acc_added, g - 1)
                sum_group(b, slots, lambda ins: ins.then_inc(group_summed, 2))

            pe.wait_ge(weff_ready, 1)
            pe.wait_ge(mix_w_in, 16)

            def mix_step(t):
                s = t.back(1)
                if t.exists():
                    pe.wait_ge(mix_xt_in[t.b], t.u * 16 + 16)
                    wait_past(pe, gelu_done, t.i - 1)
                    for o in range(2):
                        for h in range(2):
                            last = pe.matmul(bank[2 + t.b][:, o * TOK:(o + 1) * TOK], weff[:, h, o * P:(o + 1) * P],
                                             m_xt[:, t.b, h, :], start=h == 0, stop=h == 1)
                    last.then_inc(h_done, 1)
                g = t.i - MIX_FIRST
                if not t.static or 0 <= g < MIX_GROUPS:
                    agg(g, (t.b + MIX_FIRST) % 2, [slot_of(g, 0), slot_of(g, 1)])
                if s.exists():
                    pe.wait_ge(gelu_done, s.i + 1)
                    wait_past(pe, mixed, s.i - 1)
                    pe.matmul(bank[6 + s.b][:TOK, 0:C], onesb[:, 0:TOK], bias_parts[:, 1, 0:C], start=True, stop=False)
                    for o in range(2):
                        last = pe.matmul(bank[6 + s.b][:TOK, 0:C], m_h[:, s.b, o, :], mw2[:, o, :], start=False,
                                         stop=o == 1)
                    last.then_inc(mix_done, 1)

            steps(pe, mix_step, MIX_FIRST + 2, TILES + 1)

            pe.wait_ge(gelu_done, TILES)
            pe.wait_ge(mixed, TILES)
            pe.wait_ge(gnn_w_ready, 1)
            pe.wait_ge(ffn_w_in, 32)

            u = bank[2][:TOK, 0:C + 1]

            def own_part(t):
                pe.wait_ge(n_xt_in, t.i * 16 + 16)
                wait_past(pe, tanh_done, t.i)
                pe.matmul(u, onesb[:, 0:TOK], bias_parts[:, 0, :], start=True, stop=False)
                for h in range(2):
                    pe.matmul(u, n_xt[:, h, :], rootw[:, h, :], start=False, stop=False)

            def relations_part(t, h):
                pe.wait_ge(scaled, t.i + 1)
                for r in range(RELS):
                    last = pe.matmul(u, sn[:, h, r, :], relw[:, h, r, :], start=False, stop=h == 1 and r == RELS - 1)
                if h == 1:
                    last.then_inc(u_done, 1)

            def ffn_up(t, half):
                if half == 0:
                    pe.wait_ge(xt3_done, t.i + 1)
                wait_past(pe, gelu2_done, t.i * 2 + half - 1)
                for k in range(4):
                    c = 4 * half + k
                    for h in range(2):
                        last = pe.matmul(bank[4 + half][:, k * TOK:(k + 1) * TOK], w1[:, h, c * P:(c + 1) * P],
                                         xt3[:, h, :], start=h == 0, stop=h == 1)
                last.then_inc(hid_done, 1)

            def ffn_down(t):
                wait_past(pe, y_kept, t.i)
                y = bank[6][:TOK, 0:C]
                pe.matmul(y, onesb[:, 0:TOK], bias_parts[:, 2, 0:C], start=True, stop=False)
                for c in range(HCHUNKS):
                    if c % 4 == 0:
                        pe.wait_ge(gelu2_done, t.i * 2 + c // 4 + 1)
                    last = pe.matmul(y, hT[:, c, :], w2[:, c, :], start=False, stop=c == HCHUNKS - 1)
                last.then_inc(y_done, 1)

            def node_step(t):
                s, r = t.back(1), t.back(2)

                def agg_at(q):
                    if t.exists():
                        agg(t.i * NODE_GROUPS + (MIX_GROUPS + q), (MIX_GROUPS + t.b * NODE_GROUPS + q) % 2,
                            [(2 * (MIX_GROUPS + q) + k) % SLOTS for k in range(2)])

                agg_at(0)
                if s.exists():
                    own_part(s)
                agg_at(1)
                if r.exists():
                    pe.wait_ge(xn2_done, r.i + 1)
                    wait_past(pe, xt3_done, r.i)
                    for h in range(2):
                        last = turn(bank[3][:, h * TOK:(h + 1) * TOK], xn2[:TOK, h * P:(h + 1) * P], TOK)
                    last.then_inc(turned2, 1)
                if s.exists():
                    pe.wait_ge(spread_ready, s.i + 1)
                    pe.matmul(bank[7][:, 0:KEYS], onesf[:TOK, :], spread, start=True, stop=True)\
                      .then_inc(inverse_spread, 1)
                if r.exists():
                    ffn_up(r, 0)
                agg_at(2)
                if r.exists():
                    ffn_up(r, 1)
                agg_at(3)
                if s.exists():
                    relations_part(s, 0)
                agg_at(4)
                if s.exists():
                    relations_part(s, 1)
                agg_at(5)
                agg_at(6)
                if r.exists():
                    ffn_down(r)
                if t.exists():
                    pe.wait_ge(count_ready, t.i + 1)
                    turn(bank[7][:TOK, 0:97], count_rows[:, :], 97).then_inc(count_turned, 1)

            steps(pe, node_step, 4, TILES + 2)

            with pe.Fori(0, 8) as r:
                pe.wait_ge(counts_ready, r + 1)
                pe.matmul(bank[0][:TOK, 0:15], onesf[:TOK, 0:TOK], work[:TOK, 264:279], start=True, stop=True)\
                  .then_inc(counts_summed, 1)
            pe.wait_ge(counts_ready, 9)
            equal = work[:TOK, 820:820 + TILES + 1]
            pe.matmul(bank[0][:TOK, 0:TILES + 1], onesf[:TOK, 0:TOK], equal, start=True, stop=True)
            pe.matmul(bank[1][:TOK, 0:TILES], tri[:TOK, 0:TOK], equal[:, 0:TILES], start=True, stop=True)\
              .then_inc(counts_summed, 1)


_INS = ["x", "src", "dst", "edge_type_4", "L0_gnn_rel_weight", "L0_gnn_root_weight", "L0_gnn_rgcn_bias",
        "L0_gnn_att_weight", "L0_gnn_att_bias", "L0_mix_w_qkv", "L0_mix_b_qkv", "L0_mix_kln_g", "L0_mix_kln_b",
        "L0_mix_vln_g", "L0_mix_vln_b", "L0_mix_w1", "L0_mix_b1", "L0_mix_w2", "L0_mix_b2", "L0_ffn_wr", "L0_ffn_br",
        "L0_ffn_w1", "L0_ffn_b1", "L0_ffn_w2", "L0_ffn_b2"]


def kernel(**inputs):
    import numpy as np
    import concourse.bacc as bacc
    from concourse.bass_utils import run_bass_kernel_spmd

    nc = bacc.Bacc("TRN2", target_bir_lowering=False, num_devices=1)
    arrays, args = {}, []
    for name in _INS:
        a = np.ascontiguousarray(inputs[name])
        arrays[f"in_{name}"] = a
        args.append(nc.dram_tensor(f"in_{name}", a.shape, mybir.dt.from_np(a.dtype), kind="ExternalInput").ap())
    args.append(nc.dram_tensor("out", (N, C), mybir.dt.float32, kind="ExternalOutput").ap())
    gps_block(nc, *args)
    result = run_bass_kernel_spmd(nc, [arrays], core_ids=[0])
    return result.results[0]["out"]
```

```python
import concourse.bass as bass
from concourse import mybir
from contextlib import ExitStack

N = 3125
C = 256
EDGES = 50000
RELS = 4
HEADS, HEADC = 8, 32
HIDDEN = 1024
P = 128
TOK = 125
TILES = N // TOK
KEYS = TOK * RELS
WIN = 128
GROUP = 256
GROUPS = -(-EDGES // GROUP)
GATHERS = 2 * GROUPS
SLOTS = 7
NODE_GROUPS = 7
MIX_GROUPS = GROUPS - TILES * NODE_GROUPS
MIX_FIRST = TILES - MIX_GROUPS
ACC = (N - 1) * RELS + WIN
GENERAL_WINDOWS = -(-N * RELS // WIN)
KEPT = 1561
EPS = 1e-5
PAD_NODE = 1000000
HCHUNKS = HIDDEN // P
DVE_TILES = 15
PARTS = 65
TURN_AT = 22
SPREAD = ((0, 112), (112, 13))
STORED = 4 * 16


class Tile:

    def __init__(self, half, offset):
        self.half, self.offset = half, offset
        self.static = half is None
        self.i = offset if self.static else half * 2 + offset
        self.b = offset % 2
        self.u = offset // 2 if self.static else half + offset // 2

    def back(self, n):
        return Tile(self.half, self.offset - n)

    def exists(self):
        return not self.static or 0 <= self.offset < TILES


def steps(eng, step, first, last, ahead=0):
    stop = first + (TILES - ahead - first) // 2 * 2
    for i in range(first):
        step(Tile(None, i))
    with eng.Fori(0, (stop - first) // 2) as half:
        for k in range(2):
            step(Tile(half, first + k))
    for i in range(stop, last):
        step(Tile(None, i))


def wait_past(eng, sem, count):
    if not isinstance(count, int) or count > 0:
        eng.wait_ge(sem, count)


class Links:

    def __init__(self, eng, sem):
        self.eng, self.sem, self.start, self.n = eng, sem, 0, 0

    def at(self, start):
        self.start, self.n = start, 0

    def __call__(self, ins):
        self.n += 1
        ins.then_inc(self.sem, 1)
        self.eng.wait_ge(self.sem, self.start + self.n)


def gps_block(nc, x, src, dst, etype, rel_w, root_w, gnn_b, att_w, att_b, w_qkv, b_qkv, kln_g, kln_b,
              vln_g, vln_b, mix_w1, mix_b1, mix_w2, mix_b2, wr, br, ffn_w1, ffn_b1, ffn_w2, ffn_b2, out):
    f32, f16, bf16, i32, u16 = (mybir.dt.float32, mybir.dt.float16, mybir.dt.bfloat16, mybir.dt.int32,
                                mybir.dt.uint16)
    ALU, ACT, AX = mybir.AluOpType, mybir.ActivationFunctionType, mybir.AxisListType
    ds = bass.ds

    table = nc.dram_tensor("table", (N, 2 * C), f16).ap()
    xn_d = nc.dram_tensor("xn_d", (TILES, P, C), f32).ap()
    base_d = nc.dram_tensor("base_d", (TILES, P, C), f32).ap()
    xt_d = nc.dram_tensor("xt_d", (TILES, P, 2 * TOK), f32).ap()

    with ExitStack() as ctx:
        def sb(name, shape, dt):
            return ctx.enter_context(nc.sbuf_tensor(name, shape, dt))

        acc = sb("acc", [P, 2 * ACC], f32)
        acc3 = acc[:, :].rearrange("p (h k) -> p h k", h=2)
        cnt = sb("cnt", [P, ACC], u16)
        relw = sb("relw", [P, 2, RELS, C + 1], f32)
        rootw = sb("rootw", [P, 2, C + 1], f32)
        fw = sb("fw", [P, 4096], f32)
        w1 = fw[:, 0:2048].rearrange("p (a n) -> p a n", a=2)
        w2 = fw[:, 2048:4096].rearrange("p (a n) -> p a n", a=HCHUNKS)
        rows = sb("rows", [P, SLOTS, 2 * C], f16)
        onehot = sb("onehot", [P, SLOTS, WIN], f16)
        key_t = sb("key_t", [P, 2, GROUPS], f32)
        src_t = sb("src_t", [P, GATHERS], i32)
        index = sb("index", [P, 2, SLOTS], i32)
        ident = sb("ident", [P, P], f32)
        onesf = sb("onesf", [P, P], f32)
        onesh = sb("onesh", [P, P], f16)
        keyrow = sb("keyrow", [P, WIN], f16)
        base_row = sb("base_row", [1, 2 * P], i32)
        flag_row = sb("flag_row", [1, 2 * P], i32)
        any_left = sb("any_left", [1, 1], i32)
        biases = sb("biases", [PARTS, 3, C + 1], f32)
        bias_parts = sb("bias_parts", [PARTS, 3, C + 1], bf16)
        kv_parts = sb("kv_parts", [PARTS, 2 * C], bf16)
        onesb = sb("onesb", [PARTS, P], bf16)
        fb1 = sb("fb1", [P, HCHUNKS], f32)
        wr_rep = sb("wr_rep", [P, C], f32)
        br_rep = sb("br_rep", [P, 1], f32)
        w_all = sb("w_all", [P, TILES], f32)
        small = sb("small", [P, 64], f32)
        stats = sb("stats", [P, 2, 64], f32)
        ctmp = sb("ctmp", [P, 2304], f32)
        work = sb("work", [P, 5000], f32)

        tri = sb("tri", [P, P], f32)

        eps_col, zero_col, minus_one = small[:, 40:41], small[:, 41:42], small[:, 42:43]
        att2, attb, mb1, bq = small[:, 20:22], small[0:PARTS, 22:23], small[:, 24:26], small[:, 26:28]
        kg, kb, vg, vb = (small[:, 28 + k:29 + k] for k in range(4))

        mw1, wqT, b1w, wq = (ctmp[:, 512 * k:512 * k + 512].rearrange("p (a n) -> p a n", a=2) for k in range(4))
        a_rep = ctmp[:, 2048:2304]

        TEMP = 8500
        used = [2 * ACC - TEMP]

        def temp(n):
            used[0] += n
            assert used[0] <= 2 * ACC
            return acc[:, used[0] - n:used[0]]

        x_in = temp(512).rearrange("p (b n) -> p b n", b=2)
        xn = temp(512).rearrange("p (b n) -> p b n", b=2)
        tab = temp(512).bitcast(f16).rearrange("p (b n) -> p b n", b=2)
        k_total = temp(256)
        xt = temp(500).rearrange("p (b h n) -> p b h n", b=2, h=2)
        sq = temp(1024).rearrange("p (b n) -> p b n", b=2)
        kvn = temp(8 * (P + 1)).rearrange("p (b k n) -> p b k n", b=2, k=4)
        wkv = temp(1024).rearrange("p (a n) -> p a n", a=2)
        wqkv = temp(1536).rearrange("p (a n) -> p a n", a=2)
        bkv = temp(512)
        bqkv = temp(768)
        means = temp(48)

        ep = [fw[:, 512 * k:512 * k + 512] for k in range(8)]
        src_g, dst_g, typ_g = [e.bitcast(i32).rearrange("p (b n) -> p b n", b=2) for e in ep[0:3]]
        src_f, dst_f, typ_f, key_f, left_f = [e.rearrange("p (b n) -> p b n", b=2) for e in ep[3:8]]
        tmp_g = work[:, 0:512].rearrange("p (b n) -> p b n", b=2)
        out_g = work[:, 512:1024].rearrange("p (b n) -> p b n", b=2)
        thr = work[:, 1024:1048]
        gcol = work[:, 1048:1050]
        thr_i = work[:, 1050:1074].bitcast(i32)
        gcol_i = work[:, 1074:1076].bitcast(i32)
        cmp_g = work[:, 1076:1124].rearrange("p (b n) -> p b n", b=2)
        base_g = work[:, 1124:1126]
        flag_g = work[:, 1126:1128]
        min_g = work[:, 1128:1130]
        done_g = work[:, 1130:1132]
        iota_i = work[:, 1132:1260].bitcast(i32)
        left_t = work[:, 1300:1300 + 2 * GROUPS].rearrange("p (s g) -> p s g", s=2)
        left_rel = work[:, 1960:1962]
        any_f = work[0:1, 1970:1971]
        gate_junk = work[:, 2500:3780].rearrange("p (k n) -> p k n", k=5)

        kv_split = (work[0:PARTS, 2500:2756].bitcast(bf16), work[0:PARTS, 2756:3012].bitcast(bf16),
                    work[0:PARTS, 3012:3524])
        bias_split = (work[0:PARTS, 4300:4430].bitcast(bf16), work[0:PARTS, 4430:4560].bitcast(bf16),
                      work[0:PARTS, 4560:4818])

        m_xt = work[:, 2000:2500].rearrange("p (b h n) -> p b h n", b=2, h=2)
        m_x = work[:, 2500:3012].rearrange("p (b n) -> p b n", b=2)
        m_xn = sb("m_xn", [P, 2, C], f32)
        m_h = work[:, 3012:3512].rearrange("p (b h n) -> p b h n", b=2, h=2)
        m_out = work[:, 3520:4032].rearrange("p (b n) -> p b n", b=2)
        weff = work[:, 0:512].rearrange("p (a n) -> p a n", a=2)
        mw2 = work[:, 512:1024].rearrange("p (a n) -> p a n", a=2)
        kv_t = work[:, 4032:4288].rearrange("p (a n) -> p a n", a=2)
        vec = work[:, 4288:4296]
        vrow = work[:, 4300:4812]
        beff = work[:, 4850:4852]
        grow = work[:, 4860:4892]

        sn = work[:, 0:1000].rearrange("p (h r n) -> p h r n", h=2, r=RELS)
        spread = work[:TOK, 1000:1500]
        inverse = work[:TOK, 4562:4566]
        hT = work[:, 1500:2500].rearrange("p (c n) -> p c n", c=HCHUNKS)
        n_xt = work[:, 2500:2750].rearrange("p (h n) -> p h n", h=2)
        n_xn = work[:, 2750:3006]
        n_base = work[:, 3006:3262]
        th = work[:, 3262:3518]
        x1 = work[:, 3518:3774]
        xn2 = work[:, 3774:4030]
        xt3 = work[:, 4030:4280].rearrange("p (h n) -> p h n", h=2)
        junk = work[:, 4280:4536]
        ta = work[:, 4540:4541]
        ga = work[:, 4541:4542]
        st2 = work[:, 4544:4550]
        mv2 = work[:, 4550:4552]
        nw = work[:, 4552:4560]
        wcol = work[:, 4560:4561]
        count_rows = sb("count_rows", [32 * (RELS - 1) + 1, TOK], f32)

        bank = [ctx.enter_context(nc.psum_tensor(f"bank{k}", [P, 512], f32)) for k in range(8)]

        def sem(name):
            return ctx.enter_context(nc.semaphore(name))

        def sems(names):
            return [sem(n) for n in names.split()]

        edges_cleared, edges_in, weights_in, small_in, mix_w_in, ffn_w_in = sems(
            "edges_cleared edges_in weights_in small_in mix_w_in ffn_w_in")
        pool_link, dve_link, act_link, pool_consts, keys_ready, acc_cleared, cnt_cleared = sems(
            "pool_link dve_link act_link pool_consts keys_ready acc_cleared cnt_cleared")
        bases_ready, flags_ready = sems("bases_ready flags_ready")
        prep_inputs, prep_turned, src_ready, rows_ready, keys_in_place, any_ready, tail_cleared = sems(
            "prep_inputs prep_turned src_ready rows_ready keys_in_place any_ready tail_cleared")
        x_loaded = sems("x_loaded0 x_loaded1")
        stored = sems("stored0 stored1")
        eps_ready = sem("eps_ready")
        wkv_ready, stats_link, stats_order, stats_done, std_done, rstd_link, rstd_done = sems(
            "wkv_ready stats_link stats_order stats_done std_done rstd_link rstd_done")
        xn_done, hi_done, lo_done, turned, xt_done = sems(
            "xn_done hi_done lo_done turned xt_done")
        kv_done, squared, var_done, kstd_done, kstd_link, kvn_done, kv_added, kv_summed = sems(
            "kv_done squared var_done kstd_done kstd_link kvn_done kv_added kv_summed")
        wq_ready, vec_ready, vec_turned, vrow_ready, outer_done, kvt_ready, wq_turned, wqt_ready = sems(
            "wq_ready vec_ready vec_turned vrow_ready outer_done kvt_ready wq_turned wqt_ready")
        b1w_done, b1w_ready, weff_done, weff_ready, gnn_w_ready = sems(
            "b1w_done b1w_ready weff_done weff_ready gnn_w_ready")
        general_index, general_in, general_link, general_hot, general_sum, general_added = sems(
            "general_index general_in general_link general_hot general_sum general_added")
        pool_at_group, pe_at_group, general_turn = sems("pool_at_group pe_at_group general_turn")
        slot_in = [sem(f"slot_in{k}") for k in range(SLOTS)]
        index_ready, gathered, hot_done, group_summed, acc_added = sems(
            "index_ready gathered hot_done group_summed acc_added")
        mix_xt_in, mix_rows_in = sems("mix_xt_in0 mix_xt_in1"), sems("mix_rows_in0 mix_rows_in1")
        mix_stored = sems("mix_stored0 mix_stored1")
        h_done, gelu_done, base_done, mix_done, mixed = sems("h_done gelu_done base_done mix_done mixed")
        n_xt_in, n_rows_in, final_stored = sems("n_xt_in n_rows_in final_stored")
        count_ready, count_turned, inverse_ready, spread_ready, inverse_spread = sems(
            "count_ready count_turned inverse_ready spread_ready inverse_spread")
        rows_cleared, invert_link = sems("rows_cleared invert_link")
        scaled, u_done, tanh_done, node_link, x1_done = sems(
            "scaled u_done tanh_done node_link x1_done")
        route_link, xn2_done, base2_done, turned2, xt3_done, hid_done, gelu2_done, y_done, y_kept = sems(
            "route_link xn2_done base2_done turned2 xt3_done hid_done gelu2_done y_done y_kept")
        select_link, counts_ready, counts_summed, chosen = sems("select_link counts_ready counts_summed chosen")
        weights_chosen, y_weighed, added = sems("weights_chosen y_weighed added")

        block = ctx.enter_context(nc.Block())

        def load_x(eng, to, t, signal):
            n = TOK if t.static and t.i == TILES - 1 else P
            eng.dma_start(to[0:n], x[span(t.i * TOK, n), :]).then_inc(signal, 16)

        def store_table(eng, t, rows_ap, signal):
            for lo, n in SPREAD:
                eng.dma_start(table[span(t.i * TOK + lo, n), :], rows_ap[lo:lo + n]).then_inc(signal, 16)

        def span(start, n):
            return slice(start, start + n) if isinstance(start, int) else ds(start, n)

        def slot_of(g, k):
            return (g * 2 + k) % SLOTS

        def tile_of(t, ap):
            return ap[span(t.i, 1), :, :].rearrange("a p n -> p (a n)")

        @block.sync
        def _(sp):
            def norm_step(t):
                if t.static and t.offset < 1:
                    load_x(sp, x_in[:, t.b, :], t, x_loaded[t.b])
                if t.static and t.offset == 0:
                    first_loads()
                s = t.back(1)
                if s.exists():
                    sp.wait_ge(lo_done, s.i + 1)
                    store_table(sp, s, tab[:TOK, s.b, :], stored[s.b])
                    sp.dma_start(tile_of(s, xn_d), xn[:, s.b, :]).then_inc(stored[s.b], 16)
                    sp.wait_ge(xt_done, s.i + 1)
                    sp.dma_start(tile_of(s, xt_d), xt[:, s.b, :, :].rearrange("p h n -> p (h n)"))\
                      .then_inc(stored[s.b], 16)

            def first_loads():
                second = Tile(None, 1)
                load_x(sp, x_in[:, 1, :], second, x_loaded[1])
                sp.dma_start(wqkv, w_qkv.rearrange("(a p) n -> p a n", p=P)).then_inc(weights_in, 16)
                sp.dma_start(bqkv[0:PARTS, :], b_qkv.rearrange("(a n) -> a n", a=1).broadcast_to([PARTS, 3 * C]))\
                  .then_inc(weights_in, 16)
                sp.wait_ge(edges_cleared, 1)
                tail = EDGES - (GROUPS - 1) * GROUP
                full = GROUPS - 1 - P
                for ap, d in ((src_g, src), (dst_g, dst), (typ_g, etype)):
                    sp.dma_start(ap[:, 0, :], d[0:P * GROUP].rearrange("(p n) -> p n", n=GROUP)).then_inc(edges_in, 16)
                    sp.dma_start(ap[0:full, 1, :], d[P * GROUP:(GROUPS - 1) * GROUP].rearrange("(p n) -> p n", n=GROUP))\
                      .then_inc(edges_in, 16)
                    sp.dma_start(ap[full:full + 1, 1, 0:tail], d[EDGES - tail:EDGES].rearrange("(p n) -> p n", p=1))\
                      .then_inc(edges_in, 16)

            steps(sp, norm_step, 4, TILES + 1)

            sp.wait_ge(stored[0], STORED * 13)
            sp.wait_ge(stored[1], STORED * 12)
            sp.dma_start(mw2, mix_w2.rearrange("(a p) n -> p a n", p=P)).then_inc(mix_w_in, 16)
            sp.wait_ge(prep_turned, 4)
            sp.dma_start(w1, ffn_w1.rearrange("(a p) n -> p a n", p=P)).then_inc(ffn_w_in, 16)
            sp.dma_start(w2, ffn_w2.rearrange("(c p) n -> p c n", p=P)).then_inc(ffn_w_in, 16)

            def mix_step(t):
                if t.exists():
                    wait_past(sp, h_done, t.i - 1)
                    sp.dma_start(m_xt[:, t.b, :, :].rearrange("p h n -> p (h n)"), tile_of(t, xt_d))\
                      .then_inc(mix_xt_in[t.b], 16)
                r = t.back(1)
                if r.exists():
                    if r.static and r.offset == 0:
                        sp.wait_ge(weff_ready, 1)
                    wait_past(sp, mixed, r.i - 1)
                    load_x(sp, m_x[:, r.b, :], r, mix_rows_in[r.b])
                    sp.dma_start(m_xn[:, r.b, :], tile_of(r, xn_d)).then_inc(mix_rows_in[r.b], 16)

            steps(sp, mix_step, MIX_FIRST + 2, TILES + 1)
            sp.wait_ge(mix_stored[0], 16 * 13)
            sp.wait_ge(mix_stored[1], 16 * 12)

            def node_step(t):
                if t.exists():
                    if t.static and t.offset == 0:
                        sp.wait_ge(h_done, TILES)
                        sp.wait_ge(mixed, TILES)
                    wait_past(sp, u_done, t.i)
                    sp.dma_start(n_xt.rearrange("p h n -> p (h n)"), tile_of(t, xt_d)).then_inc(n_xt_in, 16)
                    wait_past(sp, x1_done, t.i)
                    sp.dma_start(n_xn[:, :], tile_of(t, xn_d)).then_inc(n_rows_in, 16)
                    sp.dma_start(n_base[:, :], tile_of(t, base_d)).then_inc(n_rows_in, 16)

            steps(sp, node_step, 4, TILES)

            for c, made in ((0, 5), (3, 5), (1, 10), (4, 10), (2, 15)):
                sp.wait_ge(added if c >= 3 else chosen, made)
                for lo, hi in ((0, 112), (112, TOK)):
                    sp.dma_start(out[c * 5 * TOK:(c + 1) * 5 * TOK, :].rearrange("(t p) n -> p t n", p=TOK)[lo:hi],
                                 acc[lo:hi, c * 5 * KEYS:(c + 1) * 5 * KEYS].rearrange("p (t k) -> p t k", k=KEYS)[:, :, 0:C])\
                      .then_inc(final_stored, 16)
            sp.wait_ge(final_stored, 16 * 10)

        @block.gpsimd
        def _(pool):
            link = Links(pool, pool_link)
            pool.memset(src_g, 0)
            pool.memset(typ_g, 0)
            link(pool.memset(dst_g, PAD_NODE))
            pool.sem_inc(edges_cleared, 1)
            link(pool.memset(ident[:, :], 0.0))
            link(pool.affine_select(out=ident[:, :], in_=ident[:, :], compare_op=ALU.not_equal, fill=1.0, base=0,
                                    pattern=[[-1, P]], channel_multiplier=1))
            pool.memset(onesf[:, :], 1.0)
            pool.memset(onesb[:, :], 1.0)
            link(pool.memset(onesh[:, :], 1.0))
            link(pool.affine_select(out=tri[:, :], in_=onesf[:, :], compare_op=ALU.is_gt, fill=0.0, base=0,
                                    pattern=[[1, P]], channel_multiplier=-1))
            link(pool.iota(iota_i, pattern=[[1, WIN]], base=0, channel_multiplier=0))
            link(pool.tensor_copy(keyrow[:, :], iota_i))
            pool.sem_inc(pool_consts, 1)
            pool.iota(thr_i, pattern=[[NODE_GROUPS, TILES - 1]], base=MIX_GROUPS + NODE_GROUPS, channel_multiplier=0)
            link(pool.iota(gcol_i, pattern=[[P, 2]], base=0, channel_multiplier=1))
            pool.tensor_copy(thr, thr_i)
            link(pool.tensor_copy(gcol, gcol_i))
            for blk in range(2):
                last = pool.tensor_scalar(cmp_g[:, blk, :], thr, gcol[:, blk:blk + 1], None, ALU.is_le)
            link(last)
            pool.wait_ge(edges_in, 16 * 9)
            pool.tensor_copy(src_f, src_g)
            pool.tensor_copy(typ_f, typ_g)
            link(pool.tensor_copy(dst_f, dst_g))
            pool.sem_inc(keys_ready, 1)
            pool.memset(acc[:, 0:2 * ACC - TEMP], 0.0).then_inc(acc_cleared, 1)
            wide = [P, 2, GROUP]
            pool.wait_ge(bases_ready, 1)
            bases = base_g.rearrange("p (b o) -> p b o", o=1).broadcast_to(wide)
            link(pool.tensor_tensor(key_f, dst_f, bases, ALU.subtract))
            link(pool.tensor_scalar(key_f, key_f, float(RELS), None, ALU.mult))
            link(pool.tensor_tensor(key_f, key_f, typ_f, ALU.add))
            pool.tensor_scalar(tmp_g, key_f, -0.5, None, ALU.is_lt)
            pool.tensor_scalar(out_g, key_f, WIN - 0.5, None, ALU.is_gt)
            link(pool.tensor_scalar(left_f, dst_f, float(RELS), None, ALU.mult))
            link(pool.tensor_tensor(tmp_g, tmp_g, out_g, ALU.add))
            link(pool.tensor_tensor(left_f, left_f, typ_f, ALU.add))
            link(pool.tensor_scalar(left_f, left_f, 1e6, None, ALU.add))
            link(pool.tensor_tensor(left_f, left_f, tmp_g, ALU.mult))
            link(pool.tensor_scalar(left_f, left_f, -1e6, None, ALU.add))
            pool.tensor_scalar(tmp_g, left_f, -0.5, None, ALU.is_gt)
            link(pool.tensor_scalar(out_g, left_f, N * RELS - 0.5, None, ALU.is_lt))
            link(pool.tensor_tensor(tmp_g, tmp_g, out_g, ALU.mult))
            pool.sem_inc(prep_inputs, 1)
            for to, ap in ((mw1, mix_w1.rearrange("(a p) n -> p a n", p=P)),
                           (rootw[:, :, 0:C], root_w.rearrange("(a p) n -> p a n", p=P)),
                           (relw[:, 0, :, 0:C], rel_w[:, 0:P, :].rearrange("r p n -> p r n")),
                           (relw[:, 1, :, 0:C], rel_w[:, P:C, :].rearrange("r p n -> p r n")),
                           (a_rep, att_w[0:1, 0:C].broadcast_to([P, C])),
                           (att2, att_w[0:1, C:2 * C].rearrange("o (a p) -> p (o a)", p=P)),
                           (biases[:, 0, 0:C], gnn_b.rearrange("(a n) -> a n", a=1).broadcast_to([PARTS, C])),
                           (biases[:, 1, 0:C], mix_b2.rearrange("(a n) -> a n", a=1).broadcast_to([PARTS, C])),
                           (biases[:, 2, 0:C], ffn_b2.rearrange("(a n) -> a n", a=1).broadcast_to([PARTS, C])),
                           (attb, att_b.rearrange("(a n) -> a n", a=1).broadcast_to([PARTS, 1])),
                           (wr_rep[:, :], wr.rearrange("c o -> o c").broadcast_to([P, C])),
                           (br_rep[:, :], br.rearrange("(a n) -> a n", a=1).broadcast_to([P, 1])),
                           (fb1[:, :], ffn_b1.rearrange("(c p) -> p c", p=P)),
                           (mb1, mix_b1.rearrange("(c p) -> p c", p=P)),
                           (grow, kln_g.rearrange("(a n) -> a n", a=1).broadcast_to([P, HEADC]))):
                pool.dma_start(to, ap, allow_slow_non_contiguous=True).then_inc(small_in, 16)
            for to, g in ((kg, kln_g), (kb, kln_b), (vg, vln_g), (vb, vln_b)):
                for h in range(4):
                    pool.dma_start(to[h * HEADC:(h + 1) * HEADC, :], g.rearrange("(n a) -> n a", a=1))\
                      .then_inc(small_in, 16)
            for h in range(HEADS):
                pool.dma_start(bq[(h % 4) * HEADC:(h % 4 + 1) * HEADC, h // 4:h // 4 + 1],
                             b_qkv[h * 3 * HEADC:h * 3 * HEADC + HEADC].rearrange("(n a) -> n a", a=1))\
                  .then_inc(small_in, 16)

            pool.memset(cnt[:, :], 0).then_inc(cnt_cleared, 1)

            pool.wait_ge(stored[0], STORED * 13)
            pool.wait_ge(stored[1], STORED * 12)
            pool.wait_ge(src_ready, 1)
            pool.wait_ge(any_ready, 1)

            def gather(into, idx):
                return pool.indirect_dma_start(into, None, table, bass.IndirectOffsetOnAxis(ap=idx, axis=0))

            left = pool.value_load(any_left[0:1, 0:1], min_val=0, max_val=1)
            with pool.If(left > 0):
                with pool.Fori(0, GROUPS) as g:
                    pool.sem_inc(pool_at_group, 1)
                    pool.wait_ge(general_turn, g + 1)
                    pool.tensor_copy(index[:, 0, 0:2], src_t[:, ds(g * 2, 2)]).then_inc(general_index, 1)
                    pool.wait_ge(general_index, g * 2 + 1)
                    pool.sem_inc(general_index, 1)
                    for k in range(2):
                        gather(rows[:, k, :], index[:, 0, k:k + 1]).then_inc(general_in, 16)
                    pool.wait_ge(general_in, g * 32 + 32)
                pool.wait_ge(general_added, GROUPS * GENERAL_WINDOWS + 1)

            def gather_round(a):
                for half in range(2):
                    pool.tensor_copy(index[:, half, :], src_t[:, span(a * (2 * SLOTS) + half * SLOTS, SLOTS)])\
                        .then_inc(index_ready, 1)
                    pool.wait_ge(index_ready, a * 2 + (half + 1))
                    for k in range(SLOTS):
                        pool.wait_ge(group_summed, a * (2 * SLOTS) + (half * SLOTS + k + 1))
                        wait_past(pool, slot_in[(k - 3) % SLOTS], a * 32 + 16 * (half + (k >= 3)))
                        pool.sem_inc(gathered, 1)
                        gather(rows[:, k, :], index[:, half, k:k + 1]).then_inc(slot_in[k], 16)

            gather_round(0)
            with pool.Fori(1, GATHERS // (2 * SLOTS)) as a:
                gather_round(a)
            for k in range(SLOTS - 3, SLOTS):
                pool.wait_ge(slot_in[k], GATHERS // SLOTS * 16)
                pool.sem_inc(gathered, 1)

            pool.wait_ge(base2_done, TILES)
            for k, i in enumerate(range(DVE_TILES, TILES)):
                pool.wait_ge(y_weighed, k + 1)
                y = acc[:TOK, i * KEYS:i * KEYS + C]
                pool.tensor_tensor(y, y, acc[:TOK, ACC + i * KEYS:ACC + i * KEYS + C], ALU.add).then_inc(added, 1)

        @block.scalar
        def _(act):
            link = Links(act, act_link)

            act.wait_ge(weights_in, 32)
            for a in range(2):
                last = act.activation(wq[:, a, :].rearrange("p (h j) -> p h j", h=HEADS),
                                      wqkv[:, a, :].rearrange("p (h t j) -> p h t j", h=HEADS, t=3)[:, :, 0, :], ACT.Copy)
            last.then_inc(wq_ready, 1)

            def norm_step(t):
                s = t.back(1)
                if t.exists():
                    act.wait_ge(rstd_done, t.i + 1)
                    wait_past(act, stored[t.b], t.u * STORED)
                    wait_past(act, turned, t.i - 1)
                    act.activation(xn[:TOK, t.b, :], x_in[:TOK, t.b, :], ACT.Identity, bias=stats[:TOK, t.b, 10:11],
                                   scale=stats[:TOK, t.b, 9:10]).then_inc(xn_done, 1)
                    act.wait_ge(xn_done, t.i + 1)
                    act.activation(tab[:TOK, t.b, 0:C], xn[:TOK, t.b, :], ACT.Copy).then_inc(hi_done, 1)
                    after_next = t.back(-2)
                    if not t.static or after_next.exists():
                        load_x(act, x_in[:, t.b, :], after_next, x_loaded[t.b])
                if s.exists():
                    act.wait_ge(kv_done, s.i + 1)
                    wait_past(act, var_done, s.i - 1)
                    act.activation(sq[:TOK, s.b, :], bank[2 + s.b][:TOK, :], ACT.Square).then_inc(squared, 1)
                if t.exists():
                    act.wait_ge(turned, t.i + 1)
                    wait_past(act, kv_done, t.i - 1)
                    act.activation(xt[:, t.b, :, :], bank[t.b][:, 0:2 * TOK].rearrange("p (h n) -> p h n", h=2),
                                   ACT.Copy).then_inc(xt_done, 1)
                    n = t.back(-1)
                    if not t.static or n.exists():
                        deviation(n)
                if s.exists():
                    act.wait_ge(var_done, s.i + 1)
                    act.activation(stats[:TOK, s.b, 32:48], stats[:TOK, s.b, 16:32], ACT.Sqrt, bias=eps_col[:TOK, :],
                                   scale=1.0 / HEADC).then_inc(kstd_done, 1)
                if t.static and t.offset == TURN_AT:
                    take_sources()

            def take_sources():
                act.wait_ge(prep_turned, 1)
                act.activation(src_t[:, :].rearrange("p (g s) -> p s g", s=2),
                               bank[5][:, 0:2 * GROUPS].rearrange("p (s g) -> p s g", s=2), ACT.Copy)\
                   .then_inc(src_ready, 1)
                act.wait_ge(prep_turned, 3)
                act.activation(base_row[:, :], bank[7][0:1, 0:2 * P], ACT.Copy, scale=float(RELS))
                act.activation(flag_row[:, :], bank[7][0:1, 2 * P:4 * P], ACT.Copy).then_inc(rows_ready, 1)

            def deviation(t):
                act.wait_ge(stats_done, t.i + 1)
                wait_past(act, rstd_done, t.i - 1)
                act.activation(stats[:TOK, t.b, 8:9], stats[:TOK, t.b, 7:8], ACT.Sqrt, bias=eps_col[:TOK, :])\
                   .then_inc(std_done, 1)

            act.wait_ge(eps_ready, 1)
            deviation(Tile(None, 0))
            steps(act, norm_step, 4, TILES + 1, ahead=2)

            def clear_tail(half):
                start = 2 * ACC - TEMP + half * TEMP // 2
                act.activation(acc[:, start:start + TEMP // 2], zero_col.broadcast_to([P, TEMP // 2]), ACT.Copy)\
                   .then_inc(tail_cleared, 1)

            act.wait_ge(vec_turned, 1)
            act.activation(vrow[0:2, :], bank[0][0:2, :], ACT.Copy).then_inc(vrow_ready, 1)
            act.wait_ge(wq_turned, 1)
            act.activation(wqT.rearrange("p a n -> p (a n)"), bank[1][:, :], ACT.Copy).then_inc(wqt_ready, 1)
            act.wait_ge(kv_summed, TILES + 1)
            act.wait_ge(stored[0], STORED * 13)
            act.wait_ge(stored[1], STORED * 12)
            act.wait_ge(prep_turned, 1)
            clear_tail(0)
            act.wait_ge(b1w_done, 1)
            act.activation(b1w.rearrange("p a n -> p (a n)"), bank[2][:, :], ACT.Copy, scale=1.0 / N)\
               .then_inc(b1w_ready, 1)
            clear_tail(1)

            act.wait_ge(weff_ready, 1)

            def mix_step(t):
                if t.exists():
                    act.wait_ge(h_done, t.i + 1)
                    wait_past(act, mix_done, t.i - 1)
                    for o in range(2):
                        last = act.activation(m_h[:, t.b, o, :], bank[2 + t.b][:, o * TOK:(o + 1) * TOK], ACT.Gelu,
                                              bias=beff[:, o:o + 1])
                    last.then_inc(gelu_done, 1)
                s = t.back(2)
                if s.exists():
                    act.wait_ge(mixed, s.i + 1)
                    act.dma_start(tile_of(s, base_d), m_out[:, s.b, :]).then_inc(mix_stored[s.b], 16)

            steps(act, mix_step, MIX_FIRST + 2, TILES + 2)

            def node_step(t):
                s, r = t.back(1), t.back(2)
                if r.exists():
                    act.wait_ge(turned2, r.i + 1)
                    wait_past(act, hid_done, r.i * 2)
                    act.activation(xt3, bank[3][:, 0:2 * TOK].rearrange("p (h n) -> p h n", h=2), ACT.Copy)\
                       .then_inc(xt3_done, 1)
                if s.exists():
                    act.wait_ge(inverse_ready, s.i + 1)
                    wait_past(act, inverse_spread, s.i)
                    for k in range(RELS):
                        last = act.activation(spread[:, k * TOK:(k + 1) * TOK], ident[:TOK, 0:TOK], ACT.Copy,
                                              scale=inverse[:, k:k + 1])
                    last.then_inc(spread_ready, 1)
                if r.exists():
                    for half in range(2):
                        act.wait_ge(hid_done, r.i * 2 + half + 1)
                        wait_past(act, y_done, r.i)
                        for c in range(4 * half, 4 * half + 4):
                            k = c - 4 * half
                            last = act.activation(hT[:, c, :], bank[4 + half][:, k * TOK:(k + 1) * TOK],
                                                  ACT.Gelu_apprx_tanh, bias=fb1[:, c:c + 1])
                        last.then_inc(gelu2_done, 1)
                if s.exists():
                    act.wait_ge(u_done, s.i + 1)
                    wait_past(act, x1_done, s.i)
                    act.activation(th[:TOK, :], bank[2][:TOK, 0:C], ACT.Tanh)
                    act.activation(ta[:TOK, :], bank[2][:TOK, C:C + 1], ACT.Tanh, scale=0.5).then_inc(tanh_done, 1)
                if t.exists():
                    if t.static and t.offset == 0:
                        act.wait_ge(rows_cleared, 1)
                    act.wait_ge(acc_added, t.i * NODE_GROUPS + MIX_GROUPS + NODE_GROUPS)
                    wait_past(act, count_turned, t.i)
                    for k in range(RELS):
                        row = 32 * k
                        last = act.activation(
                            count_rows[row:row + 1, :],
                            cnt[row:row + 1, span(t.i * KEYS, KEYS)].rearrange("p (n r) -> p n r", r=RELS)[:, :, k],
                            ACT.Relu, bias=minus_one[row:row + 1, :])
                    last.then_inc(count_ready, 1)
                if r.exists():
                    act.wait_ge(y_done, r.i + 1)
                    act.activation(acc[:TOK, span(r.i * KEYS, C)], bank[6][:TOK, 0:C], ACT.Copy).then_inc(y_kept, 1)
            steps(act, node_step, 4, TILES + 2)
            act.wait_ge(weights_chosen, 1)
            act.wait_ge(y_kept, TILES)
            for i in range(DVE_TILES, TILES):
                y = acc[:TOK, i * KEYS:i * KEYS + C]
                act.activation(y, y, ACT.Copy, scale=work[:TOK, i:i + 1]).then_inc(y_weighed, 1)

        @block.vector
        def _(dve):
            link = Links(dve, dve_link)
            dve.memset(eps_col, EPS).then_inc(eps_ready, 1)
            dve.memset(zero_col, 0.0)
            dve.memset(minus_one, -1.0)
            dve.memset(kvn[:, :, :, P:P + 1], 1.0)
            dve.memset(k_total[:TOK, :], 0.0).then_inc(kv_added, 1)
            dve.memset(xn[96:P, :, :], 0.0)
            link(dve.memset(vrow[0:1, :], 0.0))
            dve.wait_ge(weights_in, 32)
            kv_view = wqkv.rearrange("p a (h t j) -> p a h t j", h=HEADS, t=3)
            for a in range(2):
                for t in range(2):
                    dve.reduce_sum(means[:, 16 * a + 8 * t:16 * a + 8 * t + 8], kv_view[:, a, :, 1 + t, :], axis=AX.X)
            for t in range(2):
                last = dve.reduce_sum(means[0:PARTS, 32 + 8 * t:40 + 8 * t],
                                      bqkv[0:PARTS, :].rearrange("p (h t j) -> p h t j", h=HEADS, t=3)[:, :, 1 + t, :],
                                      axis=AX.X)
            link(last)
            link(dve.tensor_scalar(means[:, 0:32], means[:, 0:32], 1.0 / HEADC, None, ALU.mult))
            link(dve.tensor_scalar(means[0:PARTS, 32:48], means[0:PARTS, 32:48], 1.0 / HEADC, None, ALU.mult))
            for a in range(2):
                for t in range(2):
                    m = 16 * a + 8 * t
                    dve.tensor_tensor(wkv[:, a, C * t:C * t + C].rearrange("p (h j) -> p h j", h=HEADS),
                                      kv_view[:, a, :, 1 + t, :],
                                      means[:, m:m + 8].rearrange("p (h o) -> p h o", o=1).broadcast_to([P, HEADS, HEADC]),
                                      ALU.subtract)
            for t in range(2):
                m = 32 + 8 * t
                last = dve.tensor_tensor(
                    bkv[0:PARTS, C * t:C * t + C].rearrange("p (h j) -> p h j", h=HEADS),
                    bqkv[0:PARTS, :].rearrange("p (h t j) -> p h t j", h=HEADS, t=3)[:, :, 1 + t, :],
                    means[0:PARTS, m:m + 8].rearrange("p (h o) -> p h o", o=1).broadcast_to([PARTS, HEADS, HEADC]),
                    ALU.subtract)
            link(last)

            def split(parts, values, n, scratch):
                hi, lo, rest = (ap[:, 0:n] for ap in scratch)
                dve.memset(parts, 0.0)
                link(dve.tensor_copy(hi, values))
                dve.tensor_copy(parts[0:1, :], hi[0:1, :])
                link(dve.tensor_tensor(rest, values, hi, ALU.subtract))
                link(dve.tensor_copy(lo, rest))
                dve.tensor_copy(parts[32:33, :], lo[32:33, :])
                link(dve.tensor_tensor(rest, rest, lo, ALU.subtract))
                return dve.tensor_copy(parts[64:65, :], rest[64:65, :])

            split(kv_parts[:, :], bkv[0:PARTS, :], 2 * C, kv_split).then_inc(wkv_ready, 1)

            def norm_step(t):
                s = t.back(1)
                if t.exists():
                    n = t.back(-1)
                    if not t.static or n.exists():
                        take_stats(n)
                    if t.static and t.offset == 3:
                        group_bases()
                    if t.static and t.offset == TURN_AT:
                        dve.wait_ge(prep_inputs, 1)
                        dve.reduce_sum(flag_g, tmp_g, axis=AX.X).then_inc(flags_ready, 1)
                    dve.wait_ge(hi_done, t.i + 1)
                    dve.tensor_tensor(tab[:TOK, t.b, C:2 * C], xn[:TOK, t.b, :], tab[:TOK, t.b, 0:C], ALU.subtract)\
                       .then_inc(lo_done, 1)
                if s.exists():
                    dve.wait_ge(squared, s.i + 1)
                    dve.reduce_sum(stats[:TOK, s.b, 16:32], sq[:TOK, s.b, :].rearrange("p (g j) -> p g j", j=HEADC),
                                   axis=AX.X).then_inc(var_done, 1)
                n = t.back(-1)
                if t.exists() and (not t.static or n.exists()):
                    invert_deviation(n)
                r = t.back(2)
                if r.exists():
                    dve.wait_ge(kvn_done, r.i + 1)
                    dve.wait_ge(kv_added, r.i + 1)
                    total = k_total[:TOK, :].rearrange("p (k n) -> p k n", k=2)
                    dve.tensor_tensor(total, total, kvn[:TOK, r.b, 0:2, 0:P], ALU.add).then_inc(kv_added, 1)
                if s.exists():
                    dve.wait_ge(kstd_done, s.i + 1)
                    dve.reciprocal(stats[:TOK, s.b, 48:64], stats[:TOK, s.b, 32:48]).then_inc(kstd_link, 1)
                    dve.wait_ge(kstd_link, s.i + 1)
                    wait_past(dve, kv_summed, s.i - 1)
                    wait_past(dve, kv_added, s.i)
                    dve.tensor_tensor(kvn[:TOK, s.b, :, 0:P].rearrange("p k (g j) -> p k g j", j=HEADC),
                                      bank[2 + s.b][:TOK, :].rearrange("p (k g j) -> p k g j", k=4, j=HEADC),
                                      stats[:TOK, s.b, 48:64].rearrange("p (k g o) -> p k g o", k=4, o=1)
                                      .broadcast_to([TOK, 4, 4, HEADC]), ALU.mult).then_inc(kvn_done, 1)
                if t.static and t.offset == TURN_AT + 1:
                    take_keys()
                if t.static and t.offset == TILES - 1:
                    take_left()

            def invert_deviation(t):
                dve.wait_ge(std_done, t.i + 1)
                wait_past(dve, xn_done, t.i - 1)
                dve.reciprocal(stats[:TOK, t.b, 9:10], stats[:TOK, t.b, 8:9]).then_inc(rstd_link, 1)
                dve.wait_ge(rstd_link, t.i + 1)
                dve.tensor_scalar(stats[:TOK, t.b, 10:11], stats[:TOK, t.b, 6:7], stats[:TOK, t.b, 9:10], -1.0,
                                  ALU.mult, ALU.mult).then_inc(rstd_done, 1)

            def take_stats(t):
                dve.wait_ge(x_loaded[t.b], t.u * 16 + 16)
                wait_past(dve, rstd_done, t.i - 1)
                dve.bn_stats(stats[:TOK, t.b, 0:6], x_in[:TOK, t.b, :]).then_inc(stats_link, 1)
                dve.wait_ge(stats_link, t.i + 1)
                dve.sem_inc(stats_order, 1)
                dve.bn_aggr(stats[:TOK, t.b, 6:8], stats[:TOK, t.b, 0:6]).then_inc(stats_done, 1)

            def take_keys():
                dve.wait_ge(prep_turned, 2)
                dve.tensor_copy(key_t[:, :, :], bank[6][:, 0:2 * GROUPS].rearrange("p (s g) -> p s g", s=2))\
                   .then_inc(keys_in_place, 1)
                dve.wait_ge(rows_ready, 1)
                link(dve.reduce_sum(any_f, flag_row[0:1, 0:GROUPS], axis=AX.X))
                link(dve.tensor_scalar(any_f, any_f, 0.5, None, ALU.is_gt))
                dve.tensor_copy(any_left[:, :], any_f)

            def take_left():
                dve.wait_ge(prep_turned, 4)
                link(dve.tensor_copy(left_t, bank[5][:, 0:2 * GROUPS].rearrange("p (s g) -> p s g", s=2)))
                dve.sem_inc(any_ready, 1)

            def group_bases():
                dve.wait_ge(keys_ready, 1)
                dve.tensor_reduce(min_g, dst_f, axis=AX.X, op=ALU.min)
                link(dve.reduce_sum(done_g, cmp_g, axis=AX.X))
                link(dve.tensor_scalar(done_g, done_g, float(TOK), None, ALU.mult))
                dve.tensor_tensor(base_g, min_g, done_g, ALU.max).then_inc(bases_ready, 1)

            def gate_columns():
                link(dve.memset(biases[:, :, C:C + 1], 0.0))
                sums = [(relw[:, h, r, 0:C], relw[:, h, r, C:C + 1], P) for h in range(2) for r in range(RELS)]
                sums += [(rootw[:, h, 0:C], small[:, 4 + h:5 + h], P) for h in range(2)]
                sums += [(biases[:, 0, 0:C], small[0:PARTS, 6:7], PARTS)]
                for k, (weight, total, n) in enumerate(sums):
                    last = dve.tensor_tensor_reduce(out=gate_junk[0:n, k % 5, :], in0=weight, in1=a_rep[0:n, :],
                                                    scale=1.0, scalar=0.0, op0=ALU.mult, op1=ALU.add, accum_out=total)
                    if k % 5 == 4:
                        link(last)
                link(last)
                dve.tensor_tensor(rootw[:, :, C], small[:, 4:6], att2, ALU.add)
                link(dve.tensor_tensor(biases[:, 0, C:C + 1], small[0:PARTS, 6:7], attb, ALU.add))

            take_stats(Tile(None, 0))
            invert_deviation(Tile(None, 0))
            steps(dve, norm_step, 4, TILES + 2, ahead=2)


            dve.wait_ge(small_in, 16 * 39)
            dve.wait_ge(kv_summed, TILES + 1)
            for a in range(2):
                v = 4 * a
                dve.tensor_copy(vec[:, v:v + 1], vb)
                dve.tensor_tensor(vec[:, v + 1:v + 2], bank[4][:, a * (P + 1) + P:(a + 1) * (P + 1)], vg, ALU.mult)
                dve.tensor_tensor(small[:, a:a + 1], bank[4][:, 258 + a:259 + a], kg, ALU.mult)
                last = dve.tensor_copy(vec[:, v + 3:v + 4], kb)
            link(last)
            for a in range(2):
                last = dve.scalar_tensor_tensor(vec[:, 4 * a + 2:4 * a + 3], kb, float(N), small[:, a:a + 1],
                                                ALU.mult, ALU.add)
            last.then_inc(vec_ready, 1)
            link(dve.memset(kv_t, 0.0))

            dve.wait_ge(outer_done, 1)
            for a in range(2):
                for h in range(4):
                    lo, hi = h * HEADC, (h + 1) * HEADC
                    last = dve.scalar_tensor_tensor(kv_t[lo:hi, a, lo:hi], bank[4][lo:hi, a * (P + 1) + lo:a * (P + 1) + hi],
                                                    vg[lo:hi, :], grow[lo:hi, :], ALU.mult, ALU.mult)
            link(last)
            for a in range(2):
                for h in range(4):
                    lo, hi = h * HEADC, (h + 1) * HEADC
                    last = dve.tensor_tensor(kv_t[lo:hi, a, lo:hi], bank[3][lo:hi, a * P + lo:a * P + hi],
                                             kv_t[lo:hi, a, lo:hi], ALU.add)
            last.then_inc(kvt_ready, 1)
            gate_columns()
            link(split(bias_parts[:, 1, :], biases[:, 1, :], C + 1, bias_split))

            dve.wait_ge(weff_done, 2)
            for a in range(2):
                dve.tensor_tensor(weff[:, a, :], bank[1][:, a * C:a * C + C], mw1[:, a, :], ALU.add)
            dve.tensor_tensor(beff[:, :], bank[3][:, 400:402], mb1, ALU.add).then_inc(weff_ready, 1)

            dve.wait_ge(acc_cleared, 1)
            dve.wait_ge(cnt_cleared, 1)
            dve.wait_ge(tail_cleared, 2)

            left = dve.value_load(any_left[0:1, 0:1], min_val=0, max_val=1)
            with dve.If(left > 0):
                dve.sem_inc(general_added, 1)
                with dve.Fori(0, GROUPS) as g:
                    dve.wait_ge(pool_at_group, g + 1)
                    dve.wait_ge(pe_at_group, g + 1)
                    dve.sem_inc(general_turn, 1)
                    flagged = dve.value_load(flag_row[0:1, ds(g, 1)], min_val=0, max_val=GROUP)
                    with dve.If(flagged > 0):
                        with dve.Fori(0, GENERAL_WINDOWS) as w:
                            with dve.If(w < 1):
                                dve.tensor_copy(left_rel, left_t[:, :, ds(g, 1)].rearrange("p s o -> p (s o)"))\
                                   .then_inc(general_link, 1)
                            with dve.Else():
                                dve.tensor_scalar(left_rel, left_rel, -float(WIN), None, ALU.add).then_inc(general_link, 1)
                            dve.wait_ge(general_link, g * GENERAL_WINDOWS + w + 1)
                            for k in range(2):
                                last = dve.tensor_scalar(onehot[:, k, :], keyrow[:, :], left_rel[:, k:k + 1], None,
                                                         ALU.is_equal)
                            last.then_inc(general_hot, 1)
                            dve.wait_ge(general_sum, g * GENERAL_WINDOWS + w + 1)
                            dve.wait_ge(general_added, g * GENERAL_WINDOWS + w + 1)
                            dve.tensor_tensor(acc3[:, :, ds(w * WIN, WIN)],
                                              bank[0][:, 0:2 * WIN].rearrange("p (h k) -> p h k", h=2),
                                              acc3[:, :, ds(w * WIN, WIN)], ALU.add)
                            dve.tensor_tensor(cnt[:, ds(w * WIN, WIN)], bank[0][:, 2 * WIN:3 * WIN],
                                              cnt[:, ds(w * WIN, WIN)], ALU.add).then_inc(general_added, 1)
                    with dve.Else():
                        dve.sem_inc(general_link, GENERAL_WINDOWS)
                        dve.sem_inc(general_hot, GENERAL_WINDOWS)
                        dve.sem_inc(general_added, GENERAL_WINDOWS)
                dve.wait_ge(general_added, GROUPS * GENERAL_WINDOWS + 1)

            link(dve.memset(m_out[96:P, :, :], 0.0))
            def hot(g, slots):
                for k in range(2):
                    dve.wait_ge(group_summed, g * 2 + k + 1)
                    dve.tensor_scalar(onehot[:, span(slots[k], 1), :].rearrange("p o n -> p (o n)"), keyrow[:, :],
                                      key_t[:, k, span(g, 1)], None, ALU.is_equal).then_inc(hot_done, 1)

            def first_columns(g, n):
                _, cols = nc.values_load_multi_w_load_instructions(
                    base_row[0:1, span(g, n)], engines=[mybir.EngineType.DVE], min_val=0, max_val=ACC - WIN,
                    skip_runtime_bounds_check_because="a node's number times four")
                return cols

            def add(g, b, col):
                dve.wait_ge(group_summed, g * 2 + 2 + SLOTS)
                wait_past(dve, acc_added, g)
                dve.tensor_tensor(acc3[:, :, ds(col, WIN)], bank[b][:, 0:2 * WIN].rearrange("p (h k) -> p h k", h=2),
                                  acc3[:, :, ds(col, WIN)], ALU.add)
                dve.tensor_tensor(cnt[:, ds(col, WIN)], bank[b][:, 2 * WIN:3 * WIN], cnt[:, ds(col, WIN)], ALU.add)\
                   .then_inc(acc_added, 1)

            def mix_step(t):
                s = t.back(1)
                if s.exists():
                    dve.wait_ge(mix_rows_in[s.b], s.u * 32 + 32)
                    wait_past(dve, mix_stored[s.b], s.u * 16)
                    dve.scalar_tensor_tensor(m_out[:TOK, s.b, :], m_xn[:TOK, s.b, :], 2.0, m_x[:TOK, s.b, :],
                                             ALU.mult, ALU.add).then_inc(base_done, 1)
                    dve.wait_ge(base_done, s.i + 1)
                    dve.wait_ge(mix_done, s.i + 1)
                    dve.tensor_tensor(m_out[:TOK, s.b, :], bank[6 + s.b][:TOK, 0:C], m_out[:TOK, s.b, :], ALU.add)\
                       .then_inc(mixed, 1)
                if t.static and t.offset in (1, 2):
                    k = (0, 2)[t.offset - 1]
                    link(split(bias_parts[:, k, :], biases[:, k, :], C + 1, bias_split))
                    dve.sem_inc(gnn_w_ready, 1)
                g = t.i - MIX_FIRST
                if not t.static or 0 <= g < MIX_GROUPS:
                    hot(g + 2, [slot_of(g + 2, 0), slot_of(g + 2, 1)])
                    add(g, (t.b + MIX_FIRST) % 2, first_columns(g, 1)[0])

            dve.wait_ge(keys_in_place, 1)
            hot(0, [0, 1])
            hot(1, [2, 3])
            steps(dve, mix_step, MIX_FIRST + 2, TILES + 1)

            dve.memset(count_rows[:, :], 0.0).then_inc(rows_cleared, 1)
            def invert_counts(t):
                dve.wait_ge(count_turned, t.i + 1)
                if t.static and t.offset == 0:
                    dve.wait_ge(mix_done, TILES)
                dve.tensor_scalar(inverse, bank[7][:TOK, 0:32 * RELS].rearrange("p (r k) -> p r k", k=32)[:, :, 0], 1.0,
                                  None, ALU.add).then_inc(invert_link, 1)
                dve.wait_ge(invert_link, t.i + 1)
                dve.reciprocal(inverse, inverse).then_inc(inverse_ready, 1)

            def scale_sums(t):
                dve.wait_ge(inverse_spread, t.i + 1)
                wait_past(dve, u_done, t.i)
                for h in range(2):
                    last = dve.tensor_tensor(sn[:, h, :, :],
                                             acc3[:, h, span(t.i * KEYS, KEYS)].rearrange("p (n r) -> p r n", r=RELS),
                                             bank[7][:, 0:KEYS].rearrange("p (r n) -> p r n", r=RELS), ALU.mult)
                last.then_inc(scaled, 1)

            NODE_LINKS = 13
            v, half, y, e, y_step = (nw[:TOK, k:k + 1] for k in (0, 1, 6, 2, 3))

            def blend(t, node):
                dve.wait_ge(tanh_done, t.i + 1)
                dve.wait_ge(n_rows_in, t.i * 32 + 32)
                wait_past(dve, xn2_done, t.i)
                dve.tensor_tensor(th[:TOK, :], th[:TOK, :], n_xn[:TOK, :], ALU.subtract)
                node(dve.tensor_scalar(ga[:TOK, :], ta[:TOK, :], 0.5, 0.5, ALU.mult, ALU.add))
                node(dve.scalar_tensor_tensor(x1[:TOK, :], th[:TOK, :], ga[:TOK, :], n_base[:TOK, :], ALU.mult, ALU.add))

            def take_second_stats(node):
                node(dve.bn_stats(st2[:TOK, :], x1[:TOK, :]))
                dve.sem_inc(x1_done, 1)
                node(dve.bn_aggr(mv2[:TOK, :], st2[:TOK, :]))

            def estimate(t, node):
                node(dve.tensor_scalar(v, mv2[:TOK, 1:2], EPS, None, ALU.add))
                dve.tensor_scalar(e, v, -0.5, None, ALU.mult)
                node(dve.tensor_scalar(half.bitcast(i32), v.bitcast(i32), 1, None, ALU.logical_shift_right))
                node(dve.tensor_scalar(y.bitcast(i32), half.bitcast(i32), -1.0, float(0x5f3759df), ALU.mult, ALU.add))

            def newton(node):
                node(dve.scalar_tensor_tensor(y_step, y, e, y, ALU.mult, ALU.mult))
                node(dve.scalar_tensor_tensor(y, y_step, 1.5, y, ALU.add, ALU.mult))

            def newton_end(t, node):
                newton(node)
                assert node.n == NODE_LINKS, node.n
                wait_past(dve, turned2, t.i)
                wait_past(dve, base2_done, t.i)
                dve.tensor_scalar(xn2[:TOK, :], x1[:TOK, :], mv2[:TOK, 0:1], y, ALU.subtract, ALU.mult)\
                   .then_inc(xn2_done, 1)

            def route(t):
                dve.wait_ge(xn2_done, t.i + 1)
                dve.tensor_tensor_reduce(out=junk[:TOK, :], in0=xn2[:TOK, :], in1=wr_rep[:TOK, :], scale=1.0, scalar=0.0,
                                         op0=ALU.mult, op1=ALU.add, accum_out=wcol[:TOK, :]).then_inc(route_link, 1)
                dve.wait_ge(route_link, t.i + 1)
                dve.tensor_copy(w_all[:TOK, span(t.i, 1)], wcol[:TOK, :])
                dve.tensor_tensor(acc[:TOK, span(t.i * KEYS + ACC, C)], x1[:TOK, :], xn2[:TOK, :], ALU.add)\
                   .then_inc(base2_done, 1)

            def node_step(t):
                s, r = t.back(1), t.back(2)
                node = Links(dve, node_link)
                node.at(s.i * NODE_LINKS)
                if t.exists():
                    cols = first_columns(t.i * NODE_GROUPS + MIX_GROUPS, NODE_GROUPS)
                for q in range(NODE_GROUPS):
                    if t.exists():
                        g = t.i * NODE_GROUPS + (MIX_GROUPS + q)
                        if not (t.static and g + 2 >= GROUPS):
                            hot(g + 2, [(2 * (MIX_GROUPS + t.b * NODE_GROUPS + q + 2) + k) % SLOTS for k in range(2)])
                        add(g, (MIX_GROUPS + t.b * NODE_GROUPS + q) % 2, cols[q])
                    if q == 1 and s.exists():
                        scale_sums(s)
                    if q == 2 and r.exists():
                        route(r)
                    if q == 5 and s.exists():
                        blend(s, node)
                if s.exists():
                    take_second_stats(node)
                if s.exists():
                    estimate(s, node)
                    newton(node)
                    newton(node)
                    newton_end(s, node)
                if t.exists():
                    invert_counts(t)

            steps(dve, node_step, 4, TILES + 2)

            dve.wait_ge(base2_done, TILES)
            pick = Links(dve, select_link)
            T, S = TOK, TILES

            def field(at, n):
                return work[:T, at:at + n]

            w, sign, hi_i, lo_i, hi, lo = (field(32 * k, S) for k in range(6))
            dve.wait_ge(turned2, TILES)
            pick(dve.tensor_scalar(w, w_all[:T, :], br_rep[:T, :], None, ALU.add))
            pick(dve.tensor_scalar(sign.bitcast(i32), w.bitcast(i32), 31, 0x7fffffff, ALU.arith_shift_right,
                                   ALU.bitwise_and))
            pick(dve.tensor_tensor(sign.bitcast(i32), sign.bitcast(i32), w.bitcast(i32), ALU.bitwise_xor))
            dve.tensor_scalar(hi_i.bitcast(i32), sign.bitcast(i32), 16, None, ALU.arith_shift_right)
            pick(dve.tensor_scalar(lo_i.bitcast(i32), sign.bitcast(i32), 0xffff, None, ALU.bitwise_and))
            dve.tensor_scalar(hi, hi_i.bitcast(i32), 32768.0, None, ALU.add)
            pick(dve.tensor_copy(lo, lo_i.bitcast(i32)))
            digits = keyrow[:T, 1:16]
            bases, found, thresholds = (field(240, 1), field(242, 1)), field(241, 1), field(248, 15)
            per_row, hits = field(264, 15), field(280, 15)
            steps_row = field(1100, 60).rearrange("p (d o) -> p d o", d=4)
            cmp = work[:T, 300:300 + 15 * S].rearrange("p (d s) -> p d s", d=15)
            low = field(700, S)
            for d in range(4):
                last = dve.tensor_scalar(steps_row[:, d, :], digits, 16.0 ** (3 - d), None, ALU.mult)
            pick(last)

            def kth_largest(keys, rounds_before):
                cur, new = bases
                dve.memset(cur, 0.0)
                pick(dve.memset(found, 0.0))
                for d in range(4):
                    dve.scalar_tensor_tensor(thresholds, steps_row[:, d, :], found, cur.broadcast_to([T, 15]),
                                             ALU.add, ALU.add)
                    pick(dve.tensor_tensor(new, cur, found, ALU.add))
                    cur, new = new, cur
                    pick(dve.tensor_tensor(cmp, keys.rearrange("p (o s) -> p o s", o=1).broadcast_to([T, 15, S]),
                                           thresholds.rearrange("p (d o) -> p d o", o=1).broadcast_to([T, 15, S]),
                                           ALU.is_ge))
                    dve.reduce_sum(per_row, cmp, axis=AX.X).then_inc(counts_ready, 1)
                    dve.wait_ge(counts_summed, d + (rounds_before + 1))
                    pick(dve.tensor_scalar(hits, bank[0][:T, 0:15], KEPT - 0.5, 16.0 ** (3 - d), ALU.is_gt, ALU.mult))
                    pick(dve.reduce_sum(found, hits, axis=AX.X))
                pick(dve.tensor_tensor(new, cur, found, ALU.add))
                return new

            cur = kth_largest(hi, 0)
            t0, t1 = field(730, S), field(760, S)
            dve.tensor_scalar(t0, hi, cur, 65537.0, ALU.is_gt, ALU.mult)
            pick(dve.tensor_scalar(t1, hi, cur, None, ALU.is_equal))
            pick(dve.scalar_tensor_tensor(low, lo, 1.0, t1, ALU.add, ALU.mult))
            pick(dve.tensor_tensor(low, low, t0, ALU.add))
            pick(dve.tensor_scalar(low, low, -1.0, None, ALU.add))
            cur = kth_largest(low, 4)
            greater, equal = field(790, S), field(820, S + 1)
            dve.tensor_scalar(greater, low, cur, None, ALU.is_gt)
            pick(dve.tensor_scalar(equal[:, 0:S], low, cur, None, ALU.is_equal))
            dve.reduce_sum(equal[:, S:S + 1], greater, axis=AX.X).then_inc(counts_ready, 1)
            dve.wait_ge(counts_summed, 9)
            sums = [work[:T, 860 + 64 * k:860 + 64 * k + 64] for k in range(2)]
            for s_ in sums:
                dve.memset(s_[:, 0:32], 0.0)
            pick(dve.tensor_copy(sums[0][:, 32:32 + S + 1], bank[0][:T, 0:S + 1]))
            a, b = sums
            shift = 1
            while shift < S:
                pick(dve.tensor_tensor(b[:, 32:32 + S], a[:, 32:32 + S], a[:, 32 - shift:32 - shift + S], ALU.add))
                a, b = b, a
                shift *= 2
            before, room = field(1000, S), field(1030, 1)
            pick(dve.tensor_tensor(before, bank[1][:T, 0:S], a[:, 31:31 + S], ALU.add))
            pick(dve.tensor_scalar(room, sums[0][:, 32 + S:33 + S], -1.0, float(KEPT), ALU.mult, ALU.add))
            pick(dve.tensor_scalar(before, before, room, None, ALU.is_lt))
            pick(dve.tensor_tensor(before, before, equal[:, 0:S], ALU.mult))
            pick(dve.tensor_tensor(before, before, greater, ALU.add))
            pick(dve.tensor_tensor(w, w, before, ALU.mult))
            dve.sem_inc(weights_chosen, 1)
            dve.wait_ge(y_kept, TILES)
            for i in range(DVE_TILES):
                y = acc[:T, i * KEYS:i * KEYS + C]
                dve.scalar_tensor_tensor(y, y, w[:, i:i + 1], acc[:T, ACC + i * KEYS:ACC + i * KEYS + C], ALU.mult,
                                         ALU.add).then_inc(chosen, 1)

        @block.tensor
        def _(pe):
            pe.sem_inc(group_summed, SLOTS)
            pe.wait_ge(wkv_ready, 1)
            pe.wait_ge(pool_consts, 1)
            pe.matmul(bank[4][:, 0:260], vrow[0:1, 0:P], vrow[0:1, 0:260], start=True, stop=False, skip_group_check=True)

            def turn(to, rows_ap, n_rows, **flags):
                return pe.transpose(to, rows_ap, ident[:n_rows, :n_rows])

            def norm_step(t):
                s, r = t.back(1), t.back(2)
                if s.exists():
                    pe.wait_ge(xt_done, s.i + 1)
                    wait_past(pe, kvn_done, s.i - 1)
                    pe.matmul(bank[2 + s.b][:TOK, :], onesb[:, 0:TOK], kv_parts[:, :], start=True, stop=False)
                    for h in range(2):
                        last = pe.matmul(bank[2 + s.b][:TOK, :], xt[:, s.b, h, :], wkv[:, h, :], start=False, stop=h == 1)
                    last.then_inc(kv_done, 1)
                if t.exists():
                    pe.wait_ge(xn_done, t.i + 1)
                    wait_past(pe, xt_done, t.i - 1)
                    for h in range(2):
                        last = turn(bank[t.b][:, h * TOK:(h + 1) * TOK], xn[:TOK, t.b, h * P:(h + 1) * P], TOK)
                    last.then_inc(turned, 1)
                if r.exists():
                    pe.wait_ge(kvn_done, r.i + 1)
                    for a in range(2):
                        k, v = kvn[:TOK, r.b, a, :], kvn[:TOK, r.b, 2 + a, 0:P]
                        last = pe.matmul(bank[4][:, a * (P + 1):(a + 1) * (P + 1)], v, k, start=False, stop=False,
                                         skip_group_check=True)
                    last.then_inc(kv_summed, 1)
                if t.static and t.offset == TURN_AT:
                    turn_keys()
                if t.static and t.offset == TILES - 1:
                    pe.wait_ge(src_ready, 1)
                    turn_edges(5, left_f).then_inc(prep_turned, 1)

            def turn_edges(b, ap):
                for blk, n in ((0, P), (1, GROUPS - P)):
                    for k in range(2):
                        last = turn(bank[b][:, k * GROUPS + blk * P:k * GROUPS + blk * P + n],
                                    ap[:n, blk, k * P:(k + 1) * P], n)
                return last

            def turn_keys():
                pe.wait_ge(keys_ready, 1)
                turn_edges(5, src_f).then_inc(prep_turned, 1)
                pe.wait_ge(prep_inputs, 1)
                turn_edges(6, key_f).then_inc(prep_turned, 1)
                pe.wait_ge(flags_ready, 1)
                for k, ap in enumerate((base_g[:, 0:1], base_g[:, 1:2], flag_g[:, 0:1], flag_g[:, 1:2])):
                    last = turn(bank[7][0:1, k * P:(k + 1) * P], ap, P)
                last.then_inc(prep_turned, 1)

            steps(pe, norm_step, 4, TILES + 2, ahead=2)
            pe.wait_ge(kv_added, TILES + 1)
            for a in range(2):
                last = pe.matmul(bank[4][:, 258 + a:259 + a], k_total[:TOK, a * P:(a + 1) * P], onesf[:TOK, 0:1],
                                 start=False, stop=True, skip_group_check=True)
            last.then_inc(kv_summed, 1)

            pe.wait_ge(vec_ready, 1)
            for k in range(4):
                last = turn(bank[0][0:2, k * P:(k + 1) * P], vec[:, 2 * k:2 * k + 2], P)
            last.then_inc(vec_turned, 1)
            pe.wait_ge(wq_ready, 1)
            for a in range(2):
                for h in range(2):
                    last = turn(bank[1][:, a * C + h * P:a * C + (h + 1) * P], wq[:, h, a * P:(a + 1) * P], P)
            last.then_inc(wq_turned, 1)
            pe.wait_ge(vrow_ready, 1)
            for a in range(2):
                last = pe.matmul(bank[3][:, a * P:(a + 1) * P], vrow[0:2, 2 * a * P:(2 * a + 1) * P],
                                 vrow[0:2, (2 * a + 1) * P:(2 * a + 2) * P], start=True, stop=True)
            last.then_inc(outer_done, 1)
            pe.wait_ge(kvt_ready, 1)
            for a in range(2):
                last = pe.matmul(bank[2][:, a * C:(a + 1) * C], kv_t[:, a, :], mw1[:, a, :], start=True, stop=True)
            last.then_inc(b1w_done, 1)
            pe.wait_ge(b1w_ready, 1)
            pe.wait_ge(wqt_ready, 1)
            for h in range(2):
                for a in range(2):
                    last = pe.matmul(bank[1][:, h * C:(h + 1) * C], wqT[:, a, h * P:(h + 1) * P], b1w[:, a, :],
                                     start=a == 0, stop=a == 1)
            last.then_inc(weff_done, 1)
            for o in range(2):
                for a in range(2):
                    last = pe.matmul(bank[3][:, 400 + o:401 + o], b1w[:, a, o * P:(o + 1) * P], bq[:, a:a + 1], start=a == 0,
                              stop=a == 1)
            last.then_inc(weff_done, 1)

            def sum_group(b, slots, last_inc):
                rows_k = [rows[:, span(s_, 1), :].rearrange("p o n -> p (o n)") for s_ in slots]
                hot_k = [onehot[:, span(s_, 1), :].rearrange("p o n -> p (o n)") for s_ in slots]
                for h in range(2):
                    for k in range(2):
                        for part in range(2):
                            pe.matmul(bank[b][:, h * WIN:(h + 1) * WIN],
                                      rows_k[k][:, part * C + h * P:part * C + (h + 1) * P], hot_k[k],
                                      start=k == 0 and part == 0, stop=k == 1 and part == 1)
                for k in range(2):
                    last = pe.matmul(bank[b][:, 2 * WIN:3 * WIN], onesh[:, :], hot_k[k], start=k == 0, stop=k == 1)
                last_inc(last)

            pe.wait_ge(any_ready, 1)
            pe.wait_ge(vrow_ready, 1)
            left = pe.value_load(any_left[0:1, 0:1], min_val=0, max_val=1)
            with pe.If(left > 0):
                with pe.Fori(0, GROUPS) as g:
                    pe.sem_inc(pe_at_group, 1)
                    pe.wait_ge(general_turn, g + 1)
                    flagged = pe.value_load(flag_row[0:1, ds(g, 1)], min_val=0, max_val=GROUP)
                    with pe.If(flagged > 0):
                        with pe.Fori(0, GENERAL_WINDOWS) as w:
                            pe.wait_ge(general_in, g * 32 + 32)
                            pe.wait_ge(general_hot, g * GENERAL_WINDOWS + w + 1)
                            pe.wait_ge(general_added, g * GENERAL_WINDOWS + w + 1)
                            sum_group(0, [0, 1], lambda ins: ins.then_inc(general_sum, 1))
                    with pe.Else():
                        pe.sem_inc(general_sum, GENERAL_WINDOWS)

            def agg(g, b, slots):
                pe.wait_ge(gathered, g * 2 + 5)
                pe.wait_ge(hot_done, g * 2 + 2)
                wait_past(pe, acc_added, g - 1)
                sum_group(b, slots, lambda ins: ins.then_inc(group_summed, 2))

            pe.wait_ge(weff_ready, 1)
            pe.wait_ge(mix_w_in, 16)

            def mix_step(t):
                s = t.back(1)
                if t.exists():
                    pe.wait_ge(mix_xt_in[t.b], t.u * 16 + 16)
                    wait_past(pe, gelu_done, t.i - 1)
                    for o in range(2):
                        for h in range(2):
                            last = pe.matmul(bank[2 + t.b][:, o * TOK:(o + 1) * TOK], weff[:, h, o * P:(o + 1) * P],
                                             m_xt[:, t.b, h, :], start=h == 0, stop=h == 1)
                    last.then_inc(h_done, 1)
                g = t.i - MIX_FIRST
                if not t.static or 0 <= g < MIX_GROUPS:
                    agg(g, (t.b + MIX_FIRST) % 2, [slot_of(g, 0), slot_of(g, 1)])
                if s.exists():
                    pe.wait_ge(gelu_done, s.i + 1)
                    wait_past(pe, mixed, s.i - 1)
                    pe.matmul(bank[6 + s.b][:TOK, 0:C], onesb[:, 0:TOK], bias_parts[:, 1, 0:C], start=True, stop=False)
                    for o in range(2):
                        last = pe.matmul(bank[6 + s.b][:TOK, 0:C], m_h[:, s.b, o, :], mw2[:, o, :], start=False,
                                         stop=o == 1)
                    last.then_inc(mix_done, 1)

            steps(pe, mix_step, MIX_FIRST + 2, TILES + 1)

            pe.wait_ge(gelu_done, TILES)
            pe.wait_ge(mixed, TILES)
            pe.wait_ge(gnn_w_ready, 2)
            pe.wait_ge(ffn_w_in, 32)

            u = bank[2][:TOK, 0:C + 1]

            def own_part(t):
                pe.wait_ge(n_xt_in, t.i * 16 + 16)
                wait_past(pe, tanh_done, t.i)
                pe.matmul(u, onesb[:, 0:TOK], bias_parts[:, 0, :], start=True, stop=False)
                for h in range(2):
                    pe.matmul(u, n_xt[:, h, :], rootw[:, h, :], start=False, stop=False)

            def relations_part(t, h):
                pe.wait_ge(scaled, t.i + 1)
                for r in range(RELS):
                    last = pe.matmul(u, sn[:, h, r, :], relw[:, h, r, :], start=False, stop=h == 1 and r == RELS - 1)
                if h == 1:
                    last.then_inc(u_done, 1)

            def turn_normed(t):
                pe.wait_ge(xn2_done, t.i + 1)
                wait_past(pe, xt3_done, t.i)
                for h in range(2):
                    last = turn(bank[3][:, h * TOK:(h + 1) * TOK], xn2[:TOK, h * P:(h + 1) * P], TOK)
                last.then_inc(turned2, 1)

            def ffn_up(t, half):
                if half == 0:
                    pe.wait_ge(xt3_done, t.i + 1)
                wait_past(pe, gelu2_done, t.i * 2 + half - 1)
                for k in range(4):
                    c = 4 * half + k
                    for h in range(2):
                        last = pe.matmul(bank[4 + half][:, k * TOK:(k + 1) * TOK], w1[:, h, c * P:(c + 1) * P],
                                         xt3[:, h, :], start=h == 0, stop=h == 1)
                last.then_inc(hid_done, 1)

            def ffn_down(t):
                wait_past(pe, y_kept, t.i)
                y = bank[6][:TOK, 0:C]
                pe.matmul(y, onesb[:, 0:TOK], bias_parts[:, 2, 0:C], start=True, stop=False)
                for c in range(HCHUNKS):
                    if c % 4 == 0:
                        pe.wait_ge(gelu2_done, t.i * 2 + c // 4 + 1)
                    last = pe.matmul(y, hT[:, c, :], w2[:, c, :], start=False, stop=c == HCHUNKS - 1)
                last.then_inc(y_done, 1)

            def node_step(t):
                s, r = t.back(1), t.back(2)

                def agg_at(q):
                    if t.exists():
                        agg(t.i * NODE_GROUPS + (MIX_GROUPS + q), (MIX_GROUPS + t.b * NODE_GROUPS + q) % 2,
                            [(2 * (MIX_GROUPS + q) + k) % SLOTS for k in range(2)])

                agg_at(0)
                if s.exists():
                    own_part(s)
                    pe.wait_ge(count_ready, s.i + 1)
                    turn(bank[7][:TOK, 0:97], count_rows[:, :], 97).then_inc(count_turned, 1)
                agg_at(1)
                if r.exists():
                    turn_normed(r)
                if r.exists():
                    ffn_up(r, 0)
                if s.exists():
                    pe.wait_ge(spread_ready, s.i + 1)
                    pe.matmul(bank[7][:, 0:KEYS], onesf[:TOK, :], spread, start=True, stop=True)\
                      .then_inc(inverse_spread, 1)
                agg_at(2)
                if r.exists():
                    ffn_up(r, 1)
                agg_at(3)
                if s.exists():
                    relations_part(s, 0)
                agg_at(4)
                if s.exists():
                    relations_part(s, 1)
                agg_at(5)
                agg_at(6)
                if r.exists():
                    ffn_down(r)

            steps(pe, node_step, 4, TILES + 1)

            def count_round(k):
                pe.wait_ge(counts_ready, k + 1)
                pe.matmul(bank[0][:TOK, 0:15], onesf[:TOK, 0:TOK], work[:TOK, 264:279], start=True, stop=True)\
                  .then_inc(counts_summed, 1)

            last_tile = Tile(None, TILES - 1)
            turn_normed(last_tile)
            ffn_up(last_tile, 0)
            count_round(0)
            ffn_up(last_tile, 1)
            count_round(1)
            ffn_down(last_tile)
            for k in range(2, 8):
                count_round(k)
            pe.wait_ge(counts_ready, 9)
            equal = work[:TOK, 820:820 + TILES + 1]
            pe.matmul(bank[0][:TOK, 0:TILES + 1], onesf[:TOK, 0:TOK], equal, start=True, stop=True)
            pe.matmul(bank[1][:TOK, 0:TILES], tri[:TOK, 0:TOK], equal[:, 0:TILES], start=True, stop=True)\
              .then_inc(counts_summed, 1)


_INS = ["x", "src", "dst", "edge_type_4", "L0_gnn_rel_weight", "L0_gnn_root_weight", "L0_gnn_rgcn_bias",
        "L0_gnn_att_weight", "L0_gnn_att_bias", "L0_mix_w_qkv", "L0_mix_b_qkv", "L0_mix_kln_g", "L0_mix_kln_b",
        "L0_mix_vln_g", "L0_mix_vln_b", "L0_mix_w1", "L0_mix_b1", "L0_mix_w2", "L0_mix_b2", "L0_ffn_wr", "L0_ffn_br",
        "L0_ffn_w1", "L0_ffn_b1", "L0_ffn_w2", "L0_ffn_b2"]


def kernel(**inputs):
    import numpy as np
    import concourse.bacc as bacc
    from concourse.bass_utils import run_bass_kernel_spmd

    nc = bacc.Bacc("TRN2", target_bir_lowering=False, num_devices=1)
    arrays, args = {}, []
    for name in _INS:
        a = np.ascontiguousarray(inputs[name])
        arrays[f"in_{name}"] = a
        args.append(nc.dram_tensor(f"in_{name}", a.shape, mybir.dt.from_np(a.dtype), kind="ExternalInput").ap())
    args.append(nc.dram_tensor("out", (N, C), mybir.dt.float32, kind="ExternalOutput").ap())
    gps_block(nc, *args)
    result = run_bass_kernel_spmd(nc, [arrays], core_ids=[0])
    return result.results[0]["out"]
```
